# Optimizing a Trainium2 kernel written in Bass

```python
import numpy as np
import jax
import jax.numpy as jnp

def _softmax(x, axis=-1):
    return jax.nn.softmax(x, axis=axis)

def _gelu(x):
    return jax.nn.gelu(x, approximate=True)

def _silu(x):
    return jax.nn.silu(x)

def _sigmoid(x):
    return jax.nn.sigmoid(x)

def _layernorm(x, axis=-1, eps=1e-05):
    m = jnp.mean(x, axis=axis, keepdims=True)
    v = jnp.var(x, axis=axis, keepdims=True)
    return (x - m) / jnp.sqrt(v + eps)

def _scatter_add(tgt, idx, src, axis=0):
    return tgt.at[idx].add(src)

def _segment_sum(src, seg, n):
    return jax.ops.segment_sum(src, seg, n)
kernel_name = 'mk_prb_d1_jaxref_r4_a3a1dd'

def setup_inputs(seed: int=0):
    np.random.seed(seed)
    _w = jnp.asarray

    def _L0_attn_setup():
        import math
        import jax, jax.numpy as jnp
        import numpy as np
        D = 256
        H = 16
        CH = 8
        EPS = 1e-05

        def _layernorm(x, w, b):
            mu = jnp.mean(x, axis=-1, keepdims=True)
            var = jnp.mean((x - mu) ** 2, axis=-1, keepdims=True)
            return (x - mu) * jax.lax.rsqrt(var + EPS) * w + b

        def _token_diffusion(x, Wqk, Wv, Wo, tau):
            b, n, d = x.shape
            dh = d // H
            qk = (x @ Wqk).reshape(b, n, H, dh).transpose(0, 2, 1, 3)
            v = (x @ Wv).reshape(b, n, H, dh).transpose(0, 2, 1, 3)
            dot = jnp.einsum('bhnd,bhmd->bhnm', qk, qk)
            q2 = jnp.sum(qk * qk, axis=-1)
            logits = (2.0 * dot - q2[..., :, None] - q2[..., None, :]) / math.sqrt(dh)
            logits = logits * tau
            attn = jax.nn.softmax(logits, axis=-1)
            out = jnp.einsum('bhnm,bhmd->bhnd', attn, v)
            out = out.transpose(0, 2, 1, 3).reshape(b, n, d)
            return out @ Wo

        def _channel_diffusion(x, Wqk, Wv, Wo, tau):
            b, n, d = x.shape
            dh = d // CH
            qk = (x @ Wqk).transpose(0, 2, 1).reshape(b, CH, dh, n)
            v = (x @ Wv).transpose(0, 2, 1).reshape(b, CH, dh, n)
            dot = jnp.einsum('bhcn,bhdn->bhcd', qk, qk)
            q2 = jnp.sum(qk * qk, axis=-1)
            logits = (2.0 * dot - q2[..., :, None] - q2[..., None, :]) / math.sqrt(n)
            logits = logits * tau
            attn = jax.nn.softmax(logits, axis=-1)
            out = jnp.einsum('bhcd,bhdn->bhcn', attn, v)
            out = out.reshape(b, d, n).transpose(0, 2, 1)
            return out @ Wo
        key = jax.random.key(seed)
        ks = jax.random.split(key, 8)
        s = 1.0 / math.sqrt(D)
        inp = {'x': jax.random.normal(ks[0], (8, 256, D), dtype=jnp.float32), 'Wqk_t': jax.random.normal(ks[1], (D, D), dtype=jnp.float32) * s, 'Wv_t': jax.random.normal(ks[2], (D, D), dtype=jnp.float32) * s, 'Wo_t': jax.random.normal(ks[3], (D, D), dtype=jnp.float32) * s, 'tau_t': jnp.ones((H, 1, 1), dtype=jnp.float32), 'Wqk_c': jax.random.normal(ks[4], (D, D), dtype=jnp.float32) * s, 'Wv_c': jax.random.normal(ks[5], (D, D), dtype=jnp.float32) * s, 'Wo_c': jax.random.normal(ks[6], (D, D), dtype=jnp.float32) * s, 'tau_c': jnp.ones((CH, 1, 1), dtype=jnp.float32), 'ln1_w': jnp.ones((D,), dtype=jnp.float32), 'ln1_b': jnp.zeros((D,), dtype=jnp.float32), 'ln2_w': jnp.ones((D,), dtype=jnp.float32), 'ln2_b': jnp.zeros((D,), dtype=jnp.float32), 'gamma1': 0.0001 * jnp.ones((D,), dtype=jnp.float32), 'gamma2': 0.0001 * jnp.ones((D,), dtype=jnp.float32)}
        return inp
    _L0_attn_in = _L0_attn_setup()

    def _L0_ffn_setup():
        import jax, jax.numpy as jnp
        import numpy as np
        D_MODEL = 256
        D_FF = 1024
        N_EXPERTS = 8
        INIT_SCALE = 0.1

        def _trunc_normal(key, shape, std):
            return std * jax.random.truncated_normal(key, -2.0, 2.0, shape, dtype=jnp.float32)
        key = jax.random.key(seed)
        ks = jax.random.split(key, 5)
        x = jax.random.normal(ks[0], (4, 256, D_MODEL), dtype=jnp.float32)
        router_W = _trunc_normal(ks[1], (D_MODEL, N_EXPERTS), INIT_SCALE / np.sqrt(D_MODEL))
        router_b = jnp.zeros((N_EXPERTS,), dtype=jnp.float32)
        W1 = _trunc_normal(ks[2], (N_EXPERTS, D_MODEL, D_FF), INIT_SCALE / np.sqrt(D_MODEL))
        b1 = jnp.zeros((N_EXPERTS, D_FF), dtype=jnp.float32)
        W2 = _trunc_normal(ks[3], (N_EXPERTS, D_FF, D_MODEL), INIT_SCALE / np.sqrt(D_FF))
        b2 = jnp.zeros((N_EXPERTS, D_MODEL), dtype=jnp.float32)
        return {'x': x, 'router_W': router_W, 'router_b': router_b, 'W1': W1, 'b1': b1, 'W2': W2, 'b2': b2}
    _L0_ffn_in = _L0_ffn_setup()
    _d = {'L0_attn_x': _L0_attn_in['x'], 'L0_attn_Wqk_t': _L0_attn_in['Wqk_t'], 'L0_attn_Wv_t': _L0_attn_in['Wv_t'], 'L0_attn_Wo_t': _L0_attn_in['Wo_t'], 'L0_attn_tau_t': _L0_attn_in['tau_t'], 'L0_attn_Wqk_c': _L0_attn_in['Wqk_c'], 'L0_attn_Wv_c': _L0_attn_in['Wv_c'], 'L0_attn_Wo_c': _L0_attn_in['Wo_c'], 'L0_attn_tau_c': _L0_attn_in['tau_c'], 'L0_attn_ln1_w': _L0_attn_in['ln1_w'], 'L0_attn_ln1_b': _L0_attn_in['ln1_b'], 'L0_attn_ln2_w': _L0_attn_in['ln2_w'], 'L0_attn_ln2_b': _L0_attn_in['ln2_b'], 'L0_attn_gamma1': _L0_attn_in['gamma1'], 'L0_attn_gamma2': _L0_attn_in['gamma2'], 'L0_ffn_router_W': _L0_ffn_in['router_W'], 'L0_ffn_router_b': _L0_ffn_in['router_b'], 'L0_ffn_W1': _L0_ffn_in['W1'], 'L0_ffn_b1': _L0_ffn_in['b1'], 'L0_ffn_W2': _L0_ffn_in['W2'], 'L0_ffn_b2': _L0_ffn_in['b2']}
    _x0 = _d['L0_attn_x']
    _d['L0_attn_x'] = jax.random.normal(jax.random.fold_in(jax.random.key(seed), 1), (2, 2048, 256), dtype=_x0.dtype)
    del _x0
    return _d

def reference(L0_attn_x, L0_attn_Wqk_t, L0_attn_Wv_t, L0_attn_Wo_t, L0_attn_tau_t, L0_attn_Wqk_c, L0_attn_Wv_c, L0_attn_Wo_c, L0_attn_tau_c, L0_attn_ln1_w, L0_attn_ln1_b, L0_attn_ln2_w, L0_attn_ln2_b, L0_attn_gamma1, L0_attn_gamma2, L0_ffn_router_W, L0_ffn_router_b, L0_ffn_W1, L0_ffn_b1, L0_ffn_W2, L0_ffn_b2):

    def _L0_attn_ref(x, Wqk_t, Wv_t, Wo_t, tau_t, Wqk_c, Wv_c, Wo_c, tau_c, ln1_w, ln1_b, ln2_w, ln2_b, gamma1, gamma2):
        import math
        import jax, jax.numpy as jnp
        import numpy as np
        D = 256
        H = 16
        CH = 8
        EPS = 1e-05

        def _layernorm(x, w, b):
            mu = jnp.mean(x, axis=-1, keepdims=True)
            var = jnp.mean((x - mu) ** 2, axis=-1, keepdims=True)
            return (x - mu) * jax.lax.rsqrt(var + EPS) * w + b

        def _token_diffusion(x, Wqk, Wv, Wo, tau):
            b, n, d = x.shape
            dh = d // H
            qk = (x @ Wqk).reshape(b, n, H, dh).transpose(0, 2, 1, 3)
            v = (x @ Wv).reshape(b, n, H, dh).transpose(0, 2, 1, 3)
            dot = jnp.einsum('bhnd,bhmd->bhnm', qk, qk)
            q2 = jnp.sum(qk * qk, axis=-1)
            logits = (2.0 * dot - q2[..., :, None] - q2[..., None, :]) / math.sqrt(dh)
            logits = logits * tau
            attn = jax.nn.softmax(logits, axis=-1)
            out = jnp.einsum('bhnm,bhmd->bhnd', attn, v)
            out = out.transpose(0, 2, 1, 3).reshape(b, n, d)
            return out @ Wo

        def _channel_diffusion(x, Wqk, Wv, Wo, tau):
            b, n, d = x.shape
            dh = d // CH
            qk = (x @ Wqk).transpose(0, 2, 1).reshape(b, CH, dh, n)
            v = (x @ Wv).transpose(0, 2, 1).reshape(b, CH, dh, n)
            dot = jnp.einsum('bhcn,bhdn->bhcd', qk, qk)
            q2 = jnp.sum(qk * qk, axis=-1)
            logits = (2.0 * dot - q2[..., :, None] - q2[..., None, :]) / math.sqrt(n)
            logits = logits * tau
            attn = jax.nn.softmax(logits, axis=-1)
            out = jnp.einsum('bhcd,bhdn->bhcn', attn, v)
            out = out.reshape(b, d, n).transpose(0, 2, 1)
            return out @ Wo
        x = x + _token_diffusion(_layernorm(x, ln1_w, ln1_b), Wqk_t, Wv_t, Wo_t, tau_t) * gamma1
        x = x + _channel_diffusion(_layernorm(x, ln2_w, ln2_b), Wqk_c, Wv_c, Wo_c, tau_c) * gamma2
        return x

    def _L0_ffn_ref(x, router_W, router_b, W1, b1, W2, b2):
        import jax, jax.numpy as jnp
        import numpy as np
        D_MODEL = 256
        D_FF = 1024
        N_EXPERTS = 8
        INIT_SCALE = 0.1

        def _trunc_normal(key, shape, std):
            return std * jax.random.truncated_normal(key, -2.0, 2.0, shape, dtype=jnp.float32)
        logits = jnp.einsum('bsd,de->bse', x.astype(jnp.float32), router_W) + router_b
        probs = jax.nn.softmax(logits, axis=-1)
        top1 = jnp.argmax(probs, axis=-1)
        mask = jax.nn.one_hot(top1, N_EXPERTS, dtype=x.dtype)
        gates = mask * probs.astype(x.dtype)
        h = jax.nn.relu(jnp.einsum('bsd,edf->besf', x, W1) + b1[:, None, :])
        y = jnp.einsum('besf,efd->besd', h, W2) + b2[:, None, :]
        out = jnp.einsum('bse,besd->bsd', gates, y)
        return out
    x = L0_attn_x
    xn = _layernorm(x, axis=-1)
    x = x + _L0_attn_ref(xn, L0_attn_Wqk_t, L0_attn_Wv_t, L0_attn_Wo_t, L0_attn_tau_t, L0_attn_Wqk_c, L0_attn_Wv_c, L0_attn_Wo_c, L0_attn_tau_c, L0_attn_ln1_w, L0_attn_ln1_b, L0_attn_ln2_w, L0_attn_ln2_b, L0_attn_gamma1, L0_attn_gamma2) + _L0_ffn_ref(xn, L0_ffn_router_W, L0_ffn_router_b, L0_ffn_W1, L0_ffn_b1, L0_ffn_W2, L0_ffn_b2)
    return x

_drawn_inputs = setup_inputs


def setup_inputs(seed=0):
    import zlib

    import numpy as np

    out = dict(_drawn_inputs(seed))
    spreads = {'L0_attn_tau_t': (1.0, 0.6),
     'L0_attn_tau_c': (1.0, 0.2),
     'L0_attn_ln1_w': (1.0, 0.6),
     'L0_attn_ln1_b': (0.0, 2.0),
     'L0_attn_ln2_w': (1.0, 0.6),
     'L0_attn_ln2_b': (0.0, 2.0),
     'L0_attn_gamma1': (9.999999747378752e-05, 0.6),
     'L0_attn_gamma2': (9.999999747378752e-05, 0.6),
     'L0_ffn_router_b': (0.0, 0.8),
     'L0_ffn_b1': (0.0, 0.8),
     'L0_ffn_b2': (0.0, 0.8)}
    factors = {'L0_attn_Wqk_t': 8.0,
     'L0_attn_Wv_t': 64.0,
     'L0_attn_Wo_t': 64.0,
     'L0_attn_Wv_c': 55.894,
     'L0_attn_Wo_c': 57.022,
     'L0_ffn_router_W': 8.0,
     'L0_ffn_W1': 8.0,
     'L0_ffn_W2': 8.0}
    for name, (base, spread) in spreads.items():
        noise = np.random.default_rng([zlib.crc32(name.encode()), seed]).standard_normal(out[name].shape)
        drawn = base * np.exp(spread * noise) if base else spread * noise
        out[name] = jnp.asarray(drawn.astype(out[name].dtype))
    for name, factor in factors.items():
        out[name] = (out[name] * factor).astype(out[name].dtype)
    return out
```

```python
from contextlib import ExitStack

import numpy as np
import concourse.bass as bass
from concourse import mybir

F32 = mybir.dt.float32
BF16 = mybir.dt.bfloat16
I32 = mybir.dt.int32
U32 = mybir.dt.uint32
ALU = mybir.AluOpType
ACT = mybir.ActivationFunctionType
AX = mybir.AxisListType

P = 128
ALG_P = 10
FIN = (2, 6)
EPS = 1e-5


def at_least(eng, sem, value):
    if isinstance(value, int) and value <= 0:
        return
    eng.wait_ge(sem, value)


def apart(eng):
    eng.nop(nofuse=True)


def build(nc, x, Wqk_t, Wv_t, Wo_t, tau_t, Wqk_c, Wv_c, Wo_c, tau_c, ln1_w, ln1_b, ln2_w, ln2_b,
          gamma1, gamma2, router_W, router_b, W1, b1, W2, b2, out):
    NB, S, D = x.shape
    H = tau_t.shape[0]
    CH = tau_c.shape[0]
    DH = D // H
    CD = D // CH
    NE, _, F = W1.shape
    KC = D // P
    FC = F // P
    TOK = NB * S
    TILES = TOK // P
    TB = S // P
    GT = 4
    GROUPS = TILES // GT
    GN = GT * P
    GB = GROUPS // NB
    HC = P // DH
    SLOT_TILES = (TOK - NE) // P + NE
    VW = DH + 1
    NCHUNK = S // 512
    QK_SCALE = 1.0 / float(np.sqrt(DH))
    CQ_SCALE = 1.0 / float(np.sqrt(S))

    xt = x.rearrange("b (t p) d -> p (b t) d", p=P)
    outt = out.rearrange("b (t p) d -> p (b t) d", p=P)

    q_parts = nc.dram_tensor("q_parts", [6, NB * D, S], BF16).ap()
    w_parts = nc.dram_tensor("w_parts", [3, NB * H, S], BF16).ap()
    x_slots = nc.dram_tensor("x_slots", [SLOT_TILES * P, D], F32).ap()
    y_slots = nc.dram_tensor("y_slots", [SLOT_TILES * P, D], F32).ap()
    xn_rows = nc.dram_tensor("xn_rows", [P, TILES, D], F32).ap()
    b1_cols = nc.dram_tensor("b1_cols", [NE, P, FC], F32).ap()

    with ExitStack() as ctx:
        def sb(name, shape, dt=F32):
            return ctx.enter_context(nc.sbuf_tensor(name, shape, dt))

        def sem(name):
            return ctx.enter_context(nc.semaphore(name))

        ps = ctx.enter_context(nc.psum_tensor("ps", [P, 8, 512], F32))

        XNW = sb("XNW", [P, 3 * 2 * KC * F])
        XN = XNW[:, 0:TILES * D].rearrange("p (t d) -> p t d", t=TILES)
        XN_REST = XNW[:, TILES * D:]
        Aflat = sb("A", [P, NB * H * TB * DH])
        A = Aflat[:, :].rearrange("p (h t d) -> p h t d", h=NB * H, t=TB)
        Vflat = sb("V", [P, NB * H * TB * VW])
        V = Vflat[:, :].rearrange("p (h m d) -> p h m d", h=NB * H, m=TB)
        YG = Vflat[:, 0:TILES * D].rearrange("p (t d) -> p t d", t=TILES)
        ident = sb("ident", [P, P])
        wqk = sb("wqk", [P, KC, D])
        wv = sb("wv", [P, KC, D])
        wo = sb("wo", [P, KC, D])
        wqkc = sb("wqkc", [P, KC, D])
        wvc = sb("wvc", [P, KC, D])
        woc = sb("woc", [P, KC, D])
        wvcT = sb("wvcT", [P, KC, D])
        l1w = sb("l1w", [P, KC])
        l1b = sb("l1b", [P, KC])
        l2w = sb("l2w", [P, D])
        l2b = sb("l2b", [P, D])
        g1r = sb("g1r", [P, D])
        g2r = sb("g2r", [P, D])
        tau2 = sb("tau2", [P, KC])
        tauh = sb("tauh", [H, 1])
        tauc = sb("tauc", [P, KC])
        ones = sb("ones", [P, P])
        blockones = sb("blockones", [P, P])
        diag = sb("diag", [P, CD])
        gate = sb("gate", [P, TILES])
        pos_u = sb("pos_u", [P, TILES], U32)
        emap = sb("emap", [1, SLOT_TILES], I32)
        nhalf = sb("nhalf", [P, GT])
        mv1 = sb("mv1", [P, 2, GT, 2])
        mv2 = sb("mv2", [P, 2, GT, 2])
        st1 = sb("st1", [P, 2, GT, 6])
        ve1 = sb("ve1", [P, 2, GT])
        ve2 = sb("ve2", [P, 2, GT])
        rs1 = sb("rs1", [P, 2, GT])
        rs2 = sb("rs2", [P, 2, GT])
        xg = sb("xg", [P, 2, GT, D])
        work = sb("work", [P, 16640])

        def views(area):
            at = [0]

            def take(shape, dt=F32):
                n = int(np.prod(shape))
                words = n if dt == F32 else n // 2
                v = area[:, at[0]:at[0] + words]
                at[0] += words
                assert at[0] <= area.shape[1], at[0]
                if dt != F32:
                    v = v.bitcast(dt)
                if len(shape) > 1:
                    names = "abcdef"[:len(shape)]
                    v = v.rearrange("p (" + " ".join(names) + ") -> p " + " ".join(names),
                                    **{k: s for k, s in zip(names, shape)})
                return v
            return take

        take = views(Aflat[:, :])
        xng = take([2, GT, D])
        zg = take([2, GT, D])
        xnT = take([2, KC, GN])
        aT = take([2, KC, GN])
        qp = views(XN_REST)([2, 3, KC, GN], BF16)
        take = views(work[:, :])
        qf = take([KC, GN])
        gf = take([KC, GN])
        sq = take([KC, GN])
        qr = take([KC, GN])
        gr = take([KC, GN])
        gp = take([2, 3, KC, GN], BF16)
        wf = take([GN])
        wr = take([GN])
        wp = take([2, 3, GN], BF16)
        zero = take([D])
        sel = take([KC, H])
        tri = take([P])
        rw = take([KC, NE])
        rb = take([NE])
        lg = take([TILES, NE])
        ex = take([TILES, NE])
        mask = take([TILES, NE])
        cnt = take([TILES, NE])
        cum = take([TILES, NE])
        s32 = take([4, TILES])
        s8 = take([6, NE])
        s8i = take([NE]).bitcast(I32)
        io_i = take([SLOT_TILES]).bitcast(I32)
        io_k = take([SLOT_TILES])
        ek = take([SLOT_TILES, NE])
        ek1 = take([SLOT_TILES])
        io_e = take([NE])
        io_ei = take([NE]).bitcast(I32)
        b1row = take([P])
        b1T = take([NE * FC])

        xload = [sem("x_loaded0"), sem("x_loaded1")]
        const_loaded = sem("const_loaded")
        late_loaded = sem("late_loaded")
        pool_step = sem("pool_step")
        dve_front_step = sem("dve_front_step")
        dve_back_step = sem("dve_back_step")
        dve_route_step = sem("dve_route_step")
        scales_made = sem("scales_made")
        act_step = sem("act_step")
        consts_made = sem("consts_made")
        zero_made = sem("zero_made")
        slots_zeroed = sem("slots_zeroed")
        var1_ready = sem("var1_ready")
        rstd1_ready = sem("rstd1_ready")
        var2_ready = sem("var2_ready")
        rstd2_ready = sem("rstd2_ready")
        xn_ready = sem("xn_ready")
        z_ready = sem("z_ready")
        xn_kept = [sem("xn_kept0"), sem("xn_kept1")]
        tr_ready = sem("tr_ready")
        tr_taken = sem("tr_taken")
        router_done = sem("router_done")
        q_ready = sem("q_ready")
        q_taken = sem("q_taken")
        q_split = sem("q_split")
        g_split = sem("g_split")
        v_ready = sem("v_ready")
        v_taken = sem("v_taken")
        w_ready = sem("w_ready")
        w_taken = sem("w_taken")
        w_split = sem("w_split")
        parts_stored = [sem("parts_stored0"), sem("parts_stored1")]
        b1_turned = sem("b1_turned")
        b1_copied = sem("b1_copied")
        b1_stored = sem("b1_stored")
        logits_shifted = sem("logits_shifted")
        logits_exp = sem("logits_exp")
        mask_ready = sem("mask_ready")
        ranks_ready = sem("ranks_ready")
        iota_rows = sem("iota_rows")

        N_CONST = 9 + H + CH
        with nc.Block() as block:
            @block.sync
            def _(sp):
                def load_x(G, par):
                    at_least(sp, xn_ready, G - 1)
                    sp.dma_start(xg[:, par], xt[:, bass.ds(G * GT, GT), :]).then_inc(xload[par], 16)

                def keep(G, par):
                    sp.wait_ge(xn_ready, G + 1)
                    sp.dma_start(XN[:, bass.ds(G * GT, GT), :], xng[:, par]).then_inc(xn_kept[par], 16)
                    sp.dma_start(xn_rows[:, bass.ds(G * GT, GT), :], xng[:, par]).then_inc(xn_kept[par], 16)

                def store_parts(G, par):
                    b, tok = G // GB, (G % GB) * GN
                    sp.wait_ge(q_split, G + 1)
                    for part in range(3):
                        sp.dma_start(q_parts[part, bass.ds(b * D, D), bass.ds(tok, GN)]
                                     .rearrange("(c p) n -> p c n", p=P), qp[:, par, part]).then_inc(parts_stored[par], 16)
                    sp.wait_ge(g_split, G + 1)
                    for part in range(3):
                        sp.dma_start(q_parts[3 + part, bass.ds(b * D, D), bass.ds(tok, GN)]
                                     .rearrange("(c p) n -> p c n", p=P), gp[:, par, part]).then_inc(parts_stored[par], 16)
                    sp.wait_ge(w_split, G + 1)
                    sp.dma_start(w_parts[:, bass.ds(b * H, H), bass.ds(tok, GN)].rearrange("c h n -> h c n"),
                                 wp[0:H, par]).then_inc(parts_stored[par], 16)

                load_x(0, 0)
                load_x(1, 1)

                def const(dst, src):
                    sp.dma_start(dst, src).then_inc(const_loaded, 16)
                const(rw, router_W.rearrange("(c p) e -> p c e", p=P))
                const(wqk[:, :, :], Wqk_t.rearrange("(c p) n -> p c n", p=P))
                const(wv[:, :, :], Wv_t.rearrange("(c p) n -> p c n", p=P))
                for c in range(KC):
                    const(l1w[:, c:c + 1], ln1_w[c * P:(c + 1) * P].rearrange("(p a) -> p a", a=1))
                    const(l1b[:, c:c + 1], ln1_b[c * P:(c + 1) * P].rearrange("(p a) -> p a", a=1))
                const(rb, router_b.partition_broadcast(P))
                const(tauh[:, :], tau_t.rearrange("h a b -> h (a b)"))
                for h in range(H):
                    c, r = h // HC, h % HC
                    const(tau2[r * DH:(r + 1) * DH, c:c + 1],
                          tau_t.rearrange("h a b -> h (a b)")[h:h + 1, :].broadcast_to([DH, 1]))
                for h in range(CH):
                    c, r = h // 4, h % 4
                    const(tauc[r * CD:(r + 1) * CD, c:c + 1],
                          tau_c.rearrange("h a b -> h (a b)")[h:h + 1, :].broadcast_to([CD, 1]))
                for dst, src in ((wo, Wo_t), (wqkc, Wqk_c), (wvc, Wv_c), (woc, Wo_c)):
                    sp.dma_start(dst[:, :, :], src.rearrange("(c p) n -> p c n", p=P)).then_inc(late_loaded, 16)
                for dst, src in ((l2w, ln2_w), (l2b, ln2_b), (g1r, gamma1), (g2r, gamma2)):
                    sp.dma_start(dst[:, :], src.partition_broadcast(P)).then_inc(late_loaded, 16)
                sp.dma_start(b1row[0:NE * FC], b1.rearrange("e (c p) -> (e c) p", p=P)).then_inc(late_loaded, 16)
                sp.wait_ge(zero_made, 1)
                for k in range(SLOT_TILES):
                    sp.dma_start(x_slots[k * P:(k + 1) * P, :], zero).then_inc(slots_zeroed, 16)
                for G in (0, 1):
                    keep(G, G)
                    load_x(G + 2, G)
                    if G == 1:
                        store_parts(0, 0)
                with sp.Fori(1, GROUPS // 2 - 1) as it:
                    for par in range(2):
                        G = 2 * it + par
                        keep(G, par)
                        load_x(G + 2, par)
                        store_parts(G - 1, 1 - par)
                for G in (GROUPS - 2, GROUPS - 1):
                    keep(G, G % 2)
                    store_parts(G - 1, 1 - G % 2)
                store_parts(GROUPS - 1, 1)
                sp.wait_ge(b1_copied, 1)
                sp.dma_start(b1_cols.rearrange("e p c -> p e c"),
                             b1T.rearrange("p (e c) -> p e c", e=NE)).then_inc(b1_stored, 16)
                for par in range(2):
                    sp.wait_ge(parts_stored[par], 7 * 16 * GROUPS // 2)
                    sp.wait_ge(xn_kept[par], 32 * GROUPS // 2)
                sp.wait_ge(b1_stored, 16)
                sp.wait_ge(slots_zeroed, 16 * SLOT_TILES)

            @block.gpsimd
            def _(pool):
                nc.gpsimd.memset(nhalf[:, :], -0.5)
                nc.gpsimd.memset(zero, 0.0).then_inc(zero_made, 1)
                nc.gpsimd.memset(ident[:, :], 0.0)
                nc.gpsimd.memset(ones[:, :], 1.0)
                nc.gpsimd.memset(tri, 1.0)
                nc.gpsimd.memset(sel, 1.0)
                nc.gpsimd.memset(blockones[:, :], 1.0)
                nc.gpsimd.memset(V[:, :, :, DH:VW], 1.0)
                nc.gpsimd.iota(io_i[0:1], pattern=[[1, SLOT_TILES]], base=0, channel_multiplier=0).then_inc(pool_step, 1)
                pool.wait_ge(pool_step, 1)
                nc.gpsimd.affine_select(out=ident[:, :], in_=ident[:, :], compare_op=ALU.not_equal, fill=1.0,
                                        base=0, pattern=[[-1, P]], channel_multiplier=1)
                nc.gpsimd.affine_select(out=tri, in_=tri, compare_op=ALU.is_gt, fill=0.0,
                                        base=0, pattern=[[1, P]], channel_multiplier=-1)
                nc.gpsimd.affine_select(out=sel, in_=sel, compare_op=ALU.is_ge, fill=0.0,
                                        base=0, pattern=[[P, KC], [-DH, H]], channel_multiplier=1)
                nc.gpsimd.affine_select(out=blockones[:, :].rearrange("p (a b) -> p a b", b=CD),
                                        in_=blockones[:, :].rearrange("p (a b) -> p a b", b=CD),
                                        compare_op=ALU.is_ge, fill=0.0, base=0, pattern=[[-CD, P // CD], [0, CD]],
                                        channel_multiplier=1).then_inc(pool_step, 1)
                pool.wait_ge(pool_step, 2)
                nc.gpsimd.affine_select(out=sel, in_=sel, compare_op=ALU.is_ge, fill=0.0,
                                        base=DH - 1, pattern=[[-P, KC], [DH, H]], channel_multiplier=-1)
                nc.gpsimd.affine_select(out=blockones[:, :].rearrange("p (a b) -> p a b", b=CD),
                                        in_=blockones[:, :].rearrange("p (a b) -> p a b", b=CD),
                                        compare_op=ALU.is_ge, fill=0.0, base=CD - 1, pattern=[[CD, P // CD], [0, CD]],
                                        channel_multiplier=-1)
                nc.gpsimd.tensor_copy(io_k[0:1], io_i[0:1]).then_inc(consts_made, 1)
                nc.gpsimd.iota(io_ei, pattern=[[1, NE]], base=0, channel_multiplier=0).then_inc(pool_step, 1)
                pool.wait_ge(pool_step, 3)
                nc.gpsimd.tensor_copy(io_e, io_ei).then_inc(iota_rows, 1)

                STEPS = 6

                def front(G, par):
                    pool.wait_ge(var1_ready, G + 1)
                    nc.gpsimd.tensor_tensor(rs1[:, par], ve1[:, par], nhalf[:, :], ALU.pow).then_inc(rstd1_ready, 1)
                    pool.wait_ge(var2_ready, G + 1)
                    nc.gpsimd.tensor_tensor(rs2[:, par], ve2[:, par], nhalf[:, :], ALU.pow).then_inc(rstd2_ready, 1)

                def back(G, par):
                    def step(n):
                        pool.wait_ge(pool_step, 3 + G * STEPS + n)
                        apart(pool)
                    pool.wait_ge(q_taken, 2 * G + 2)
                    at_least(pool, parts_stored[par], 7 * 16 * (G // 2))
                    apart(pool)
                    g = gp[:, par]
                    nc.gpsimd.tensor_copy(g[:, 0], gf).then_inc(pool_step, 1)
                    pool.wait_ge(w_taken, G + 1)
                    apart(pool)
                    w = wp[0:H, par]
                    nc.gpsimd.tensor_copy(w[:, 0], wf[0:H]).then_inc(pool_step, 1)
                    step(1)
                    nc.gpsimd.tensor_tensor(gr, gf, g[:, 0], ALU.subtract).then_inc(pool_step, 1)
                    step(2)
                    nc.gpsimd.tensor_tensor(wr[0:H], wf[0:H], w[:, 0], ALU.subtract).then_inc(pool_step, 1)
                    step(3)
                    nc.gpsimd.tensor_copy(g[:, 1], gr).then_inc(pool_step, 1)
                    step(4)
                    nc.gpsimd.tensor_copy(w[:, 1], wr[0:H]).then_inc(pool_step, 1)
                    step(5)
                    nc.gpsimd.tensor_tensor(g[:, 2], gr, g[:, 1], ALU.subtract).then_inc(g_split, 1)
                    step(6)
                    nc.gpsimd.tensor_tensor(w[:, 2], wr[0:H], w[:, 1], ALU.subtract).then_inc(w_split, 1)

                front(0, 0)
                front(1, 1)
                back(0, 0)
                with pool.Fori(1, GROUPS // 2) as it:
                    for par in range(2):
                        front(2 * it + par, par)
                        back(2 * it + par - 1, 1 - par)
                back(GROUPS - 1, 1)

            @block.vector
            def _(dve):
                def front(G, par):
                    def step(n):
                        dve.wait_ge(dve_front_step, G * 4 + n)
                        apart(dve)
                    dve.wait_ge(xload[par], 16 * (G // 2) + 16)
                    apart(dve)
                    for t in range(GT):
                        last = nc.vector.bn_stats(st1[:, par, t], xg[:, par, t])
                    last.then_inc(dve_front_step, 1)
                    step(1)
                    for t in range(GT):
                        last = nc.vector.bn_aggr(mv1[:, par, t], st1[:, par, t])
                    last.then_inc(dve_front_step, 1)
                    step(2)
                    nc.vector.tensor_scalar(ve1[:, par], mv1[:, par, :, 1], EPS, None, ALU.add).then_inc(var1_ready, 1)
                    dve.wait_ge(rstd1_ready, G + 1)
                    at_least(dve, xn_kept[par], 32 * (G // 2))
                    at_least(dve, tr_ready, 4 * (G - 1))
                    for t in range(GT):
                        last = nc.vector.tensor_scalar(xng[:, par, t], xg[:, par, t], mv1[:, par, t, 0:1],
                                                       rs1[:, par, t:t + 1], ALU.subtract, ALU.mult)
                    last.then_inc(xn_ready, 1)
                    dve.wait_ge(xn_ready, G + 1)
                    apart(dve)
                    for t in range(GT):
                        last = nc.vector.bn_stats(st1[:, par, t], xng[:, par, t])
                    last.then_inc(dve_front_step, 1)
                    step(3)
                    for t in range(GT):
                        last = nc.vector.bn_aggr(mv2[:, par, t], st1[:, par, t])
                    last.then_inc(dve_front_step, 1)
                    step(4)
                    nc.vector.tensor_scalar(ve2[:, par], mv2[:, par, :, 1], EPS, None, ALU.add).then_inc(var2_ready, 1)
                    dve.wait_ge(rstd2_ready, G + 1)
                    for t in range(GT):
                        last = nc.vector.tensor_scalar(zg[:, par, t], xng[:, par, t], mv2[:, par, t, 0:1],
                                                       rs2[:, par, t:t + 1], ALU.subtract, ALU.mult)
                    last.then_inc(z_ready, 1)

                def back(G, par):
                    def step(n):
                        dve.wait_ge(dve_back_step, G * 3 + n)
                    b, m0 = G // GB, (G % GB) * GT
                    dve.wait_ge(q_taken, 2 * G + 2)
                    at_least(dve, parts_stored[par], 7 * 16 * (G // 2))
                    q = qp[:, par]
                    nc.vector.tensor_copy(q[:, 0], qf).then_inc(dve_back_step, 1)
                    step(1)
                    nc.vector.tensor_tensor(qr, qf, q[:, 0], ALU.subtract).then_inc(dve_back_step, 1)
                    step(2)
                    nc.vector.tensor_copy(q[:, 1], qr).then_inc(dve_back_step, 1)
                    step(3)
                    nc.vector.tensor_tensor(q[:, 2], qr, q[:, 1], ALU.subtract).then_inc(q_split, 1)
                    for k in range(2):
                        dve.wait_ge(v_ready, 2 * G + k + 1)
                        nc.vector.tensor_copy(
                            V[:, bass.ds(b * H, H), bass.ds(m0 + 2 * k, 2), 0:DH].rearrange("p h m d -> p m h d"),
                            ps[:, 5 + k].rearrange("p (m h d) -> p m h d", m=2, h=H)).then_inc(v_taken, 1)


                dve.wait_ge(const_loaded, 16 * N_CONST)
                nc.vector.tensor_scalar(tau2[:, :], tau2[:, :], 2.0 * QK_SCALE, None, ALU.mult)
                nc.vector.tensor_scalar(tauc[:, :], tauc[:, :], CQ_SCALE, None, ALU.mult)
                nc.vector.tensor_scalar(tauh[:, :], tauh[:, :], -QK_SCALE, None, ALU.mult).then_inc(scales_made, 1)
                front(0, 0)
                front(1, 1)
                back(0, 0)
                with dve.Fori(1, GROUPS // 2) as it:
                    for par in range(2):
                        front(2 * it + par, par)
                        back(2 * it + par - 1, 1 - par)
                back(GROUPS - 1, 1)

                n = [0]

                def mark(ins):
                    n[0] += 1
                    ins.then_inc(dve_route_step, 1)
                    dve.wait_ge(dve_route_step, n[0])

                def over_experts(v):
                    return v.unsqueeze(2).broadcast_to([P, TILES, NE])

                def over_tiles(v):
                    return v.unsqueeze(1).broadcast_to([P, TILES, NE])
                mx, sm, pm, idx = (s32[:, k] for k in range(4))
                dve.wait_ge(late_loaded, 16 * 9)
                mark(nc.vector.tensor_tensor(wo[:, :, :], wo[:, :, :],
                                             g1r[:, :].unsqueeze(1).broadcast_to([P, KC, D]), ALU.mult))
                mark(nc.vector.tensor_reduce(diag[:, :], ident[:, :].rearrange("p (a b) -> p b a", b=CD), AX.X, ALU.add))
                dve.wait_ge(router_done, GROUPS)
                mark(nc.vector.tensor_tensor(lg, ps[:, 2, 0:TILES * NE].rearrange("p (t e) -> p t e", e=NE),
                                             over_tiles(rb), ALU.add))
                mark(nc.vector.tensor_reduce(mx, lg, AX.X, ALU.max))
                nc.vector.tensor_tensor(lg, lg, over_experts(mx), ALU.subtract).then_inc(logits_shifted, 1)
                dve.wait_ge(logits_exp, 1)
                mark(nc.vector.tensor_reduce(sm, ex, AX.X, ALU.add))
                mark(nc.vector.reciprocal(sm, sm))
                mark(nc.vector.tensor_tensor(ex, ex, over_experts(sm), ALU.mult))
                mark(nc.vector.tensor_reduce(gate[:, :], ex, AX.X, ALU.max))
                mark(nc.vector.tensor_tensor(lg, ex, over_experts(gate[:, :]), ALU.is_equal))
                dve.wait_ge(consts_made, 1)
                dve.wait_ge(iota_rows, 1)
                mark(nc.vector.tensor_scalar(s8[:, 0], io_e, float(NE), None, ALU.add))
                mark(nc.vector.scalar_tensor_tensor(lg, lg, -float(NE), over_tiles(s8[:, 0]), ALU.mult, ALU.add))
                mark(nc.vector.tensor_reduce(idx, lg, AX.X, ALU.min))
                nc.vector.tensor_tensor(mask, over_tiles(io_e), over_experts(idx), ALU.is_equal).then_inc(mask_ready, 1)
                dve.wait_ge(ranks_ready, 1)
                mark(nc.vector.tensor_copy(cnt, ps[:, 4, 0:TILES * NE].rearrange("p (t e) -> p t e", e=NE)))
                for e in range(NE):
                    last = nc.vector.tensor_tensor_scan(cum[:, :, e], ones[:, 0:TILES], cnt[:, :, e], 0.0,
                                                        ALU.mult, ALU.add)
                mark(last)
                mark(nc.vector.tensor_scalar(s8[:, 1], cum[:, TILES - 1], float(P - 1), None, ALU.add))
                mark(nc.vector.tensor_copy(s8i, s8[:, 1]))
                mark(nc.vector.tensor_scalar(s8i, s8i, 7, None, ALU.arith_shift_right))
                mark(nc.vector.tensor_copy(s8[:, 2], s8i))
                mark(nc.vector.tensor_tensor_scan(s8[:, 3], ones[:, 0:NE], s8[:, 2], 0.0, ALU.mult, ALU.add))
                mark(nc.vector.tensor_tensor(s8[:, 4], s8[:, 3], s8[:, 2], ALU.subtract))
                mark(nc.vector.tensor_scalar(s8[:, 5], s8[:, 4], float(P), None, ALU.mult))
                mark(nc.vector.tensor_tensor(cum, cum, cnt, ALU.subtract))
                mark(nc.vector.tensor_tensor(cum, cum, over_tiles(s8[:, 5]), ALU.add))
                mark(nc.vector.tensor_tensor(cum, ps[:, 3, 0:TILES * NE].rearrange("p (t e) -> p t e", e=NE), cum, ALU.add))
                mark(nc.vector.tensor_tensor(cum, cum, mask, ALU.mult))
                mark(nc.vector.tensor_reduce(mx, cum, AX.X, ALU.add))
                nc.vector.tensor_copy(pos_u[:, :], mx)
                ends = s8[0:1, 3].unsqueeze(1).broadcast_to([1, SLOT_TILES, NE])
                mark(nc.vector.tensor_tensor(ek[0:1], io_k[0:1].unsqueeze(2).broadcast_to([1, SLOT_TILES, NE]), ends,
                                             ALU.is_ge))
                mark(nc.vector.tensor_reduce(ek1[0:1], ek[0:1], AX.X, ALU.add))
                mark(nc.vector.tensor_scalar(ek1[0:1], ek1[0:1], float(NE - 1), None, ALU.min))
                mark(nc.vector.tensor_copy(emap[:, :], ek1[0:1]))

            @block.scalar
            def _(act):
                def group(G, par):
                    for k in range(4):
                        act.wait_ge(tr_ready, 4 * G + k + 1)
                        if k == 0:
                            at_least(act, router_done, G - 1)
                        if k == 2:
                            at_least(act, v_ready, 2 * (G - 1))
                        if k < 2:
                            nc.scalar.copy(xnT[:, par, k], ps[:, k]).then_inc(tr_taken, 1)
                        else:
                            nc.scalar.activation(aT[:, par, k - 2], ps[:, k - 2], ACT.Identity,
                                                 bias=l1b[:, k - 2:k - 1], scale=l1w[:, k - 2:k - 1]).then_inc(tr_taken, 1)
                    for M in range(KC):
                        act.wait_ge(q_ready, 2 * G + M + 1)
                        if M == 0:
                            at_least(act, q_split, G)
                            at_least(act, g_split, G)
                            at_least(act, w_ready, G)
                        nc.scalar.copy(qf[:, M], ps[:, 3 + M])
                        nc.scalar.mul(gf[:, M], ps[:, 3 + M], tau2[:, M:M + 1])
                        nc.scalar.activation(sq[:, M], ps[:, 3 + M], ACT.Square).then_inc(q_taken, 1)
                    act.wait_ge(w_ready, G + 1)
                    at_least(act, w_split, G)
                    nc.scalar.mul(wf[0:H], ps[0:H, 7], tauh[:, 0:1]).then_inc(w_taken, 1)

                act.wait_ge(const_loaded, 16 * N_CONST)
                act.wait_ge(scales_made, 1)
                group(0, 0)
                group(1, 1)
                with act.Fori(1, GROUPS // 2) as it:
                    for par in range(2):
                        group(2 * it + par, par)
                act.wait_ge(b1_turned, 1)
                nc.scalar.copy(b1T, ps[:, 0, 0:NE * FC]).then_inc(b1_copied, 1)
                nc.scalar.copy(wvcT[:, :, :], ps[:, 1].rearrange("p (a b) -> p a b", a=KC))
                act.wait_ge(logits_shifted, 1)
                nc.scalar.activation(ex, lg, ACT.Exp).then_inc(logits_exp, 1)

            @block.tensor
            def _(pe):
                def turn(G, par):
                    for k in range(4):
                        src = xng if k < 2 else zg
                        if k == 0:
                            pe.wait_ge(xn_ready, G + 1)
                        if k == 2:
                            pe.wait_ge(z_ready, G + 1)
                        at_least(pe, tr_taken, 4 * G + k - 1)
                        for t in range(GT):
                            last = nc.tensor.transpose(ps[:, k % 2, t * P:(t + 1) * P],
                                                       src[:, par, t, (k % 2) * P:(k % 2 + 1) * P], ident[:, :])
                        last.then_inc(tr_ready, 1)

                def products(G, par):
                    pe.wait_ge(tr_taken, 4 * G + 2)
                    for t in range(GT):
                        for c in range(KC):
                            last = nc.tensor.matmul(ps[:, 2, bass.ds((G * GT + t) * NE, NE)],
                                                    xnT[:, par, c, t * P:(t + 1) * P], rw[:, c],
                                                    start=(c == 0), stop=(c == KC - 1))
                    last.then_inc(router_done, 1)
                    pe.wait_ge(tr_taken, 4 * G + 4)
                    for M in range(KC):
                        at_least(pe, q_taken, 2 * (G - 1) + M + 1)
                        for c in range(KC):
                            last = nc.tensor.matmul(ps[:, 3 + M], wqk[:, c, M * P:(M + 1) * P], aT[:, par, c],
                                                    start=(c == 0), stop=(c == KC - 1))
                        last.then_inc(q_ready, 1)
                    for k in range(2):
                        at_least(pe, v_taken, 2 * (G - 1) + k + 1)
                        for t in range(2):
                            for c in range(KC):
                                last = nc.tensor.matmul(ps[:, 5 + k, t * D:(t + 1) * D],
                                                        aT[:, par, c, (2 * k + t) * P:(2 * k + t + 1) * P], wv[:, c],
                                                        start=(c == 0), stop=(c == KC - 1))
                        last.then_inc(v_ready, 1)
                    pe.wait_ge(q_taken, 2 * G + 2)
                    at_least(pe, w_taken, G)
                    for c in range(KC):
                        last = nc.tensor.matmul(ps[0:H, 7], sel[:, c], sq[:, c], start=(c == 0), stop=(c == KC - 1))
                    last.then_inc(w_ready, 1)

                pe.wait_ge(consts_made, 1)
                pe.wait_ge(const_loaded, 16 * N_CONST)
                for G in (0, 1):
                    turn(G, G)
                    products(G, G)
                with pe.Fori(1, GROUPS // 2) as it:
                    for par in range(2):
                        turn(2 * it + par, par)
                        products(2 * it + par, par)
                pe.wait_ge(late_loaded, 16 * 9)
                pe.wait_ge(tr_taken, 4 * GROUPS)
                nc.tensor.transpose(ps[:, 0, 0:NE * FC], b1row[0:NE * FC], ident[0:NE * FC, 0:NE * FC])
                for d in range(KC):
                    for k in range(KC):
                        last = nc.tensor.transpose(ps[:, 1, (d * KC + k) * P:(d * KC + k + 1) * P],
                                                   wvc[:, k, d * P:(d + 1) * P], ident[:, :])
                last.then_inc(b1_turned, 1)
                pe.wait_ge(mask_ready, 1)
                nc.tensor.matmul(ps[:, 3, 0:TILES * NE], tri, mask.rearrange("p t e -> p (t e)"), start=True, stop=True)
                nc.tensor.matmul(ps[:, 4, 0:TILES * NE], ones[:, :], mask.rearrange("p t e -> p (t e)"),
                                 start=True, stop=True).then_inc(ranks_ready, 1)

        take = views(work[:, :])
        stat = take([2, S], BF16)
        mov = take([2, S], BF16)
        probs = take([2, S])
        Vh = take([2, TB, VW])
        osb = take([2, 512])
        rec = take([2, TB])
        take_w = views(XNW[:, :])
        w1s = take_w([3, KC, F])
        w2s = take_w([3, FC, D])
        b1s = take([3, FC])
        b2s = take([3, D])
        xs = take([3, D])
        xsT = take([3, KC, P])
        hT = take([FC, P])
        ysb = take([3, D])
        STAT_PARTS = (0, 0, 0, 1, 1, 2)
        MOV_PARTS = (3, 4, 5, 3, 4, 3)
        KROWS = P
        AUX = 6 * DH
        PAIRS = NB * H // 2
        STEPS = 2 * TB
        FIRST = PAIRS - SLOT_TILES // 3
        assert SLOT_TILES == 3 * (PAIRS - FIRST)
        SUBS = 10
        STACK_DMAS = 14
        TILE_DMAS = 5
        AV, Y, RING = 4, 5, 6

        stack_loaded = [sem("stack_loaded0"), sem("stack_loaded1")]
        tile_loaded = [sem(f"tile_loaded{k}") for k in range(3)]
        rows_set = sem("rows_set")
        logits_ready = sem("logits_ready")
        probs_ready = sem("probs_ready")
        av_done = sem("av_done")
        v_copied = sem("v_copied")
        o_cleared = sem("o_cleared")
        o_copied = sem("o_copied")
        rec_ready = sem("rec_ready")
        ring_ready = sem("ring_ready")
        ring_taken = sem("ring_taken")
        y_ready = sem("y_ready")
        y_taken = sem("y_taken")
        y_stored = [sem(f"y_stored{k}") for k in range(3)]
        scattered = sem("scattered")
        a_ready = sem("a_ready")

        def ring_base(i, experts):
            if isinstance(i, int) and i == 0:
                return 0
            if not experts:
                return 2 * i - 1
            return 2 * FIRST - 1 + 32 * (i - FIRST)

        def plan(i, experts):
            steps = []
            for s in range(STEPS):
                uses = []
                if experts and s < 3 * SUBS:
                    sub = s % SUBS
                    if sub == 0:
                        uses += [("x", s // SUBS, 0), ("x", s // SUBS, 1)]
                    elif sub <= FC:
                        uses += [("h", s // SUBS, sub - 1)]
                if s == 1 and not (isinstance(i, int) and i == 0):
                    uses += [("o", 1, -1)]
                if s == TB + 1:
                    uses += [("o", 0, 0)]
                steps.append(uses)
            return steps

        def use_numbers(uses_by_step):
            table, k = {}, 0
            for uses in uses_by_step:
                for u in uses:
                    table[u] = k
                    k += 1
            return table

        def bank(i, k):
            first = 0 if isinstance(i, int) and i == 0 else 1
            return RING + (first + k) % 2

        with nc.Block() as block:
            @block.sync
            def _(sp):
                def load_stack(i, hh):
                    at_least(sp, logits_ready, 2 * (STEPS * (i - 1) + TB * (hh + 1)))
                    r0 = i * 2 * DH + hh * DH
                    for k in range(6):
                        sp.dma_start(stat[k * DH:(k + 1) * DH, hh], q_parts[STAT_PARTS[k], bass.ds(r0, DH), :]
                                     ).then_inc(stack_loaded[hh], 16)
                        sp.dma_start(mov[k * DH:(k + 1) * DH, hh], q_parts[MOV_PARTS[k], bass.ds(r0, DH), :]
                                     ).then_inc(stack_loaded[hh], 16)
                    w = w_parts[:, bass.ds(i * 2 + hh, 1), :].rearrange("c h n -> (c h) n")
                    sp.dma_start(stat[AUX + 3:AUX + 6, hh], w).then_inc(stack_loaded[hh], 16)
                    sp.dma_start(mov[AUX:AUX + 3, hh], w).then_inc(stack_loaded[hh], 16)

                def load_tile(i, tt):
                    n = 3 * (i - FIRST) + tt
                    at_least(sp, y_taken, n - 2)
                    e = sp.value_load(emap[0:1, bass.ds(n, 1)], min_val=0, max_val=NE - 1)

                    def get(dst, src):
                        sp.dma_start(dst, src).then_inc(tile_loaded[tt], 16)
                    get(xs[:, tt], x_slots[bass.ds(n * P, P), :])
                    get(w1s[:, tt], W1[bass.ds(e, 1)].rearrange("e (c p) f -> p (e c) f", p=P))
                    get(b1s[:, tt], b1_cols[bass.ds(e, 1)].rearrange("e p c -> (e p) c"))
                    get(w2s[:, tt], W2[bass.ds(e, 1)].rearrange("e (c p) n -> p (e c) n", p=P))
                    get(b2s[:, tt], b2[bass.ds(e, 1), :].broadcast_to([P, D]))

                sp.wait_ge(rows_set, 1)
                load_stack(0, 0)
                load_stack(0, 1)
                for i in range(FIRST - 1):
                    load_stack(i + 1, 0)
                    load_stack(i + 1, 1)
                sp.wait_ge(scattered, 16 * TILES)
                for tt in range(3):
                    load_tile(FIRST, tt)
                load_stack(FIRST, 0)
                load_stack(FIRST, 1)

                def ahead(i):
                    load_tile(i + 1, 0)
                    load_stack(i + 1, 0)
                    load_tile(i + 1, 1)
                    load_tile(i + 1, 2)
                    load_stack(i + 1, 1)
                with sp.Fori(FIRST, PAIRS - 1) as i:
                    ahead(i)

            @block.gpsimd
            def _(pool):
                def copy_v(i, hh):
                    at_least(pool, av_done, STEPS * (i - 1) + TB * (hh + 1))
                    apart(pool)
                    nc.gpsimd.tensor_copy(Vh[:, hh], V[:, bass.ds(2 * i + hh, 1)].rearrange("p h m d -> p (h m) d")
                                          ).then_inc(v_copied, 1)

                def store_y(i, tt):
                    n = 3 * (i - FIRST) + tt
                    pool.wait_ge(y_taken, n + 1)
                    pool.dma_start(y_slots[bass.ds(n * P, P), :], ysb[:, tt]).then_inc(y_stored[tt], 16)

                copy_v(0, 0)
                copy_v(0, 1)
                for t in range(TILES):
                    nc.gpsimd.indirect_dma_start(x_slots, bass.IndirectOffsetOnAxis(ap=pos_u[:, t:t + 1], axis=0),
                                                 XN[:, t], None).then_inc(scattered, 16)
                for i in range(1, FIRST + 1):
                    copy_v(i, 0)
                    copy_v(i, 1)
                with pool.Fori(FIRST, PAIRS - 1) as i:
                    store_y(i, 0)
                    copy_v(i + 1, 0)
                    store_y(i, 1)
                    store_y(i, 2)
                    copy_v(i + 1, 1)
                for tt in range(3):
                    store_y(PAIRS - 1, tt)
                for tt in range(3):
                    pool.wait_ge(y_stored[tt], 16 * (PAIRS - FIRST))

            @block.scalar
            def _(act):
                def body(i):
                    for s in range(STEPS):
                        g = STEPS * i + s
                        for half in range(2):
                            act.wait_ge(logits_ready, 2 * g + half + 1)
                            if half == 0:
                                at_least(act, av_done, g - 1)
                            nc.scalar.activation(probs[:, s % 2, half * 1024:(half + 1) * 1024],
                                                 ps[:, 2 * half:2 * half + 2].rearrange("p a b -> p (a b)"),
                                                 ACT.Exp).then_inc(probs_ready, 1)
                body(0)
                with act.Fori(1, PAIRS) as i:
                    body(i)

            @block.vector
            def _(dve):
                nc.vector.memset(ps[:, AV], 0.0)
                for hh in range(2):
                    nc.vector.memset(stat[AUX:P, hh], 0.0)
                    last = nc.vector.memset(mov[AUX:P, hh], 0.0)
                last.then_inc(o_cleared, 1)
                dve.wait_ge(o_cleared, 1)
                for hh in range(2):
                    nc.vector.memset(stat[AUX:AUX + 6, hh], 1.0)
                    last = nc.vector.memset(mov[AUX:AUX + 6, hh], 1.0)
                last.then_inc(rows_set, 1)

                def take_o(i, hh):
                    head = 2 * i + hh
                    dve.wait_ge(av_done, TB * (head + 1))
                    nc.vector.tensor_copy(osb[:, hh], ps[:, AV]).then_inc(o_copied, 1)

                def norm(i, experts, use, hh, shift):
                    head = 2 * (i + shift) + hh
                    k = use[("o", hh, shift)]
                    t4 = ps[:, bank(i, k)].rearrange("p (k j c) -> p j k c", k=4, j=NCHUNK)
                    dve.wait_ge(ring_ready, ring_base(i, experts) + k + 1)
                    r = rec[:, hh].rearrange("p (j k) -> p j k", j=NCHUNK)
                    nc.vector.reciprocal(r, t4[:, :, :, DH]).then_inc(rec_ready, 1)
                    dve.wait_ge(rec_ready, head + 1)
                    nc.vector.tensor_tensor(
                        A[:, bass.ds(head, 1)].rearrange("p h (j k) d -> p (h j) k d", j=NCHUNK),
                        t4[:, :, :, 0:DH], r.unsqueeze(3).broadcast_to([P, NCHUNK, 4, DH]), ALU.mult
                    ).then_inc(ring_taken, 1)

                def body(i, experts):
                    uses = plan(i, experts)
                    use = use_numbers(uses)
                    for s in range(STEPS):
                        if s == 0 and not (isinstance(i, int) and i == 0):
                            take_o(i - 1, 1)
                        if s == TB:
                            take_o(i, 0)
                        for u in uses[s]:
                            kind, a, b = u
                            k = use[u]
                            if kind == "o":
                                norm(i, experts, use, a, b)
                                continue
                            dve.wait_ge(ring_ready, ring_base(i, experts) + k + 1)
                            if kind == "x":
                                nc.vector.tensor_copy(xsT[:, a, b], ps[:, bank(i, k), 0:P]).then_inc(ring_taken, 1)
                            else:
                                nc.vector.tensor_scalar(hT[:, b], ps[:, bank(i, k), 0:P], b1s[:, a, b:b + 1], 0.0,
                                                        ALU.add, ALU.max).then_inc(ring_taken, 1)
                        if experts and s < 3 * SUBS and s % SUBS == SUBS - 1:
                            tt = s // SUBS
                            dve.wait_ge(y_ready, 3 * (i - FIRST) + tt + 1)
                            at_least(dve, y_stored[tt], 16 * (i - FIRST))
                            nc.vector.tensor_tensor(ysb[:, tt], ps[:, Y, 0:D], b2s[:, tt], ALU.add).then_inc(y_taken, 1)

                body(0, False)
                with dve.Fori(1, FIRST) as i:
                    body(i, False)
                body(FIRST, True)
                with dve.Fori(FIRST + 1, PAIRS) as i:
                    body(i, True)
                take_o(PAIRS - 1, 1)
                norm(PAIRS, True, {("o", 1, -1): 0}, 1, -1)

            @block.tensor
            def _(pe):
                def logits(i, s):
                    hh, m = s // TB, s % TB
                    g = STEPS * i + s
                    if m == 0:
                        pe.wait_ge(stack_loaded[hh], 16 * STACK_DMAS * (i + 1))
                    for half in range(2):
                        at_least(pe, probs_ready, 2 * g + half - 1)
                        for j in range(2):
                            q0 = (2 * half + j) * 512
                            last = nc.tensor.matmul(ps[:, 2 * half + j], stat[:, hh, m * P:(m + 1) * P],
                                                    mov[:, hh, q0:q0 + 512], start=True, stop=True)
                        last.then_inc(logits_ready, 1)

                def values(i, s):
                    hh, m = s // TB, s % TB
                    g = STEPS * i + s
                    if m == 0:
                        pe.wait_ge(v_copied, 2 * i + hh + 1)
                        at_least(pe, o_copied, 2 * i + hh)
                    pe.wait_ge(probs_ready, 2 * g + 2)
                    for j in range(NCHUNK):
                        last = nc.tensor.matmul(ps[32 * j:32 * j + VW, AV], Vh[:, hh, m],
                                                probs[:, s % 2, j * 512:(j + 1) * 512],
                                                start=(m == 0), stop=(m == TB - 1), tile_position=(0, 32 * j))
                    last.then_inc(av_done, 1)

                def turn_o(i, k, hh, shift):
                    pe.wait_ge(o_copied, 2 * (i + shift) + hh + 1)
                    for c in range(4):
                        last = nc.tensor.transpose(ps[:, bank(i, k), c * P:(c + 1) * P],
                                                   osb[:, hh, c * P:(c + 1) * P], ident[:, :])
                    last.then_inc(ring_ready, 1)

                def body(i, experts, last_one=False):
                    uses = plan(i, experts)
                    use = use_numbers(uses)
                    for s in range(STEPS):
                        if s + 1 < STEPS:
                            logits(i, s + 1)
                        elif not last_one:
                            logits(i + 1, 0)
                        sub, tt = s % SUBS, s // SUBS
                        for u in uses[s]:
                            kind, a, b = u
                            k = use[u]
                            at_least(pe, ring_taken, ring_base(i, experts) + k - 1)
                            if kind == "o":
                                turn_o(i, k, a, b)
                            elif kind == "x":
                                if b == 0:
                                    pe.wait_ge(tile_loaded[a], 16 * TILE_DMAS * (i - FIRST + 1))
                                nc.tensor.transpose(ps[:, bank(i, k), 0:P], xs[:, a, b * P:(b + 1) * P],
                                                    ident[:, :]).then_inc(ring_ready, 1)
                            else:
                                if b == 0:
                                    pe.wait_ge(ring_taken, ring_base(i, experts) + use[("x", a, 1)] + 1)
                                for c in range(KC):
                                    last = nc.tensor.matmul(ps[:, bank(i, k), 0:P], w1s[:, a, c, b * P:(b + 1) * P],
                                                            xsT[:, a, c], start=(c == 0), stop=(c == KC - 1))
                                last.then_inc(ring_ready, 1)
                        if experts and tt < 3 and sub >= 2:
                            c = sub - 2
                            pe.wait_ge(ring_taken, ring_base(i, experts) + use[("h", tt, c)] + 1)
                            if c == 0:
                                at_least(pe, y_taken, 3 * (i - FIRST) + tt)
                            ins = nc.tensor.matmul(ps[:, Y, 0:D], hT[:, c], w2s[:, tt, c],
                                                   start=(c == 0), stop=(c == FC - 1))
                            if c == FC - 1:
                                ins.then_inc(y_ready, 1)
                        values(i, s)

                pe.wait_ge(rows_set, 1)
                logits(0, 0)
                body(0, False)
                with pe.Fori(1, FIRST) as i:
                    body(i, False)
                body(FIRST, True)
                with pe.Fori(FIRST + 1, PAIRS - 1) as i:
                    body(i, True)
                body(PAIRS - 1, True, True)
                at_least(pe, ring_taken, ring_base(PAIRS, True) - 1)
                turn_o(PAIRS, 0, 1, -1)

        take = views(work[:, :])
        At = take([2, GT, D])
        AT = take([2, KC, GN])
        a2g = take([2, GT, D])
        a2T = take([KC, TOK])
        a2s = At.rearrange("p g t (c n) -> p g (t c n)", c=KC).rearrange("p g (c n) -> p g c n", c=KC)
        og = a2g
        take_m = views(XN_REST)
        gram = take_m([NB, KC, D])
        t1 = take_m([NB, KC, D])
        rr = take_m([NB, KC, D])
        mb = take_m([NB, KC, D])
        pblk = take([NB * KC, P])
        dd = take([NB * KC, CD])
        dm = take([NB * KC, CD])
        ll = take([NB * KC, CD])
        c4 = take([3, NB * KC])

        def use_a(G):
            return 0 if isinstance(G, int) and G == 0 else 4 * G - 2

        def use_a2(G):
            return 4 * G + 2 if isinstance(G, int) and G == GROUPS - 1 else 4 * G + 4

        gathered = sem("gathered")
        at_copied = sem("at_copied")
        ring3_ready = sem("ring3_ready")
        ring3_taken = sem("ring3_taken")
        wo_ready = sem("wo_ready")
        x1_ready = sem("x1_ready")
        c_step = sem("c_step")
        var3_ready = sem("var3_ready")
        rstd3_ready = sem("rstd3_ready")
        a2_ready = sem("a2_ready")
        gram_cleared = sem("gram_cleared")
        gram_done = sem("gram_done")
        gram_copied = sem("gram_copied")
        alg_pe = sem("alg_pe")
        alg_dve = sem("alg_dve")
        alg_exp = sem("alg_exp")
        staged = sem("staged")
        fin_ready = sem("fin_ready")
        fin_taken = sem("fin_taken")
        sum_ready = sem("sum_ready")
        x_again = [sem("x_again0"), sem("x_again1")]
        out_stored = [sem("out_stored0"), sem("out_stored1")]
        f_step = sem("f_step")
        xn_back = [sem("xn_back0"), sem("xn_back1")]

        with nc.Block() as block:
            @block.sync
            def _(sp):
                def load(G, par):
                    at_least(sp, sum_ready, G - 1)
                    sp.dma_start(xg[:, par], xt[:, bass.ds(G * GT, GT), :]).then_inc(x_again[par], 16)

                def store(G, par):
                    sp.wait_ge(sum_ready, G + 1)
                    sp.dma_start(outt[:, bass.ds(G * GT, GT), :], og[:, par]).then_inc(out_stored[par], 16)
                for b in range(NB):
                    sp.dma_start(XN[:, b * TB:(b + 1) * TB], xn_rows[:, b * TB:(b + 1) * TB]).then_inc(xn_back[b], 16)
                load(0, 0)
                load(1, 1)
                with sp.Fori(0, GROUPS // 2 - 1) as it:
                    for par in range(2):
                        G = 2 * it + par
                        store(G, par)
                        load(G + 2, par)
                store(GROUPS - 2, 0)
                store(GROUPS - 1, 1)
                for par in range(2):
                    sp.wait_ge(out_stored[par], 16 * GROUPS // 2)

            @block.gpsimd
            def _(pool):
                def rstd(G, par):
                    pool.wait_ge(var3_ready, G + 1)
                    nc.gpsimd.tensor_tensor(rs1[:, par], ve1[:, par], nhalf[:, :], ALU.pow).then_inc(rstd3_ready, 1)

                for G in range(GROUPS):
                    rstd(G, G % 2)
                    for t in range(G * GT, (G + 1) * GT):
                        nc.gpsimd.indirect_dma_start(YG[:, t], None, y_slots,
                                                     bass.IndirectOffsetOnAxis(ap=pos_u[:, t:t + 1], axis=0)
                                                     ).then_inc(gathered, 16)

            @block.scalar
            def _(act):
                def stage_a(G, par):
                    b, t0 = G // GB, (G % GB) * GT
                    if not isinstance(G, int) or G >= 2:
                        act.wait_ge(ring3_ready, 4 * G - 8)
                    for t in range(GT):
                        last = nc.scalar.copy(
                            At[:, par, t].rearrange("p (h d) -> p h d", h=H),
                            A[:, bass.ds(b * H, H), bass.ds(t0 + t, 1)].rearrange("p h t d -> p (h t) d"))
                    last.then_inc(at_copied, 1)

                def take_at(G, par):
                    for c in range(KC):
                        act.wait_ge(ring3_ready, use_a(G) + c + 1)
                        if c == 0:
                            at_least(act, wo_ready, 2 * (G - 1))
                        nc.scalar.copy(AT[:, par, c], ps[:, c]).then_inc(ring3_taken, 1)

                def take_a2(G, par):
                    for c in range(KC):
                        act.wait_ge(ring3_ready, use_a2(G) + c + 1)
                        nc.scalar.copy(a2T[:, c, bass.ds(G * GN, GN)], ps[:, c]).then_inc(ring3_taken, 1)

                stage_a(0, 0)
                take_at(0, 0)

                def turn(G, par):
                    stage_a(G + 1, 1 - par)
                    take_at(G + 1, 1 - par)
                    take_a2(G, par)
                turn(0, 0)
                turn(1, 1)
                with act.Fori(1, GROUPS // 2 - 1) as it:
                    for par in range(2):
                        turn(2 * it + par, par)
                turn(GROUPS - 2, 0)
                take_a2(GROUPS - 1, 1)
                act.wait_ge(gram_done, GROUPS)
                nc.scalar.copy(gram.rearrange("p b c n -> p b (c n)"), ps[:, 4:6]).then_inc(gram_copied, 1)
                act.wait_ge(alg_pe, 1)
                nc.scalar.copy(t1.rearrange("p b c n -> p b (c n)"), ps[:, 6:8]).then_inc(gram_copied, 1)
                act.wait_ge(alg_exp, 1)
                nc.scalar.activation(ll, ll, ACT.Exp).then_inc(gram_copied, 1)
                act.wait_ge(alg_pe, 4)
                nc.scalar.copy(rr.rearrange("p b c n -> p b (c n)"), ps[:, 6:8]).then_inc(gram_copied, 1)

                def stage_f(G, par):
                    at_least(act, fin_ready, 2 * (G - 1))
                    nc.scalar.copy(a2s[:, par], a2T[:, :, bass.ds(G * GN, GN)]).then_inc(staged, 1)
                stage_f(0, 0)
                stage_f(1, 1)
                with act.Fori(1, GROUPS // 2) as it:
                    for par in range(2):
                        stage_f(2 * it + par, par)

            @block.vector
            def _(dve):
                nc.vector.memset(pblk, 0.0)
                nc.vector.memset(ps[:, 4:6], 0.0).then_inc(gram_cleared, 1)

                def normed(G, par):
                    def step(n):
                        dve.wait_ge(c_step, 4 * G + n)
                        apart(dve)
                    for k in range(2):
                        dve.wait_ge(wo_ready, 2 * G + k + 1)
                        xv = XN[:, bass.ds(G * GT + 2 * k, 2)]
                        nc.vector.tensor_tensor(xv, ps[:, 2 + k].rearrange("p (t d) -> p t d", t=2), xv,
                                                ALU.add).then_inc(x1_ready, 1)
                    dve.wait_ge(x1_ready, 2 * G + 2)
                    apart(dve)
                    for t in range(GT):
                        last = nc.vector.bn_stats(st1[:, par, t], XN[:, bass.ds(G * GT + t, 1)].rearrange("p a d -> p (a d)"))
                    last.then_inc(c_step, 1)
                    step(1)
                    for t in range(GT):
                        last = nc.vector.bn_aggr(mv1[:, par, t], st1[:, par, t])
                    last.then_inc(c_step, 1)
                    step(2)
                    nc.vector.tensor_scalar(ve1[:, par], mv1[:, par, :, 1], EPS, None, ALU.add).then_inc(var3_ready, 1)
                    dve.wait_ge(rstd3_ready, G + 1)
                    at_least(dve, gram_done, G - 1)
                    for t in range(GT):
                        last = nc.vector.tensor_scalar(a2g[:, par, t], XN[:, bass.ds(G * GT + t, 1)].rearrange("p a d -> p (a d)"),
                                                       mv1[:, par, t, 0:1], rs1[:, par, t:t + 1],
                                                       ALU.subtract, ALU.mult)
                    last.then_inc(c_step, 1)
                    step(3)
                    rows = [P, GT, D]
                    nc.vector.tensor_tensor(a2g[:, par], a2g[:, par], l2w[:, :].unsqueeze(1).broadcast_to(rows),
                                            ALU.mult).then_inc(c_step, 1)
                    step(4)
                    nc.vector.tensor_tensor(a2g[:, par], a2g[:, par], l2b[:, :].unsqueeze(1).broadcast_to(rows),
                                            ALU.add).then_inc(a2_ready, 1)
                for b in range(NB):
                    dve.wait_ge(xn_back[b], 16)
                for G in (0, 1):
                    normed(G, G)
                with dve.Fori(1, GROUPS // 2) as it:
                    for par in range(2):
                        normed(2 * it + par, par)

                BK = NB * KC
                n = [0]

                def mark(ins):
                    n[0] += 1
                    ins.then_inc(alg_dve, 1)
                    dve.wait_ge(alg_dve, n[0])

                def wide(v):
                    return v.unsqueeze(2).broadcast_to([P, BK, CD])
                dots = ps[:, 0].rearrange("p (k c) -> p k c", k=BK)
                dve.wait_ge(alg_pe, 2)
                for r in range(P // CD):
                    q = slice(r * CD, (r + 1) * CD)
                    last = nc.vector.tensor_copy(dd[q], dots[q, :, q])
                mark(last)
                mark(nc.vector.tensor_tensor(dm, dd, diag[:, :].unsqueeze(1).broadcast_to([P, BK, CD]), ALU.mult))
                mark(nc.vector.tensor_reduce(c4[:, 0], dm, AX.X, ALU.add))
                dve.wait_ge(alg_pe, 3)
                mark(nc.vector.scalar_tensor_tensor(ll, dd, 2.0, ps[:, 1, 0:BK * CD].rearrange("p (k c) -> p k c", k=BK),
                                                    ALU.mult, ALU.subtract))
                mark(nc.vector.tensor_tensor(ll, ll, wide(c4[:, 0]), ALU.subtract))
                for b in range(NB):
                    for c in range(KC):
                        last = nc.vector.tensor_scalar(ll[:, b * KC + c], ll[:, b * KC + c], tauc[:, c:c + 1], None, ALU.mult)
                mark(last)
                mark(nc.vector.tensor_reduce(c4[:, 1], ll, AX.X, ALU.max))
                nc.vector.tensor_tensor(ll, ll, wide(c4[:, 1]), ALU.subtract).then_inc(alg_exp, 1)
                dve.wait_ge(gram_copied, 3)
                mark(nc.vector.tensor_reduce(c4[:, 2], ll, AX.X, ALU.add))
                mark(nc.vector.reciprocal(c4[:, 2], c4[:, 2]))
                for r in range(P // CD):
                    q = slice(r * CD, (r + 1) * CD)
                    last = nc.vector.tensor_tensor(pblk[q, :, q], ll[q], c4[q, 2].unsqueeze(2).broadcast_to([CD, BK, CD]),
                                                   ALU.mult)
                mark(last)
                PB = n[0]
                assert PB == ALG_P, PB
                dve.wait_ge(alg_pe, 5)
                mark(nc.vector.tensor_tensor(mb.rearrange("p b c n -> p (b c) n"),
                                             ps[:, 2:4].rearrange("p b (c n) -> p (b c) n", c=KC),
                                             g2r[:, :].unsqueeze(1).broadcast_to([P, BK, D]), ALU.mult))

                def final(G, par):
                    def step(k):
                        dve.wait_ge(f_step, G + k)
                    at_least(dve, out_stored[par], 16 * (G // 2))
                    for k in range(2):
                        dve.wait_ge(fin_ready, 2 * G + k + 1)
                        last = nc.vector.tensor_tensor(og[:, par, 2 * k:2 * k + 2],
                                                       ps[:, FIN[par] + k].rearrange("p (t d) -> p t d", t=2),
                                                       XN[:, bass.ds(G * GT + 2 * k, 2)], ALU.add)
                        last.then_inc(fin_taken, 1)
                    dve.wait_ge(x_again[par], 16 * (G // 2) + 16)
                    dve.wait_ge(fin_taken, 2 * G + 2)
                    nc.vector.tensor_tensor(og[:, par], og[:, par], xg[:, par], ALU.add).then_inc(f_step, 1)
                    step(1)
                    for t in range(GT):
                        yv = YG[:, bass.ds(G * GT + t, 1)].rearrange("p a d -> p (a d)")
                        last = nc.vector.scalar_tensor_tensor(og[:, par, t], yv, gate[:, bass.ds(G * GT + t, 1)],
                                                              og[:, par, t], ALU.mult, ALU.add)
                    last.then_inc(sum_ready, 1)
                dve.wait_ge(gathered, 16 * TILES)
                for G in (0, 1):
                    final(G, G)
                with dve.Fori(1, GROUPS // 2) as it:
                    for par in range(2):
                        final(2 * it + par, par)

            @block.tensor
            def _(pe):
                def attn_out(G, par):
                    pe.wait_ge(at_copied, G + 1)
                    for c in range(KC):
                        at_least(pe, ring3_taken, use_a(G) + c - 1)
                        for t in range(GT):
                            last = nc.tensor.transpose(ps[:, c, t * P:(t + 1) * P], At[:, par, t, c * P:(c + 1) * P],
                                                       ident[:, :])
                        last.then_inc(ring3_ready, 1)
                    pe.wait_ge(ring3_taken, use_a(G) + 2)
                    for k in range(2):
                        at_least(pe, x1_ready, 2 * (G - 1) + k + 1)
                        for t in range(2):
                            for c in range(KC):
                                last = nc.tensor.matmul(ps[:, 2 + k, t * D:(t + 1) * D],
                                                        AT[:, par, c, (2 * k + t) * P:(2 * k + t + 1) * P], wo[:, c],
                                                        start=(c == 0), stop=(c == KC - 1))
                        last.then_inc(wo_ready, 1)

                def gram_of(G, par):
                    b = G // GB
                    pe.wait_ge(a2_ready, G + 1)
                    for c in range(KC):
                        pe.wait_ge(ring3_taken, use_a2(G) + c - 1)
                        for t in range(GT):
                            last = nc.tensor.transpose(ps[:, c, t * P:(t + 1) * P], a2g[:, par, t, c * P:(c + 1) * P],
                                                       ident[:, :])
                        last.then_inc(ring3_ready, 1)
                    for t in range(GT):
                        for M in range(KC):
                            last = nc.tensor.matmul(ps[:, bass.ds(4 + b, 1), M * D:(M + 1) * D].rearrange("p a n -> p (a n)"),
                                                    a2g[:, par, t, M * P:(M + 1) * P], a2g[:, par, t],
                                                    start=False, stop=False, skip_group_check=True)
                    last.then_inc(gram_done, 1)

                pe.wait_ge(gram_cleared, 1)
                attn_out(0, 0)

                def turn(G, par):
                    attn_out(G + 1, 1 - par)
                    gram_of(G, par)
                turn(0, 0)
                turn(1, 1)
                with pe.Fori(1, GROUPS // 2 - 1) as it:
                    for par in range(2):
                        turn(2 * it + par, par)
                turn(GROUPS - 2, 0)
                gram_of(GROUPS - 1, 1)
                pe.wait_ge(gram_copied, 1)
                for b in range(NB):
                    for M in range(KC):
                        for c in range(KC):
                            last = nc.tensor.matmul(ps[:, 6 + b, M * D:(M + 1) * D], gram[:, b, c, M * P:(M + 1) * P],
                                                    wqkc[:, c], start=(c == 0), stop=(c == KC - 1))
                last.then_inc(alg_pe, 1)
                pe.wait_ge(gram_copied, 2)
                pe.wait_ge(ring3_taken, 4 * GROUPS)
                for b in range(NB):
                    for M in range(KC):
                        for c in range(KC):
                            last = nc.tensor.matmul(ps[:, 0, (b * KC + M) * P:(b * KC + M + 1) * P],
                                                    wqkc[:, c, M * P:(M + 1) * P], t1[:, b, c, M * P:(M + 1) * P],
                                                    start=(c == 0), stop=(c == KC - 1))
                last.then_inc(alg_pe, 1)
                pe.wait_ge(alg_dve, 2)
                nc.tensor.matmul(ps[:, 1, 0:NB * KC * CD], blockones[:, :], dm.rearrange("p k c -> p (k c)"),
                                 start=True, stop=True).then_inc(alg_pe, 1)
                pe.wait_ge(alg_dve, ALG_P)
                for b in range(NB):
                    for c in range(KC):
                        last = nc.tensor.matmul(ps[:, 6 + b, c * D:(c + 1) * D], pblk[:, b * KC + c], woc[:, c],
                                                start=True, stop=True)
                last.then_inc(alg_pe, 1)
                pe.wait_ge(gram_copied, 4)
                for b in range(NB):
                    for k in range(KC):
                        for d in range(KC):
                            last = nc.tensor.matmul(ps[:, 2 + b, k * D:(k + 1) * D], wvcT[:, d, k * P:(k + 1) * P],
                                                    rr[:, b, d], start=(d == 0), stop=(d == KC - 1))
                last.then_inc(alg_pe, 1)
                pe.wait_ge(alg_dve, ALG_P + 1)

                def finals(G, par):
                    b = G // GB
                    pe.wait_ge(staged, G + 1)
                    for k in range(2):
                        at_least(pe, fin_taken, 2 * (G - 2) + k + 1)
                        for t in range(2):
                            for c in range(KC):
                                last = nc.tensor.matmul(ps[:, FIN[par] + k, t * D:(t + 1) * D],
                                                        a2s[:, par, c, (2 * k + t) * P:(2 * k + t + 1) * P],
                                                        mb[:, bass.ds(b, 1), c].rearrange("p a n -> p (a n)"),
                                                        start=(c == 0), stop=(c == KC - 1))
                        last.then_inc(fin_ready, 1)
                for G in (0, 1):
                    finals(G, G)
                with pe.Fori(1, GROUPS // 2) as it:
                    for par in range(2):
                        finals(2 * it + par, par)


_INS = {"x": "L0_attn_x", "Wqk_t": "L0_attn_Wqk_t", "Wv_t": "L0_attn_Wv_t", "Wo_t": "L0_attn_Wo_t",
        "tau_t": "L0_attn_tau_t", "Wqk_c": "L0_attn_Wqk_c", "Wv_c": "L0_attn_Wv_c", "Wo_c": "L0_attn_Wo_c",
        "tau_c": "L0_attn_tau_c", "ln1_w": "L0_attn_ln1_w", "ln1_b": "L0_attn_ln1_b", "ln2_w": "L0_attn_ln2_w",
        "ln2_b": "L0_attn_ln2_b", "gamma1": "L0_attn_gamma1", "gamma2": "L0_attn_gamma2",
        "router_W": "L0_ffn_router_W", "router_b": "L0_ffn_router_b", "W1": "L0_ffn_W1", "b1": "L0_ffn_b1",
        "W2": "L0_ffn_W2", "b2": "L0_ffn_b2"}


def kernel(**inputs):
    import numpy as _np
    import concourse.bacc as _bacc
    from concourse import mybir as _mybir
    from concourse.bass_utils import run_bass_kernel_spmd as _run

    nc = _bacc.Bacc("TRN2", target_bir_lowering=False, num_devices=1)
    arrays, args = {}, {}
    for short, name in _INS.items():
        a = _np.ascontiguousarray(inputs[name])
        arrays[f"in_{name}_dram"] = a
        args[short] = nc.dram_tensor(f"in_{name}_dram", a.shape, _mybir.dt.from_np(a.dtype), kind="ExternalInput").ap()
    args["out"] = nc.dram_tensor("out_0_dram", inputs["L0_attn_x"].shape, _mybir.dt.float32, kind="ExternalOutput").ap()
    build(nc, **args)
    r = _run(nc, [arrays], core_ids=[0])
    return r.results[0]["out_0_dram"]
```

```python
from contextlib import ExitStack

import numpy as np
import concourse.bass as bass
from concourse import mybir

F32 = mybir.dt.float32
BF16 = mybir.dt.bfloat16
I32 = mybir.dt.int32
U32 = mybir.dt.uint32
ALU = mybir.AluOpType
ACT = mybir.ActivationFunctionType
AX = mybir.AxisListType

P = 128
ALG_P = 10
FIN = (2, 6)
EPS = 1e-5


def at_least(eng, sem, value):
    if isinstance(value, int) and value <= 0:
        return
    eng.wait_ge(sem, value)


def apart(eng):
    eng.nop(nofuse=True)


def build(nc, x, Wqk_t, Wv_t, Wo_t, tau_t, Wqk_c, Wv_c, Wo_c, tau_c, ln1_w, ln1_b, ln2_w, ln2_b,
          gamma1, gamma2, router_W, router_b, W1, b1, W2, b2, out):
    NB, S, D = x.shape
    H = tau_t.shape[0]
    CH = tau_c.shape[0]
    DH = D // H
    CD = D // CH
    NE, _, F = W1.shape
    KC = D // P
    FC = F // P
    TOK = NB * S
    TILES = TOK // P
    TB = S // P
    GT = 4
    GROUPS = TILES // GT
    GN = GT * P
    GB = GROUPS // NB
    HC = P // DH
    SLOT_TILES = (TOK - NE) // P + NE
    VW = DH + 1
    NCHUNK = S // 512
    QK_SCALE = 1.0 / float(np.sqrt(DH))
    CQ_SCALE = 1.0 / float(np.sqrt(S))

    xt = x.rearrange("b (t p) d -> p (b t) d", p=P)
    outt = out.rearrange("b (t p) d -> p (b t) d", p=P)

    q_parts = nc.dram_tensor("q_parts", [3, NB * D, S], BF16).ap()
    w_parts = nc.dram_tensor("w_parts", [3, NB * H, S], BF16).ap()
    x_slots = nc.dram_tensor("x_slots", [SLOT_TILES * P, D], F32).ap()
    y_slots = nc.dram_tensor("y_slots", [SLOT_TILES * P, D], F32).ap()
    xn_rows = nc.dram_tensor("xn_rows", [P, TILES, D], F32).ap()
    b1_cols = nc.dram_tensor("b1_cols", [NE, P, FC], F32).ap()

    with ExitStack() as ctx:
        def sb(name, shape, dt=F32):
            return ctx.enter_context(nc.sbuf_tensor(name, shape, dt))

        def sem(name):
            return ctx.enter_context(nc.semaphore(name))

        ps = ctx.enter_context(nc.psum_tensor("ps", [P, 8, 512], F32))

        XNW = sb("XNW", [P, 3 * 2 * KC * F])
        XN = XNW[:, 0:TILES * D].rearrange("p (t d) -> p t d", t=TILES)
        XN_REST = XNW[:, TILES * D:]
        Aflat = sb("A", [P, NB * H * TB * DH])
        A = Aflat[:, :].rearrange("p (h t d) -> p h t d", h=NB * H, t=TB)
        Vflat = sb("V", [P, NB * H * TB * VW])
        V = Vflat[:, :].rearrange("p (h m d) -> p h m d", h=NB * H, m=TB)
        YG = Vflat[:, 0:TILES * D].rearrange("p (t d) -> p t d", t=TILES)
        ident = sb("ident", [P, P])
        wqk = sb("wqk", [P, KC, D])
        wv = sb("wv", [P, KC, D])
        wo = sb("wo", [P, KC, D])
        wqkc = sb("wqkc", [P, KC, D])
        wvc = sb("wvc", [P, KC, D])
        woc = sb("woc", [P, KC, D])
        wvcT = sb("wvcT", [P, KC, D])
        l1w = sb("l1w", [P, KC])
        l1b = sb("l1b", [P, KC])
        l2w = sb("l2w", [P, D])
        l2b = sb("l2b", [P, D])
        g1r = sb("g1r", [P, D])
        g2r = sb("g2r", [P, D])
        tau_e = sb("tau_e", [P, NB * H])
        tauc = sb("tauc", [P, KC])
        ones = sb("ones", [P, P])
        blockones = sb("blockones", [P, P])
        diag = sb("diag", [P, CD])
        gate = sb("gate", [P, TILES])
        pos_u = sb("pos_u", [P, TILES], U32)
        emap = sb("emap", [1, SLOT_TILES], I32)
        nhalf = sb("nhalf", [P, GT])
        mv1 = sb("mv1", [P, 2, GT, 2])
        mv2 = sb("mv2", [P, 2, GT, 2])
        st1 = sb("st1", [P, 2, GT, 6])
        ve1 = sb("ve1", [P, 2, GT])
        ve2 = sb("ve2", [P, 2, GT])
        rs1 = sb("rs1", [P, 2, GT])
        rs2 = sb("rs2", [P, 2, GT])
        xg = sb("xg", [P, 2, GT, D])
        work = sb("work", [P, 16640])

        def views(area):
            at = [0]

            def take(shape, dt=F32):
                n = int(np.prod(shape))
                words = n if dt == F32 else n // 2
                v = area[:, at[0]:at[0] + words]
                at[0] += words
                assert at[0] <= area.shape[1], at[0]
                if dt != F32:
                    v = v.bitcast(dt)
                if len(shape) > 1:
                    names = "abcdef"[:len(shape)]
                    v = v.rearrange("p (" + " ".join(names) + ") -> p " + " ".join(names),
                                    **{k: s for k, s in zip(names, shape)})
                return v
            return take

        take = views(Aflat[:, :])
        xng = take([2, GT, D])
        zg = take([2, GT, D])
        xnT = take([2, KC, GN])
        aT = take([2, KC, GN])
        qp = views(XN_REST)([2, 3, KC, GN], BF16)
        take = views(work[:, :])
        stat_mov = take([2 * S])
        take_b = views(stat_mov)
        stat = take_b([2, S], BF16)
        mov = take_b([2, S], BF16)
        Vh = take([2, TB, VW])
        osb = take([2, 512])
        rec = take([2, TB])
        scale = take([2])
        big = take([2 * S])
        probs = big.rearrange("p (a b) -> p a b", a=2)
        take_b = views(big)
        qf = take_b([KC, GN])
        sq = take_b([KC, GN])
        qr = take_b([KC, GN])
        wf = take_b([GN])
        wr = take_b([GN])
        spare = take([3 * GN])
        wp = views(spare)([2, 3, GN], BF16)
        zero = take([D])
        sel = take([32])
        tri = take([P])
        rw = take([KC, NE])
        rb = take([NE])
        lg = take([TILES, NE])
        ex = take([TILES, NE])
        mask = take([TILES, NE])
        cnt = take([TILES, NE])
        cum = take([TILES, NE])
        s32 = take([4, TILES])
        s8 = take([6, NE])
        s8i = take([NE]).bitcast(I32)
        io_i = take([SLOT_TILES]).bitcast(I32)
        io_k = take([SLOT_TILES])
        ek = take([SLOT_TILES, NE])
        ek1 = take([SLOT_TILES])
        io_e = take([NE])
        io_ei = take([NE]).bitcast(I32)
        b1row = take([P])
        b1T = take([NE * FC])

        xload = [sem("x_loaded0"), sem("x_loaded1")]
        const_loaded = sem("const_loaded")
        late_loaded = sem("late_loaded")
        turned_loaded = sem("turned_loaded")
        pool_step = sem("pool_step")
        stats1_step = sem("stats1_step")
        stats2_step = sem("stats2_step")
        rest_ready = sem("rest_ready")
        q2_ready = sem("q2_ready")
        last_w_step = sem("last_w_step")
        dve_route_step = sem("dve_route_step")
        act_step = sem("act_step")
        consts_made = sem("consts_made")
        zero_made = sem("zero_made")
        slots_zeroed = sem("slots_zeroed")
        var1_ready = sem("var1_ready")
        rstd1_ready = sem("rstd1_ready")
        var2_ready = sem("var2_ready")
        rstd2_ready = sem("rstd2_ready")
        xn_ready = sem("xn_ready")
        z_ready = sem("z_ready")
        xn_kept = [sem("xn_kept0"), sem("xn_kept1")]
        tr_ready = sem("tr_ready")
        tr_taken = sem("tr_taken")
        router_done = sem("router_done")
        q_ready = sem("q_ready")
        scales_made = sem("scales_made")
        q_taken = sem("q_taken")
        q_split = sem("q_split")
        v_ready = sem("v_ready")
        v_taken = sem("v_taken")
        w_ready = sem("w_ready")
        w_taken = sem("w_taken")
        w_split = sem("w_split")
        parts_stored = [sem("parts_stored0"), sem("parts_stored1")]
        b1_turned = sem("b1_turned")
        b1_copied = sem("b1_copied")
        b1_stored = sem("b1_stored")
        lg_ready = sem("lg_ready")
        routed = sem("routed")
        logits_shifted = sem("logits_shifted")
        logits_exp = sem("logits_exp")
        mask_ready = sem("mask_ready")
        ranks_ready = sem("ranks_ready")
        iota_rows = sem("iota_rows")

        rows_set = sem("rows_set")
        rows_zeroed = sem("rows_zeroed")
        stack_loaded = [sem("stack_loaded0"), sem("stack_loaded1")]
        v_copied = sem("v_copied")
        scale_set = sem("scale_set")
        STAT_PARTS = (0, 0, 0, 1, 1, 2)
        MOV_PARTS = (0, 1, 2, 0, 1, 0)
        AUX = 6 * DH
        STACK_DMAS = 14
        PART_DMAS = 5

        def fill_stack(sp, i, hh):
            r0 = i * 2 * DH + hh * DH
            for k in range(6):
                sp.dma_start(stat[k * DH:(k + 1) * DH, hh], q_parts[STAT_PARTS[k], bass.ds(r0, DH), :]
                             ).then_inc(stack_loaded[hh], 16)
                sp.dma_start(mov[k * DH:(k + 1) * DH, hh], q_parts[MOV_PARTS[k], bass.ds(r0, DH), :]
                             ).then_inc(stack_loaded[hh], 16)
            w = w_parts[:, bass.ds(i * 2 + hh, 1), :].rearrange("c h n -> (c h) n")
            sp.dma_start(stat[AUX + 3:AUX + 6, hh], w).then_inc(stack_loaded[hh], 16)
            sp.dma_start(mov[AUX:AUX + 3, hh], w).then_inc(stack_loaded[hh], 16)

        def fill_v(i, hh):
            nc.gpsimd.tensor_copy(scale[:, hh:hh + 1], tau_e[:, bass.ds(2 * i + hh, 1)]).then_inc(scale_set, 1)
            nc.gpsimd.tensor_copy(Vh[:, hh], V[:, bass.ds(2 * i + hh, 1)].rearrange("p h m d -> p (h m) d")
                                  ).then_inc(v_copied, 1)

        N_CONST = 8 + NB
        N_LATE = 7 + CH
        with nc.Block() as block:
            @block.sync
            def _(sp):
                def load_x(G, par):
                    at_least(sp, xn_ready, G - 1)
                    sp.dma_start(xg[:, par], xt[:, bass.ds(G * GT, GT), :]).then_inc(xload[par], 16)

                def keep(G, par):
                    sp.wait_ge(xn_ready, G + 1)
                    sp.dma_start(XN[:, bass.ds(G * GT, GT), :], xng[:, par]).then_inc(xn_kept[par], 16)
                    sp.dma_start(xn_rows[:, bass.ds(G * GT, GT), :], xng[:, par]).then_inc(xn_kept[par], 16)

                def store_parts(G, par):
                    b, tok = G // GB, (G % GB) * GN
                    sp.wait_ge(q_split, G + 1)
                    for part in range(3):
                        sp.dma_start(q_parts[part, bass.ds(b * D, D), bass.ds(tok, GN)]
                                     .rearrange("(c p) n -> p c n", p=P), qp[:, par, part]).then_inc(parts_stored[par], 16)
                    sp.wait_ge(w_split, G + 1)
                    for c in range(KC):
                        sp.dma_start(w_parts[:, bass.ds(b * H + c * HC, HC), bass.ds(tok, GN)].rearrange("c h n -> h c n"),
                                     wp[32 * c:32 * c + HC, par]).then_inc(parts_stored[par], 16)

                load_x(0, 0)
                load_x(1, 1)

                def const(dst, src):
                    sp.dma_start(dst, src).then_inc(const_loaded, 16)
                const(rw, router_W.rearrange("(c p) e -> p c e", p=P))
                const(wqk[:, :, :], Wqk_t.rearrange("(c p) n -> p c n", p=P))
                const(wv[:, :, :], Wv_t.rearrange("(c p) n -> p c n", p=P))
                for c in range(KC):
                    const(l1w[:, c:c + 1], ln1_w[c * P:(c + 1) * P].rearrange("(p a) -> p a", a=1))
                    const(l1b[:, c:c + 1], ln1_b[c * P:(c + 1) * P].rearrange("(p a) -> p a", a=1))
                const(rb, router_b.partition_broadcast(P))
                for b in range(NB):
                    const(tau_e[:, b * H:(b + 1) * H], tau_t.rearrange("h a b -> (h a b)").partition_broadcast(P))
                for G in (0, 1):
                    keep(G, G)
                    load_x(G + 2, G)
                    if G == 1:
                        store_parts(0, 0)
                sp.dma_start(wvc[:, :, :], Wv_c.rearrange("(c p) n -> p c n", p=P)).then_inc(turned_loaded, 16)
                sp.dma_start(b1row[0:NE * FC], b1.rearrange("e (c p) -> (e c) p", p=P)).then_inc(turned_loaded, 16)
                with sp.Fori(1, GROUPS // 2 - 1) as it:
                    for par in range(2):
                        G = 2 * it + par
                        keep(G, par)
                        load_x(G + 2, par)
                        store_parts(G - 1, 1 - par)
                sp.wait_ge(parts_stored[0], PART_DMAS * 16 * 3)
                sp.wait_ge(parts_stored[1], PART_DMAS * 16 * 2)
                sp.wait_ge(rows_set, 1)
                fill_stack(sp, 0, 0)
                for G in (GROUPS - 2, GROUPS - 1):
                    keep(G, G % 2)
                    store_parts(G - 1, 1 - G % 2)
                fill_stack(sp, 0, 1)
                store_parts(GROUPS - 1, 1)
                sp.wait_ge(b1_copied, 1)
                sp.dma_start(b1_cols.rearrange("e p c -> p e c"),
                             b1T.rearrange("p (e c) -> p e c", e=NE)).then_inc(b1_stored, 16)

            @block.gpsimd
            def _(pool):
                nc.gpsimd.memset(nhalf[:, :], -0.5)
                nc.gpsimd.memset(zero, 0.0).then_inc(zero_made, 1)
                nc.gpsimd.memset(ident[:, :], 0.0)
                nc.gpsimd.memset(ones[:, :], 1.0)
                nc.gpsimd.memset(tri, 1.0)
                nc.gpsimd.memset(sel[:, 0:HC], -0.5)
                nc.gpsimd.memset(sel[:, HC:], 0.0)
                nc.gpsimd.memset(blockones[:, :], 1.0)
                nc.gpsimd.memset(V[:, :, :, DH:VW], 1.0)
                nc.gpsimd.iota(io_i[0:1], pattern=[[1, SLOT_TILES]], base=0, channel_multiplier=0).then_inc(pool_step, 1)
                pool.wait_ge(pool_step, 1)
                nc.gpsimd.affine_select(out=ident[:, :], in_=ident[:, :], compare_op=ALU.not_equal, fill=1.0,
                                        base=0, pattern=[[-1, P]], channel_multiplier=1)
                nc.gpsimd.affine_select(out=tri, in_=tri, compare_op=ALU.is_gt, fill=0.0,
                                        base=0, pattern=[[1, P]], channel_multiplier=-1)
                nc.gpsimd.affine_select(out=sel[:, 0:HC], in_=sel[:, 0:HC], compare_op=ALU.is_ge, fill=0.0,
                                        base=0, pattern=[[-DH, HC]], channel_multiplier=1)
                nc.gpsimd.affine_select(out=blockones[:, :].rearrange("p (a b) -> p a b", b=CD),
                                        in_=blockones[:, :].rearrange("p (a b) -> p a b", b=CD),
                                        compare_op=ALU.is_ge, fill=0.0, base=0, pattern=[[-CD, P // CD], [0, CD]],
                                        channel_multiplier=1).then_inc(pool_step, 1)
                pool.wait_ge(pool_step, 2)
                nc.gpsimd.affine_select(out=sel[:, 0:HC], in_=sel[:, 0:HC], compare_op=ALU.is_ge, fill=0.0,
                                        base=DH - 1, pattern=[[DH, HC]], channel_multiplier=-1)
                nc.gpsimd.affine_select(out=blockones[:, :].rearrange("p (a b) -> p a b", b=CD),
                                        in_=blockones[:, :].rearrange("p (a b) -> p a b", b=CD),
                                        compare_op=ALU.is_ge, fill=0.0, base=CD - 1, pattern=[[CD, P // CD], [0, CD]],
                                        channel_multiplier=-1)
                nc.gpsimd.tensor_copy(io_k[0:1], io_i[0:1]).then_inc(consts_made, 1)
                nc.gpsimd.iota(io_ei, pattern=[[1, NE]], base=0, channel_multiplier=0).then_inc(pool_step, 1)
                pool.wait_ge(pool_step, 3)
                nc.gpsimd.tensor_copy(io_e, io_ei).then_inc(iota_rows, 1)

                def rstd1(G, par):
                    pool.wait_ge(var1_ready, G + 1)
                    nc.gpsimd.tensor_tensor(rs1[:, par], ve1[:, par], nhalf[:, :], ALU.pow).then_inc(rstd1_ready, 1)

                def rstd2(G, par):
                    pool.wait_ge(var2_ready, G + 1)
                    nc.gpsimd.tensor_tensor(rs2[:, par], ve2[:, par], nhalf[:, :], ALU.pow).then_inc(rstd2_ready, 1)

                def back(G, par):
                    def step(n):
                        pool.wait_ge(pool_step, 3 + 2 * G + n)
                    rows = slice(0, 64)
                    w = wp[rows, par]
                    pool.wait_ge(w_taken, G + 1)
                    nc.gpsimd.tensor_tensor(wr[rows], wf[rows], w[:, 0], ALU.subtract).then_inc(pool_step, 1)
                    step(1)
                    apart(pool)
                    nc.gpsimd.tensor_copy(w[:, 1], wr[rows]).then_inc(pool_step, 1)
                    step(2)
                    nc.gpsimd.tensor_tensor(w[:, 2], wr[rows], w[:, 1], ALU.subtract).then_inc(w_split, 1)

                def group(G, par, first=False, last=False):
                    rstd2(G, par)
                    if not last:
                        rstd1(G + 1, 1 - par)
                    if not first:
                        back(G - 1, 1 - par)

                rstd1(0, 0)
                group(0, 0, first=True)
                group(1, 1)
                with pool.Fori(1, GROUPS // 2 - 1) as it:
                    for par in range(2):
                        group(2 * it + par, par)
                pool.wait_ge(scales_made, 1)
                pool.wait_ge(v_taken, 2 * GB)
                fill_v(0, 0)
                group(GROUPS - 2, 0)
                fill_v(0, 1)
                group(GROUPS - 1, 1, last=True)

            @block.vector
            def _(dve):
                def stats_x(G, par):
                    def step(n):
                        dve.wait_ge(stats1_step, G * 2 + n)
                        apart(dve)
                    dve.wait_ge(xload[par], 16 * (G // 2) + 16)
                    apart(dve)
                    for t in range(GT):
                        last = nc.vector.bn_stats(st1[:, par, t], xg[:, par, t])
                    last.then_inc(stats1_step, 1)
                    step(1)
                    for t in range(GT):
                        last = nc.vector.bn_aggr(mv1[:, par, t], st1[:, par, t])
                    last.then_inc(stats1_step, 1)
                    step(2)
                    nc.vector.tensor_scalar(ve1[:, par], mv1[:, par, :, 1], EPS, None, ALU.add).then_inc(var1_ready, 1)

                def make_xn(G, par):
                    def step(n):
                        dve.wait_ge(stats2_step, G * 2 + n)
                        apart(dve)
                    dve.wait_ge(rstd1_ready, G + 1)
                    at_least(dve, xn_kept[par], 32 * (G // 2))
                    at_least(dve, tr_ready, 4 * (G - 1))
                    for t in range(GT):
                        last = nc.vector.tensor_scalar(xng[:, par, t], xg[:, par, t], mv1[:, par, t, 0:1],
                                                       rs1[:, par, t:t + 1], ALU.subtract, ALU.mult)
                    last.then_inc(xn_ready, 1)
                    dve.wait_ge(xn_ready, G + 1)
                    apart(dve)
                    for t in range(GT):
                        last = nc.vector.bn_stats(st1[:, par, t], xng[:, par, t])
                    last.then_inc(stats2_step, 1)
                    step(1)
                    for t in range(GT):
                        last = nc.vector.bn_aggr(mv2[:, par, t], st1[:, par, t])
                    last.then_inc(stats2_step, 1)
                    step(2)
                    nc.vector.tensor_scalar(ve2[:, par], mv2[:, par, :, 1], EPS, None, ALU.add).then_inc(var2_ready, 1)

                def make_z(G, par):
                    dve.wait_ge(rstd2_ready, G + 1)
                    for t in range(GT):
                        last = nc.vector.tensor_scalar(zg[:, par, t], xng[:, par, t], mv2[:, par, t, 0:1],
                                                       rs2[:, par, t:t + 1], ALU.subtract, ALU.mult)
                    last.then_inc(z_ready, 1)

                def back(G, par):
                    dve.wait_ge(q_taken, 2 * G + 2)
                    at_least(dve, q_split, G)
                    nc.vector.tensor_tensor(qr, qf, qp[:, par, 0], ALU.subtract).then_inc(rest_ready, 1)
                    dve.wait_ge(rest_ready, G + 1)
                    nc.vector.tensor_copy(qp[:, par, 1], qr).then_inc(q2_ready, 1)
                    dve.wait_ge(q2_ready, G + 1)
                    nc.vector.tensor_tensor(qp[:, par, 2], qr, qp[:, par, 1], ALU.subtract).then_inc(q_split, 1)

                def group(G, par, first=False, last=False):
                    make_xn(G, par)
                    if not last:
                        stats_x(G + 1, 1 - par)
                    make_z(G, par)
                    if not first:
                        back(G - 1, 1 - par)

                words = stat_mov[AUX:P]
                nc.vector.memset(words, 0.0).then_inc(rows_zeroed, 1)
                stats_x(0, 0)
                group(0, 0, first=True)
                dve.wait_ge(rows_zeroed, 1)
                pair = float(np.array([0x3F803F80], np.uint32).view(np.float32)[0])
                nc.vector.memset(stat_mov[AUX:AUX + 6], pair).then_inc(rows_set, 1)
                dve.wait_ge(const_loaded, 16 * N_CONST)
                nc.vector.tensor_scalar(tau_e[:, :], tau_e[:, :], 2.0 * QK_SCALE, None, ALU.mult).then_inc(scales_made, 1)
                group(1, 1)
                with dve.Fori(1, GROUPS // 2 - 1) as it:
                    for par in range(2):
                        group(2 * it + par, par)
                group(GROUPS - 2, 0)
                group(GROUPS - 1, 1, last=True)
                dve.wait_ge(router_done, GROUPS)
                nc.vector.tensor_tensor(lg, ps[:, 2, 0:TILES * NE].rearrange("p (t e) -> p t e", e=NE),
                                        rb.unsqueeze(1).broadcast_to([P, TILES, NE]), ALU.add).then_inc(lg_ready, 1)
                back(GROUPS - 1, 1)
                rows, w = slice(0, 64), wp[0:64, 1]
                dve.wait_ge(w_taken, GROUPS)
                dve.wait_ge(w_split, GROUPS - 1)
                nc.vector.tensor_tensor(wr[rows], wf[rows], w[:, 0], ALU.subtract).then_inc(last_w_step, 1)
                dve.wait_ge(last_w_step, 1)
                nc.vector.tensor_copy(w[:, 1], wr[rows]).then_inc(last_w_step, 1)
                dve.wait_ge(last_w_step, 2)
                nc.vector.tensor_tensor(w[:, 2], wr[rows], w[:, 1], ALU.subtract).then_inc(w_split, 1)

            @block.scalar
            def _(act):
                def group(G, par):
                    for k in range(4):
                        act.wait_ge(tr_ready, 4 * G + k + 1)
                        if k == 0:
                            at_least(act, router_done, G - 1)
                        if k == 2:
                            at_least(act, v_ready, 2 * (G - 1))
                        if k < 2:
                            nc.scalar.copy(xnT[:, par, k], ps[:, k]).then_inc(tr_taken, 1)
                        else:
                            nc.scalar.activation(aT[:, par, k - 2], ps[:, k - 2], ACT.Identity,
                                                 bias=l1b[:, k - 2:k - 1], scale=l1w[:, k - 2:k - 1]).then_inc(tr_taken, 1)
                    at_least(act, parts_stored[par], PART_DMAS * 16 * (G // 2))
                    for M in range(KC):
                        act.wait_ge(q_ready, 2 * G + M + 1)
                        if M == 0:
                            at_least(act, rest_ready, G)
                            at_least(act, w_ready, G)
                        nc.scalar.copy(qp[:, par, 0, M], ps[:, 3 + M])
                        nc.scalar.activation(sq[:, M], ps[:, 3 + M], ACT.Square)
                        nc.scalar.copy(qf[:, M], ps[:, 3 + M]).then_inc(q_taken, 1)
                    b, m0 = G // GB, (G % GB) * GT
                    for k in range(2):
                        act.wait_ge(v_ready, 2 * G + k + 1)
                        nc.scalar.copy(
                            V[:, bass.ds(b * H, H), bass.ds(m0 + 2 * k, 2), 0:DH].rearrange("p h m d -> p m h d"),
                            ps[:, 5 + k].rearrange("p (m h d) -> p m h d", m=2, h=H)).then_inc(v_taken, 1)
                    act.wait_ge(w_ready, G + 1)
                    at_least(act, w_split, G)
                    nc.scalar.copy(wp[0:64, par, 0], ps[0:64, 7])
                    nc.scalar.copy(wf[0:64], ps[0:64, 7]).then_inc(w_taken, 1)

                act.wait_ge(const_loaded, 16 * N_CONST)
                group(0, 0)
                group(1, 1)
                with act.Fori(1, GROUPS // 2) as it:
                    for par in range(2):
                        group(2 * it + par, par)
                act.wait_ge(b1_turned, 1)
                nc.scalar.copy(b1T, ps[:, 0, 0:NE * FC]).then_inc(b1_copied, 1)
                nc.scalar.copy(wvcT[:, :, :], ps[:, 1].rearrange("p (a b) -> p a b", a=KC))

            @block.tensor
            def _(pe):
                def turn(G, par):
                    for k in range(4):
                        src = xng if k < 2 else zg
                        if k == 0:
                            pe.wait_ge(xn_ready, G + 1)
                        if k == 2:
                            pe.wait_ge(z_ready, G + 1)
                        at_least(pe, tr_taken, 4 * G + k - 1)
                        for t in range(GT):
                            last = nc.tensor.transpose(ps[:, k % 2, t * P:(t + 1) * P],
                                                       src[:, par, t, (k % 2) * P:(k % 2 + 1) * P], ident[:, :])
                        last.then_inc(tr_ready, 1)

                def products(G, par):
                    pe.wait_ge(tr_taken, 4 * G + 2)
                    for t in range(GT):
                        for c in range(KC):
                            last = nc.tensor.matmul(ps[:, 2, bass.ds((G * GT + t) * NE, NE)],
                                                    xnT[:, par, c, t * P:(t + 1) * P], rw[:, c],
                                                    start=(c == 0), stop=(c == KC - 1))
                    last.then_inc(router_done, 1)
                    pe.wait_ge(tr_taken, 4 * G + 4)
                    for M in range(KC):
                        at_least(pe, q_taken, 2 * (G - 1) + M + 1)
                        for c in range(KC):
                            last = nc.tensor.matmul(ps[:, 3 + M], wqk[:, c, M * P:(M + 1) * P], aT[:, par, c],
                                                    start=(c == 0), stop=(c == KC - 1))
                        last.then_inc(q_ready, 1)
                    for k in range(2):
                        at_least(pe, v_taken, 2 * (G - 1) + k + 1)
                        for t in range(2):
                            for c in range(KC):
                                last = nc.tensor.matmul(ps[:, 5 + k, t * D:(t + 1) * D],
                                                        aT[:, par, c, (2 * k + t) * P:(2 * k + t + 1) * P], wv[:, c],
                                                        start=(c == 0), stop=(c == KC - 1))
                        last.then_inc(v_ready, 1)
                    pe.wait_ge(q_taken, 2 * G + 2)
                    at_least(pe, w_taken, G)
                    for c in range(KC):
                        last = nc.tensor.matmul(ps[32 * c:32 * (c + 1), 7], sel, sq[:, c], start=True, stop=True,
                                                tile_position=(0, 32 * c))
                    last.then_inc(w_ready, 1)

                pe.wait_ge(consts_made, 1)
                pe.wait_ge(const_loaded, 16 * N_CONST)
                for G in (0, 1):
                    turn(G, G)
                    products(G, G)
                with pe.Fori(1, GROUPS // 2) as it:
                    for par in range(2):
                        turn(2 * it + par, par)
                        products(2 * it + par, par)
                pe.wait_ge(turned_loaded, 16 * 2)
                pe.wait_ge(tr_taken, 4 * GROUPS)
                nc.tensor.transpose(ps[:, 0, 0:NE * FC], b1row[0:NE * FC], ident[0:NE * FC, 0:NE * FC])
                for d in range(KC):
                    for k in range(KC):
                        last = nc.tensor.transpose(ps[:, 1, (d * KC + k) * P:(d * KC + k + 1) * P],
                                                   wvc[:, k, d * P:(d + 1) * P], ident[:, :])
                last.then_inc(b1_turned, 1)

        take_w = views(XNW[:, :])
        w1s = take_w([3, KC, F])
        w2s = take_w([3, FC, D])
        b1s = take([3, FC])
        b2s = take([3, D])
        xs = take([3, D])
        hT = take([FC, P])
        take_s = views(spare)
        xsT = take_s([3, KC, P])
        ysb = take_s([3, D])
        PAIRS = NB * H // 2
        STEPS = 2 * TB
        FIRST = PAIRS - SLOT_TILES // 3
        assert SLOT_TILES == 3 * (PAIRS - FIRST)
        SUBS = 10
        TILE_DMAS = 5
        AV, Y, RING = 4, 5, 6

        tile_loaded = [sem(f"tile_loaded{k}") for k in range(3)]
        logits_ready = sem("logits_ready")
        probs_ready = sem("probs_ready")
        av_done = sem("av_done")
        o_cleared = sem("o_cleared")
        o_copied = sem("o_copied")
        rec_ready = sem("rec_ready")
        ring_ready = sem("ring_ready")
        ring_taken = sem("ring_taken")
        y_ready = sem("y_ready")
        y_taken = sem("y_taken")
        y_stored = [sem(f"y_stored{k}") for k in range(3)]
        scattered = sem("scattered")
        a_ready = sem("a_ready")

        def ring_base(i, experts):
            if isinstance(i, int) and i == 0:
                return 0
            if not experts:
                return 2 * i - 1
            return 2 * FIRST - 1 + 32 * (i - FIRST)

        def plan(i, experts):
            steps = []
            for s in range(STEPS):
                uses = []
                if experts and s < 3 * SUBS:
                    sub = s % SUBS
                    if sub == 0:
                        uses += [("x", s // SUBS, 0), ("x", s // SUBS, 1)]
                    elif sub <= FC:
                        uses += [("h", s // SUBS, sub - 1)]
                if s == 1 and not (isinstance(i, int) and i == 0):
                    uses += [("o", 1, -1)]
                if s == TB + 1:
                    uses += [("o", 0, 0)]
                steps.append(uses)
            return steps

        def use_numbers(uses_by_step):
            table, k = {}, 0
            for uses in uses_by_step:
                for u in uses:
                    table[u] = k
                    k += 1
            return table

        def bank(i, k):
            first = 0 if isinstance(i, int) and i == 0 else 1
            return RING + (first + k) % 2

        with nc.Block() as block:
            @block.sync
            def _(sp):
                def load_stack(i, hh):
                    at_least(sp, logits_ready, 2 * (STEPS * (i - 1) + TB * (hh + 1)))
                    fill_stack(sp, i, hh)

                def load_tile(i, tt):
                    n = 3 * (i - FIRST) + tt
                    at_least(sp, y_taken, n - 2)
                    e = sp.value_load(emap[0:1, bass.ds(n, 1)], min_val=0, max_val=NE - 1)

                    def get(dst, src):
                        sp.dma_start(dst, src).then_inc(tile_loaded[tt], 16)
                    get(xs[:, tt], x_slots[bass.ds(n * P, P), :])
                    get(w1s[:, tt], W1[bass.ds(e, 1)].rearrange("e (c p) f -> p (e c) f", p=P))
                    get(b1s[:, tt], b1_cols[bass.ds(e, 1)].rearrange("e p c -> (e p) c"))
                    get(w2s[:, tt], W2[bass.ds(e, 1)].rearrange("e (c p) n -> p (e c) n", p=P))
                    get(b2s[:, tt], b2[bass.ds(e, 1), :].broadcast_to([P, D]))

                sp.wait_ge(zero_made, 1)
                sp.dma_start(x_slots.rearrange("(k p) d -> p k d", p=P),
                             zero.unsqueeze(1).broadcast_to([P, SLOT_TILES, D])).then_inc(slots_zeroed, 16)
                for dst, src in ((wo, Wo_t), (wqkc, Wqk_c), (woc, Wo_c)):
                    sp.dma_start(dst[:, :, :], src.rearrange("(c p) n -> p c n", p=P)).then_inc(late_loaded, 16)
                for dst, src in ((l2w, ln2_w), (l2b, ln2_b), (g1r, gamma1), (g2r, gamma2)):
                    sp.dma_start(dst[:, :], src.partition_broadcast(P)).then_inc(late_loaded, 16)
                for h in range(CH):
                    c, r = h // 4, h % 4
                    sp.dma_start(tauc[r * CD:(r + 1) * CD, c:c + 1],
                                 tau_c.rearrange("h a b -> h (a b)")[h:h + 1, :].broadcast_to([CD, 1])
                                 ).then_inc(late_loaded, 16)
                for par in range(2):
                    sp.wait_ge(parts_stored[par], PART_DMAS * 16 * GROUPS // 2)
                for i in range(FIRST - 1):
                    load_stack(i + 1, 0)
                    load_stack(i + 1, 1)
                sp.wait_ge(routed, 1)
                sp.wait_ge(b1_stored, 16)
                sp.wait_ge(scattered, 16 * TILES)
                for tt in range(3):
                    load_tile(FIRST, tt)
                load_stack(FIRST, 0)
                load_stack(FIRST, 1)

                def ahead(i):
                    load_tile(i + 1, 0)
                    load_stack(i + 1, 0)
                    load_tile(i + 1, 1)
                    load_tile(i + 1, 2)
                    load_stack(i + 1, 1)
                with sp.Fori(FIRST, PAIRS - 1) as i:
                    ahead(i)

            @block.gpsimd
            def _(pool):
                def copy_v(i, hh):
                    at_least(pool, av_done, STEPS * (i - 1) + TB * (hh + 1))
                    apart(pool)
                    fill_v(i, hh)

                def store_y(i, tt):
                    n = 3 * (i - FIRST) + tt
                    pool.wait_ge(y_taken, n + 1)
                    pool.dma_start(y_slots[bass.ds(n * P, P), :], ysb[:, tt]).then_inc(y_stored[tt], 16)

                pool.wait_ge(routed, 1)
                pool.wait_ge(slots_zeroed, 16)
                for par in range(2):
                    pool.wait_ge(xn_kept[par], 32 * GROUPS // 2)
                for t in range(TILES):
                    if t == TILES // 2:
                        copy_v(1, 0)
                    nc.gpsimd.indirect_dma_start(x_slots, bass.IndirectOffsetOnAxis(ap=pos_u[:, t:t + 1], axis=0),
                                                 XN[:, t], None).then_inc(scattered, 16)
                copy_v(1, 1)
                for i in range(2, FIRST + 1):
                    copy_v(i, 0)
                    copy_v(i, 1)
                with pool.Fori(FIRST, PAIRS - 1) as i:
                    store_y(i, 0)
                    copy_v(i + 1, 0)
                    store_y(i, 1)
                    store_y(i, 2)
                    copy_v(i + 1, 1)
                for tt in range(3):
                    store_y(PAIRS - 1, tt)
                for tt in range(3):
                    pool.wait_ge(y_stored[tt], 16 * (PAIRS - FIRST))

            @block.scalar
            def _(act):
                def body(i, route=False):
                    for s in range(STEPS):
                        g = STEPS * i + s
                        if route and s == 2:
                            act.wait_ge(logits_shifted, 1)
                            nc.scalar.activation(ex, lg, ACT.Exp).then_inc(logits_exp, 1)
                        if s % TB == 0:
                            act.wait_ge(scale_set, 2 * i + s // TB + 1)
                        for half in range(2):
                            act.wait_ge(logits_ready, 2 * g + half + 1)
                            if half == 0:
                                at_least(act, av_done, g - 1)
                            nc.scalar.activation(probs[:, s % 2, half * 1024:(half + 1) * 1024],
                                                 ps[:, 2 * half:2 * half + 2].rearrange("p a b -> p (a b)"),
                                                 ACT.Exp, scale=scale[:, s // TB:s // TB + 1]
                                                 ).then_inc(probs_ready, 1)
                body(0, route=True)
                with act.Fori(1, PAIRS) as i:
                    body(i)

            @block.vector
            def _(dve):
                nc.vector.memset(ps[:, AV], 0.0).then_inc(o_cleared, 1)

                def take_o(i, hh):
                    head = 2 * i + hh
                    dve.wait_ge(av_done, TB * (head + 1))
                    nc.vector.tensor_copy(osb[:, hh], ps[:, AV]).then_inc(o_copied, 1)

                def norm(i, experts, use, hh, shift):
                    head = 2 * (i + shift) + hh
                    k = use[("o", hh, shift)]
                    t4 = ps[:, bank(i, k)].rearrange("p (k j c) -> p j k c", k=4, j=NCHUNK)
                    dve.wait_ge(ring_ready, ring_base(i, experts) + k + 1)
                    r = rec[:, hh].rearrange("p (j k) -> p j k", j=NCHUNK)
                    nc.vector.reciprocal(r, t4[:, :, :, DH]).then_inc(rec_ready, 1)
                    dve.wait_ge(rec_ready, head + 1)
                    nc.vector.tensor_tensor(
                        A[:, bass.ds(head, 1)].rearrange("p h (j k) d -> p (h j) k d", j=NCHUNK),
                        t4[:, :, :, 0:DH], r.unsqueeze(3).broadcast_to([P, NCHUNK, 4, DH]), ALU.mult
                    ).then_inc(ring_taken, 1)

                def body(i, experts):
                    uses = plan(i, experts)
                    use = use_numbers(uses)
                    for s in range(STEPS):
                        if s == 0 and not (isinstance(i, int) and i == 0):
                            take_o(i - 1, 1)
                        if s == TB:
                            take_o(i, 0)
                        for u in uses[s]:
                            kind, a, b = u
                            k = use[u]
                            if kind == "o":
                                norm(i, experts, use, a, b)
                                continue
                            dve.wait_ge(ring_ready, ring_base(i, experts) + k + 1)
                            if kind == "x":
                                nc.vector.tensor_copy(xsT[:, a, b], ps[:, bank(i, k), 0:P]).then_inc(ring_taken, 1)
                            else:
                                nc.vector.tensor_scalar(hT[:, b], ps[:, bank(i, k), 0:P], b1s[:, a, b:b + 1], 0.0,
                                                        ALU.add, ALU.max).then_inc(ring_taken, 1)
                        if experts and s < 3 * SUBS and s % SUBS == SUBS - 1:
                            tt = s // SUBS
                            dve.wait_ge(y_ready, 3 * (i - FIRST) + tt + 1)
                            at_least(dve, y_stored[tt], 16 * (i - FIRST))
                            nc.vector.tensor_tensor(ysb[:, tt], ps[:, Y, 0:D], b2s[:, tt], ALU.add).then_inc(y_taken, 1)

                n = [0]

                def mark(ins):
                    n[0] += 1
                    ins.then_inc(dve_route_step, 1)
                    dve.wait_ge(dve_route_step, n[0])

                def over_experts(v):
                    return v.unsqueeze(2).broadcast_to([P, TILES, NE])

                def over_tiles(v):
                    return v.unsqueeze(1).broadcast_to([P, TILES, NE])
                mx, sm, pm, idx = (s32[:, k] for k in range(4))
                dve.wait_ge(lg_ready, 1)
                mark(nc.vector.tensor_reduce(mx, lg, AX.X, ALU.max))
                nc.vector.tensor_tensor(lg, lg, over_experts(mx), ALU.subtract).then_inc(logits_shifted, 1)
                dve.wait_ge(logits_exp, 1)
                mark(nc.vector.tensor_reduce(sm, ex, AX.X, ALU.add))
                mark(nc.vector.reciprocal(sm, sm))
                mark(nc.vector.tensor_tensor(ex, ex, over_experts(sm), ALU.mult))
                mark(nc.vector.tensor_reduce(gate[:, :], ex, AX.X, ALU.max))
                mark(nc.vector.tensor_tensor(lg, ex, over_experts(gate[:, :]), ALU.is_equal))
                dve.wait_ge(consts_made, 1)
                dve.wait_ge(iota_rows, 1)
                mark(nc.vector.tensor_scalar(s8[:, 0], io_e, float(NE), None, ALU.add))
                mark(nc.vector.scalar_tensor_tensor(lg, lg, -float(NE), over_tiles(s8[:, 0]), ALU.mult, ALU.add))
                mark(nc.vector.tensor_reduce(idx, lg, AX.X, ALU.min))
                nc.vector.tensor_tensor(mask, over_tiles(io_e), over_experts(idx), ALU.is_equal).then_inc(mask_ready, 1)
                dve.wait_ge(ranks_ready, 1)
                mark(nc.vector.tensor_copy(cnt, ps[:, Y, TILES * NE:2 * TILES * NE].rearrange("p (t e) -> p t e", e=NE)))
                for e in range(NE):
                    last = nc.vector.tensor_tensor_scan(cum[:, :, e], ones[:, 0:TILES], cnt[:, :, e], 0.0,
                                                        ALU.mult, ALU.add)
                mark(last)
                mark(nc.vector.tensor_scalar(s8[:, 1], cum[:, TILES - 1], float(P - 1), None, ALU.add))
                mark(nc.vector.tensor_copy(s8i, s8[:, 1]))
                mark(nc.vector.tensor_scalar(s8i, s8i, 7, None, ALU.arith_shift_right))
                mark(nc.vector.tensor_copy(s8[:, 2], s8i))
                mark(nc.vector.tensor_tensor_scan(s8[:, 3], ones[:, 0:NE], s8[:, 2], 0.0, ALU.mult, ALU.add))
                mark(nc.vector.tensor_tensor(s8[:, 4], s8[:, 3], s8[:, 2], ALU.subtract))
                mark(nc.vector.tensor_scalar(s8[:, 5], s8[:, 4], float(P), None, ALU.mult))
                mark(nc.vector.tensor_tensor(cum, cum, cnt, ALU.subtract))
                mark(nc.vector.tensor_tensor(cum, cum, over_tiles(s8[:, 5]), ALU.add))
                mark(nc.vector.tensor_tensor(cum, ps[:, Y, 0:TILES * NE].rearrange("p (t e) -> p t e", e=NE), cum, ALU.add))
                mark(nc.vector.tensor_tensor(cum, cum, mask, ALU.mult))
                mark(nc.vector.tensor_reduce(mx, cum, AX.X, ALU.add))
                ends = s8[0:1, 3].unsqueeze(1).broadcast_to([1, SLOT_TILES, NE])
                mark(nc.vector.tensor_tensor(ek[0:1], io_k[0:1].unsqueeze(2).broadcast_to([1, SLOT_TILES, NE]), ends,
                                             ALU.is_ge))
                mark(nc.vector.tensor_reduce(ek1[0:1], ek[0:1], AX.X, ALU.add))
                mark(nc.vector.tensor_scalar(ek1[0:1], ek1[0:1], float(NE - 1), None, ALU.min))
                mark(nc.vector.tensor_copy(emap[:, :], ek1[0:1]))
                nc.vector.tensor_copy(pos_u[:, :], mx).then_inc(routed, 1)
                dve.wait_ge(late_loaded, 16 * N_LATE)
                mark(nc.vector.tensor_tensor(wo[:, :, :], wo[:, :, :],
                                             g1r[:, :].unsqueeze(1).broadcast_to([P, KC, D]), ALU.mult))
                mark(nc.vector.tensor_scalar(tauc[:, :], tauc[:, :], CQ_SCALE, None, ALU.mult))
                mark(nc.vector.tensor_reduce(diag[:, :], ident[:, :].rearrange("p (a b) -> p b a", b=CD), AX.X, ALU.add))

                body(0, False)
                with dve.Fori(1, FIRST) as i:
                    body(i, False)
                body(FIRST, True)
                with dve.Fori(FIRST + 1, PAIRS) as i:
                    body(i, True)
                take_o(PAIRS - 1, 1)
                norm(PAIRS, True, {("o", 1, -1): 0}, 1, -1)

            @block.tensor
            def _(pe):
                def logits(i, s):
                    hh, m = s // TB, s % TB
                    g = STEPS * i + s
                    if m == 0:
                        pe.wait_ge(stack_loaded[hh], 16 * STACK_DMAS * (i + 1))
                    for half in range(2):
                        at_least(pe, probs_ready, 2 * g + half - 1)
                        for j in range(2):
                            q0 = (2 * half + j) * 512
                            last = nc.tensor.matmul(ps[:, 2 * half + j], stat[:, hh, m * P:(m + 1) * P],
                                                    mov[:, hh, q0:q0 + 512], start=True, stop=True)
                        last.then_inc(logits_ready, 1)

                def values(i, s):
                    hh, m = s // TB, s % TB
                    g = STEPS * i + s
                    if m == 0:
                        pe.wait_ge(v_copied, 2 * i + hh + 1)
                        at_least(pe, o_copied, 2 * i + hh)
                    pe.wait_ge(probs_ready, 2 * g + 2)
                    for j in range(NCHUNK):
                        last = nc.tensor.matmul(ps[32 * j:32 * j + VW, AV], Vh[:, hh, m],
                                                probs[:, s % 2, j * 512:(j + 1) * 512],
                                                start=(m == 0), stop=(m == TB - 1), tile_position=(0, 32 * j))
                    last.then_inc(av_done, 1)

                def turn_o(i, k, hh, shift):
                    pe.wait_ge(o_copied, 2 * (i + shift) + hh + 1)
                    for c in range(4):
                        last = nc.tensor.transpose(ps[:, bank(i, k), c * P:(c + 1) * P],
                                                   osb[:, hh, c * P:(c + 1) * P], ident[:, :])
                    last.then_inc(ring_ready, 1)

                def body(i, experts, last_one=False, route=False):
                    uses = plan(i, experts)
                    use = use_numbers(uses)
                    for s in range(STEPS):
                        if s + 1 < STEPS:
                            logits(i, s + 1)
                        elif not last_one:
                            logits(i + 1, 0)
                        if route and s == 10:
                            pe.wait_ge(mask_ready, 1)
                            picks, n = mask.rearrange("p t e -> p (t e)"), TILES * NE
                            nc.tensor.matmul(ps[:, Y, 0:n], tri, picks, start=True, stop=True)
                            nc.tensor.matmul(ps[:, Y, n:2 * n], ones[:, :], picks, start=True, stop=True
                                             ).then_inc(ranks_ready, 1)
                        sub, tt = s % SUBS, s // SUBS
                        for u in uses[s]:
                            kind, a, b = u
                            k = use[u]
                            at_least(pe, ring_taken, ring_base(i, experts) + k - 1)
                            if kind == "o":
                                turn_o(i, k, a, b)
                            elif kind == "x":
                                if b == 0:
                                    pe.wait_ge(tile_loaded[a], 16 * TILE_DMAS * (i - FIRST + 1))
                                nc.tensor.transpose(ps[:, bank(i, k), 0:P], xs[:, a, b * P:(b + 1) * P],
                                                    ident[:, :]).then_inc(ring_ready, 1)
                            else:
                                if b == 0:
                                    pe.wait_ge(ring_taken, ring_base(i, experts) + use[("x", a, 1)] + 1)
                                for c in range(KC):
                                    last = nc.tensor.matmul(ps[:, bank(i, k), 0:P], w1s[:, a, c, b * P:(b + 1) * P],
                                                            xsT[:, a, c], start=(c == 0), stop=(c == KC - 1))
                                last.then_inc(ring_ready, 1)
                        if experts and tt < 3 and sub >= 2:
                            c = sub - 2
                            pe.wait_ge(ring_taken, ring_base(i, experts) + use[("h", tt, c)] + 1)
                            if c == 0:
                                at_least(pe, y_taken, 3 * (i - FIRST) + tt)
                            ins = nc.tensor.matmul(ps[:, Y, 0:D], hT[:, c], w2s[:, tt, c],
                                                   start=(c == 0), stop=(c == FC - 1))
                            if c == FC - 1:
                                ins.then_inc(y_ready, 1)
                        values(i, s)

                logits(0, 0)
                pe.wait_ge(o_cleared, 1)
                body(0, False, route=True)
                with pe.Fori(1, FIRST) as i:
                    body(i, False)
                body(FIRST, True)
                with pe.Fori(FIRST + 1, PAIRS - 1) as i:
                    body(i, True)
                body(PAIRS - 1, True, True)
                at_least(pe, ring_taken, ring_base(PAIRS, True) - 1)
                turn_o(PAIRS, 0, 1, -1)

        take = views(work[:, :])
        At = take([2, GT, D])
        AT = take([2, KC, GN])
        a2g = take([2, GT, D])
        a2T = take([KC, TOK])
        a2s = At.rearrange("p g t (c n) -> p g (t c n)", c=KC).rearrange("p g (c n) -> p g c n", c=KC)
        og = a2g
        take_m = views(XN_REST)
        gram = take_m([NB, KC, D])
        t1 = take_m([NB, KC, D])
        rr = take_m([NB, KC, D])
        mb = take_m([NB, KC, D])
        pblk = take([NB * KC, P])
        dd = take([NB * KC, CD])
        dm = take([NB * KC, CD])
        ll = take([NB * KC, CD])
        c4 = take([3, NB * KC])

        def use_a(G):
            return 0 if isinstance(G, int) and G == 0 else 4 * G - 2

        def use_a2(G):
            return 4 * G + 2 if isinstance(G, int) and G == GROUPS - 1 else 4 * G + 4

        gathered = sem("gathered")
        at_copied = sem("at_copied")
        ring3_ready = sem("ring3_ready")
        ring3_taken = sem("ring3_taken")
        wo_ready = sem("wo_ready")
        x1_ready = sem("x1_ready")
        c_step = sem("c_step")
        var3_ready = sem("var3_ready")
        rstd3_ready = sem("rstd3_ready")
        a2_ready = sem("a2_ready")
        gram_cleared = sem("gram_cleared")
        gram_done = sem("gram_done")
        gram_copied = sem("gram_copied")
        alg_pe = sem("alg_pe")
        alg_dve = sem("alg_dve")
        alg_exp = sem("alg_exp")
        staged = sem("staged")
        fin_ready = sem("fin_ready")
        fin_taken = sem("fin_taken")
        sum_ready = sem("sum_ready")
        x_again = [sem("x_again0"), sem("x_again1")]
        out_stored = [sem("out_stored0"), sem("out_stored1")]
        f_step = sem("f_step")
        xn_back = [sem("xn_back0"), sem("xn_back1")]

        with nc.Block() as block:
            @block.sync
            def _(sp):
                def load(G, par):
                    at_least(sp, sum_ready, G - 1)
                    sp.dma_start(xg[:, par], xt[:, bass.ds(G * GT, GT), :]).then_inc(x_again[par], 16)

                def store(G, par):
                    sp.wait_ge(sum_ready, G + 1)
                    sp.dma_start(outt[:, bass.ds(G * GT, GT), :], og[:, par]).then_inc(out_stored[par], 16)
                for b in range(NB):
                    sp.dma_start(XN[:, b * TB:(b + 1) * TB], xn_rows[:, b * TB:(b + 1) * TB]).then_inc(xn_back[b], 16)
                load(0, 0)
                load(1, 1)
                with sp.Fori(0, GROUPS // 2 - 1) as it:
                    for par in range(2):
                        G = 2 * it + par
                        store(G, par)
                        load(G + 2, par)
                store(GROUPS - 2, 0)
                store(GROUPS - 1, 1)
                for par in range(2):
                    sp.wait_ge(out_stored[par], 16 * GROUPS // 2)

            @block.gpsimd
            def _(pool):
                def rstd(G, par):
                    pool.wait_ge(var3_ready, G + 1)
                    nc.gpsimd.tensor_tensor(rs1[:, par], ve1[:, par], nhalf[:, :], ALU.pow).then_inc(rstd3_ready, 1)

                for G in range(GROUPS):
                    rstd(G, G % 2)
                    for t in range(G * GT, (G + 1) * GT):
                        nc.gpsimd.indirect_dma_start(YG[:, t], None, y_slots,
                                                     bass.IndirectOffsetOnAxis(ap=pos_u[:, t:t + 1], axis=0)
                                                     ).then_inc(gathered, 16)

            @block.scalar
            def _(act):
                def stage_a(G, par):
                    b, t0 = G // GB, (G % GB) * GT
                    if not isinstance(G, int) or G >= 2:
                        act.wait_ge(ring3_ready, 4 * G - 8)
                    for t in range(GT):
                        last = nc.scalar.copy(
                            At[:, par, t].rearrange("p (h d) -> p h d", h=H),
                            A[:, bass.ds(b * H, H), bass.ds(t0 + t, 1)].rearrange("p h t d -> p (h t) d"))
                    last.then_inc(at_copied, 1)

                def take_at(G, par):
                    for c in range(KC):
                        act.wait_ge(ring3_ready, use_a(G) + c + 1)
                        if c == 0:
                            at_least(act, wo_ready, 2 * (G - 1))
                        nc.scalar.copy(AT[:, par, c], ps[:, c]).then_inc(ring3_taken, 1)

                def take_a2(G, par):
                    for c in range(KC):
                        act.wait_ge(ring3_ready, use_a2(G) + c + 1)
                        nc.scalar.copy(a2T[:, c, bass.ds(G * GN, GN)], ps[:, c]).then_inc(ring3_taken, 1)

                stage_a(0, 0)
                take_at(0, 0)

                def turn(G, par):
                    stage_a(G + 1, 1 - par)
                    take_at(G + 1, 1 - par)
                    take_a2(G, par)
                turn(0, 0)
                turn(1, 1)
                with act.Fori(1, GROUPS // 2 - 1) as it:
                    for par in range(2):
                        turn(2 * it + par, par)
                turn(GROUPS - 2, 0)
                take_a2(GROUPS - 1, 1)
                act.wait_ge(gram_done, GROUPS)
                nc.scalar.copy(gram.rearrange("p b c n -> p b (c n)"), ps[:, 4:6]).then_inc(gram_copied, 1)
                act.wait_ge(alg_pe, 1)
                nc.scalar.copy(t1.rearrange("p b c n -> p b (c n)"), ps[:, 6:8]).then_inc(gram_copied, 1)
                act.wait_ge(alg_exp, 1)
                nc.scalar.activation(ll, ll, ACT.Exp).then_inc(gram_copied, 1)
                act.wait_ge(alg_pe, 4)
                nc.scalar.copy(rr.rearrange("p b c n -> p b (c n)"), ps[:, 6:8]).then_inc(gram_copied, 1)

                def stage_f(G, par):
                    at_least(act, fin_ready, 2 * (G - 1))
                    nc.scalar.copy(a2s[:, par], a2T[:, :, bass.ds(G * GN, GN)]).then_inc(staged, 1)
                stage_f(0, 0)
                stage_f(1, 1)
                with act.Fori(1, GROUPS // 2) as it:
                    for par in range(2):
                        stage_f(2 * it + par, par)

            @block.vector
            def _(dve):
                nc.vector.memset(pblk, 0.0)
                nc.vector.memset(ps[:, 4:6], 0.0).then_inc(gram_cleared, 1)

                def normed(G, par):
                    def step(n):
                        dve.wait_ge(c_step, 4 * G + n)
                        apart(dve)
                    for k in range(2):
                        dve.wait_ge(wo_ready, 2 * G + k + 1)
                        xv = XN[:, bass.ds(G * GT + 2 * k, 2)]
                        nc.vector.tensor_tensor(xv, ps[:, 2 + k].rearrange("p (t d) -> p t d", t=2), xv,
                                                ALU.add).then_inc(x1_ready, 1)
                    dve.wait_ge(x1_ready, 2 * G + 2)
                    apart(dve)
                    for t in range(GT):
                        last = nc.vector.bn_stats(st1[:, par, t], XN[:, bass.ds(G * GT + t, 1)].rearrange("p a d -> p (a d)"))
                    last.then_inc(c_step, 1)
                    step(1)
                    for t in range(GT):
                        last = nc.vector.bn_aggr(mv1[:, par, t], st1[:, par, t])
                    last.then_inc(c_step, 1)
                    step(2)
                    nc.vector.tensor_scalar(ve1[:, par], mv1[:, par, :, 1], EPS, None, ALU.add).then_inc(var3_ready, 1)
                    dve.wait_ge(rstd3_ready, G + 1)
                    at_least(dve, gram_done, G - 1)
                    for t in range(GT):
                        last = nc.vector.tensor_scalar(a2g[:, par, t], XN[:, bass.ds(G * GT + t, 1)].rearrange("p a d -> p (a d)"),
                                                       mv1[:, par, t, 0:1], rs1[:, par, t:t + 1],
                                                       ALU.subtract, ALU.mult)
                    last.then_inc(c_step, 1)
                    step(3)
                    rows = [P, GT, D]
                    nc.vector.tensor_tensor(a2g[:, par], a2g[:, par], l2w[:, :].unsqueeze(1).broadcast_to(rows),
                                            ALU.mult).then_inc(c_step, 1)
                    step(4)
                    nc.vector.tensor_tensor(a2g[:, par], a2g[:, par], l2b[:, :].unsqueeze(1).broadcast_to(rows),
                                            ALU.add).then_inc(a2_ready, 1)
                for b in range(NB):
                    dve.wait_ge(xn_back[b], 16)
                for G in (0, 1):
                    normed(G, G)
                with dve.Fori(1, GROUPS // 2) as it:
                    for par in range(2):
                        normed(2 * it + par, par)

                BK = NB * KC
                n = [0]

                def mark(ins):
                    n[0] += 1
                    ins.then_inc(alg_dve, 1)
                    dve.wait_ge(alg_dve, n[0])

                def wide(v):
                    return v.unsqueeze(2).broadcast_to([P, BK, CD])
                dots = ps[:, 0].rearrange("p (k c) -> p k c", k=BK)
                dve.wait_ge(alg_pe, 2)
                for r in range(P // CD):
                    q = slice(r * CD, (r + 1) * CD)
                    last = nc.vector.tensor_copy(dd[q], dots[q, :, q])
                mark(last)
                mark(nc.vector.tensor_tensor(dm, dd, diag[:, :].unsqueeze(1).broadcast_to([P, BK, CD]), ALU.mult))
                mark(nc.vector.tensor_reduce(c4[:, 0], dm, AX.X, ALU.add))
                dve.wait_ge(alg_pe, 3)
                mark(nc.vector.scalar_tensor_tensor(ll, dd, 2.0, ps[:, 1, 0:BK * CD].rearrange("p (k c) -> p k c", k=BK),
                                                    ALU.mult, ALU.subtract))
                mark(nc.vector.tensor_tensor(ll, ll, wide(c4[:, 0]), ALU.subtract))
                for b in range(NB):
                    for c in range(KC):
                        last = nc.vector.tensor_scalar(ll[:, b * KC + c], ll[:, b * KC + c], tauc[:, c:c + 1], None, ALU.mult)
                mark(last)
                mark(nc.vector.tensor_reduce(c4[:, 1], ll, AX.X, ALU.max))
                nc.vector.tensor_tensor(ll, ll, wide(c4[:, 1]), ALU.subtract).then_inc(alg_exp, 1)
                dve.wait_ge(gram_copied, 3)
                mark(nc.vector.tensor_reduce(c4[:, 2], ll, AX.X, ALU.add))
                mark(nc.vector.reciprocal(c4[:, 2], c4[:, 2]))
                for r in range(P // CD):
                    q = slice(r * CD, (r + 1) * CD)
                    last = nc.vector.tensor_tensor(pblk[q, :, q], ll[q], c4[q, 2].unsqueeze(2).broadcast_to([CD, BK, CD]),
                                                   ALU.mult)
                mark(last)
                PB = n[0]
                assert PB == ALG_P, PB
                dve.wait_ge(alg_pe, 5)
                mark(nc.vector.tensor_tensor(mb.rearrange("p b c n -> p (b c) n"),
                                             ps[:, 2:4].rearrange("p b (c n) -> p (b c) n", c=KC),
                                             g2r[:, :].unsqueeze(1).broadcast_to([P, BK, D]), ALU.mult))

                def final(G, par):
                    def step(k):
                        dve.wait_ge(f_step, G + k)
                    at_least(dve, out_stored[par], 16 * (G // 2))
                    for k in range(2):
                        dve.wait_ge(fin_ready, 2 * G + k + 1)
                        last = nc.vector.tensor_tensor(og[:, par, 2 * k:2 * k + 2],
                                                       ps[:, FIN[par] + k].rearrange("p (t d) -> p t d", t=2),
                                                       XN[:, bass.ds(G * GT + 2 * k, 2)], ALU.add)
                        last.then_inc(fin_taken, 1)
                    dve.wait_ge(x_again[par], 16 * (G // 2) + 16)
                    dve.wait_ge(fin_taken, 2 * G + 2)
                    nc.vector.tensor_tensor(og[:, par], og[:, par], xg[:, par], ALU.add).then_inc(f_step, 1)
                    step(1)
                    for t in range(GT):
                        yv = YG[:, bass.ds(G * GT + t, 1)].rearrange("p a d -> p (a d)")
                        last = nc.vector.scalar_tensor_tensor(og[:, par, t], yv, gate[:, bass.ds(G * GT + t, 1)],
                                                              og[:, par, t], ALU.mult, ALU.add)
                    last.then_inc(sum_ready, 1)
                dve.wait_ge(gathered, 16 * TILES)
                for G in (0, 1):
                    final(G, G)
                with dve.Fori(1, GROUPS // 2) as it:
                    for par in range(2):
                        final(2 * it + par, par)

            @block.tensor
            def _(pe):
                def attn_out(G, par):
                    pe.wait_ge(at_copied, G + 1)
                    for c in range(KC):
                        at_least(pe, ring3_taken, use_a(G) + c - 1)
                        for t in range(GT):
                            last = nc.tensor.transpose(ps[:, c, t * P:(t + 1) * P], At[:, par, t, c * P:(c + 1) * P],
                                                       ident[:, :])
                        last.then_inc(ring3_ready, 1)
                    pe.wait_ge(ring3_taken, use_a(G) + 2)
                    for k in range(2):
                        at_least(pe, x1_ready, 2 * (G - 1) + k + 1)
                        for t in range(2):
                            for c in range(KC):
                                last = nc.tensor.matmul(ps[:, 2 + k, t * D:(t + 1) * D],
                                                        AT[:, par, c, (2 * k + t) * P:(2 * k + t + 1) * P], wo[:, c],
                                                        start=(c == 0), stop=(c == KC - 1))
                        last.then_inc(wo_ready, 1)

                def gram_of(G, par):
                    b = G // GB
                    pe.wait_ge(a2_ready, G + 1)
                    for c in range(KC):
                        pe.wait_ge(ring3_taken, use_a2(G) + c - 1)
                        for t in range(GT):
                            last = nc.tensor.transpose(ps[:, c, t * P:(t + 1) * P], a2g[:, par, t, c * P:(c + 1) * P],
                                                       ident[:, :])
                        last.then_inc(ring3_ready, 1)
                    for t in range(GT):
                        for M in range(KC):
                            last = nc.tensor.matmul(ps[:, bass.ds(4 + b, 1), M * D:(M + 1) * D].rearrange("p a n -> p (a n)"),
                                                    a2g[:, par, t, M * P:(M + 1) * P], a2g[:, par, t],
                                                    start=False, stop=False, skip_group_check=True)
                    last.then_inc(gram_done, 1)

                pe.wait_ge(gram_cleared, 1)
                attn_out(0, 0)

                def turn(G, par):
                    attn_out(G + 1, 1 - par)
                    gram_of(G, par)
                turn(0, 0)
                turn(1, 1)
                with pe.Fori(1, GROUPS // 2 - 1) as it:
                    for par in range(2):
                        turn(2 * it + par, par)
                turn(GROUPS - 2, 0)
                gram_of(GROUPS - 1, 1)
                pe.wait_ge(gram_copied, 1)
                for b in range(NB):
                    for M in range(KC):
                        for c in range(KC):
                            last = nc.tensor.matmul(ps[:, 6 + b, M * D:(M + 1) * D], gram[:, b, c, M * P:(M + 1) * P],
                                                    wqkc[:, c], start=(c == 0), stop=(c == KC - 1))
                last.then_inc(alg_pe, 1)
                pe.wait_ge(gram_copied, 2)
                pe.wait_ge(ring3_taken, 4 * GROUPS)
                for b in range(NB):
                    for M in range(KC):
                        for c in range(KC):
                            last = nc.tensor.matmul(ps[:, 0, (b * KC + M) * P:(b * KC + M + 1) * P],
                                                    wqkc[:, c, M * P:(M + 1) * P], t1[:, b, c, M * P:(M + 1) * P],
                                                    start=(c == 0), stop=(c == KC - 1))
                last.then_inc(alg_pe, 1)
                pe.wait_ge(alg_dve, 2)
                nc.tensor.matmul(ps[:, 1, 0:NB * KC * CD], blockones[:, :], dm.rearrange("p k c -> p (k c)"),
                                 start=True, stop=True).then_inc(alg_pe, 1)
                pe.wait_ge(alg_dve, ALG_P)
                for b in range(NB):
                    for c in range(KC):
                        last = nc.tensor.matmul(ps[:, 6 + b, c * D:(c + 1) * D], pblk[:, b * KC + c], woc[:, c],
                                                start=True, stop=True)
                last.then_inc(alg_pe, 1)
                pe.wait_ge(gram_copied, 4)
                for b in range(NB):
                    for k in range(KC):
                        for d in range(KC):
                            last = nc.tensor.matmul(ps[:, 2 + b, k * D:(k + 1) * D], wvcT[:, d, k * P:(k + 1) * P],
                                                    rr[:, b, d], start=(d == 0), stop=(d == KC - 1))
                last.then_inc(alg_pe, 1)
                pe.wait_ge(alg_dve, ALG_P + 1)

                def finals(G, par):
                    b = G // GB
                    pe.wait_ge(staged, G + 1)
                    for k in range(2):
                        at_least(pe, fin_taken, 2 * (G - 2) + k + 1)
                        for t in range(2):
                            for c in range(KC):
                                last = nc.tensor.matmul(ps[:, FIN[par] + k, t * D:(t + 1) * D],
                                                        a2s[:, par, c, (2 * k + t) * P:(2 * k + t + 1) * P],
                                                        mb[:, bass.ds(b, 1), c].rearrange("p a n -> p (a n)"),
                                                        start=(c == 0), stop=(c == KC - 1))
                        last.then_inc(fin_ready, 1)
                for G in (0, 1):
                    finals(G, G)
                with pe.Fori(1, GROUPS // 2) as it:
                    for par in range(2):
                        finals(2 * it + par, par)


_INS = {"x": "L0_attn_x", "Wqk_t": "L0_attn_Wqk_t", "Wv_t": "L0_attn_Wv_t", "Wo_t": "L0_attn_Wo_t",
        "tau_t": "L0_attn_tau_t", "Wqk_c": "L0_attn_Wqk_c", "Wv_c": "L0_attn_Wv_c", "Wo_c": "L0_attn_Wo_c",
        "tau_c": "L0_attn_tau_c", "ln1_w": "L0_attn_ln1_w", "ln1_b": "L0_attn_ln1_b", "ln2_w": "L0_attn_ln2_w",
        "ln2_b": "L0_attn_ln2_b", "gamma1": "L0_attn_gamma1", "gamma2": "L0_attn_gamma2",
        "router_W": "L0_ffn_router_W", "router_b": "L0_ffn_router_b", "W1": "L0_ffn_W1", "b1": "L0_ffn_b1",
        "W2": "L0_ffn_W2", "b2": "L0_ffn_b2"}


def kernel(**inputs):
    import numpy as _np
    import concourse.bacc as _bacc
    from concourse import mybir as _mybir
    from concourse.bass_utils import run_bass_kernel_spmd as _run

    nc = _bacc.Bacc("TRN2", target_bir_lowering=False, num_devices=1)
    arrays, args = {}, {}
    for short, name in _INS.items():
        a = _np.ascontiguousarray(inputs[name])
        arrays[f"in_{name}_dram"] = a
        args[short] = nc.dram_tensor(f"in_{name}_dram", a.shape, _mybir.dt.from_np(a.dtype), kind="ExternalInput").ap()
    args["out"] = nc.dram_tensor("out_0_dram", inputs["L0_attn_x"].shape, _mybir.dt.float32, kind="ExternalOutput").ap()
    build(nc, **args)
    r = _run(nc, [arrays], core_ids=[0])
    return r.results[0]["out_0_dram"]
```

```python
from contextlib import ExitStack

import numpy as np
import concourse.bass as bass
from concourse import mybir

F32 = mybir.dt.float32
BF16 = mybir.dt.bfloat16
I32 = mybir.dt.int32
U32 = mybir.dt.uint32
ALU = mybir.AluOpType
ACT = mybir.ActivationFunctionType
AX = mybir.AxisListType

P = 128
EPS = 1e-5


def at_least(eng, sem, value):
    if isinstance(value, int) and value <= 0:
        return
    eng.wait_ge(sem, value)


def apart(eng):
    eng.nop(nofuse=True)


def build(nc, x, Wqk_t, Wv_t, Wo_t, tau_t, Wqk_c, Wv_c, Wo_c, tau_c, ln1_w, ln1_b, ln2_w, ln2_b,
          gamma1, gamma2, router_W, router_b, W1, b1, W2, b2, out):
    NB, S, D = x.shape
    H = tau_t.shape[0]
    CH = tau_c.shape[0]
    DH = D // H
    CD = D // CH
    NE, _, F = W1.shape
    KC = D // P
    FC = F // P
    TOK = NB * S
    TILES = TOK // P
    TB = S // P
    GT = 4
    GROUPS = TILES // GT
    GN = GT * P
    GB = GROUPS // NB
    HC = P // DH
    SLOT_TILES = (TOK - NE) // P + NE
    VW = DH + 1
    NCHUNK = S // 512
    QK_SCALE = 1.0 / float(np.sqrt(DH))
    CQ_SCALE = 1.0 / float(np.sqrt(S))

    xt = x.rearrange("b (t p) d -> p (b t) d", p=P)
    outt = out.rearrange("b (t p) d -> p (b t) d", p=P)

    q_parts = nc.dram_tensor("q_parts", [3, NB * D, S], BF16).ap()
    w_parts = nc.dram_tensor("w_parts", [3, NB * H, S], BF16).ap()
    x_slots = nc.dram_tensor("x_slots", [SLOT_TILES * P, D], F32).ap()
    y_slots = nc.dram_tensor("y_slots", [SLOT_TILES * P, D], F32).ap()
    xn_rows = nc.dram_tensor("xn_rows", [P, TILES, D], F32).ap()
    b1_cols = nc.dram_tensor("b1_cols", [NE, P, FC], F32).ap()

    with ExitStack() as ctx:
        def sb(name, shape, dt=F32):
            return ctx.enter_context(nc.sbuf_tensor(name, shape, dt))

        def sem(name):
            return ctx.enter_context(nc.semaphore(name))

        ps = ctx.enter_context(nc.psum_tensor("ps", [P, 8, 512], F32))

        XNW = sb("XNW", [P, 3 * 2 * KC * F])
        XN = XNW[:, 0:TILES * D].rearrange("p (t d) -> p t d", t=TILES)
        XN_REST = XNW[:, TILES * D:]
        Aflat = sb("A", [P, NB * H * TB * DH])
        A_heads = Aflat[:, :].rearrange("p (b t h d) -> p b t h d", b=NB, t=TB, h=H)
        A_rows = Aflat[:, :].rearrange("p (b t n) -> p b t n", b=NB, t=TB)
        Vflat = sb("V", [P, NB * H * TB * VW])
        V = Vflat[:, :].rearrange("p (h m d) -> p h m d", h=NB * H, m=TB)
        YG = Vflat[:, 0:TILES * D].rearrange("p (t d) -> p t d", t=TILES)
        ident = sb("ident", [P, P])
        wqk = sb("wqk", [P, KC, D])
        wv = sb("wv", [P, KC, D])
        wo = sb("wo", [P, KC, D])
        wqkc = sb("wqkc", [P, KC, D])
        wvc = sb("wvc", [P, KC, D])
        woc = sb("woc", [P, KC, D])
        wvcT = sb("wvcT", [P, KC, D])
        l1w = sb("l1w", [P, KC])
        l1b = sb("l1b", [P, KC])
        l2w = sb("l2w", [P, D])
        l2b = sb("l2b", [P, D])
        g1r = sb("g1r", [P, D])
        g2r = sb("g2r", [P, D])
        tau_e = sb("tau_e", [P, NB * H])
        tauc = sb("tauc", [P, KC])
        ones = sb("ones", [P, P])
        blockones = sb("blockones", [P, P])
        diag = sb("diag", [P, CD])
        gate = sb("gate", [P, TILES])
        pos_u = sb("pos_u", [P, TILES], U32)
        emap = sb("emap", [1, SLOT_TILES], I32)
        nhalf = sb("nhalf", [P, GT])
        mv1 = sb("mv1", [P, 2, GT, 2])
        mv2 = sb("mv2", [P, 2, GT, 2])
        st1 = sb("st1", [P, 2, GT, 6])
        ve1 = sb("ve1", [P, 2, GT])
        ve2 = sb("ve2", [P, 2, GT])
        rs1 = sb("rs1", [P, 2, GT])
        rs2 = sb("rs2", [P, 2, GT])
        xg = sb("xg", [P, 2, GT, D])
        work = sb("work", [P, 16640])

        def views(area):
            at = [0]

            def take(shape, dt=F32):
                n = int(np.prod(shape))
                words = n if dt == F32 else n // 2
                v = area[:, at[0]:at[0] + words]
                at[0] += words
                assert at[0] <= area.shape[1], at[0]
                if dt != F32:
                    v = v.bitcast(dt)
                if len(shape) > 1:
                    names = "abcdef"[:len(shape)]
                    v = v.rearrange("p (" + " ".join(names) + ") -> p " + " ".join(names),
                                    **{k: s for k, s in zip(names, shape)})
                return v
            return take

        take = views(Aflat[:, :])
        xng = take([2, GT, D])
        zg = take([2, GT, D])
        xnT = take([2, KC, GN])
        aT = take([2, KC, GN])
        qp = views(XN_REST)([2, 3, KC, GN], BF16)
        take = views(work[:, :])
        stat_mov = take([2 * S])
        take_b = views(stat_mov)
        stat = take_b([2, S], BF16)
        mov = take_b([2, S], BF16)
        Vh = take([2, TB, VW])
        osb = take([2, 512])
        rec = take([2, TB])
        scale = take([2])
        big = take([2 * S])
        probs = big.rearrange("p (a b) -> p a b", a=2)
        take_b = views(big)
        qf = take_b([KC, GN])
        sq = take_b([KC, GN])
        qr = take_b([KC, GN])
        wf = take_b([GN])
        wr = take_b([GN])
        spare = take([3 * GN])
        wp = views(spare)([2, 3, GN], BF16)
        zero = take([D])
        sel = take([32])
        tri = take([P])
        rw = take([KC, NE])
        rb = take([NE])
        lg = take([TILES, NE])
        ex = take([TILES, NE])
        mask = take([TILES, NE])
        cnt = take([TILES, NE])
        cum = take([TILES, NE])
        s32 = take([4, TILES])
        s8 = take([6, NE])
        s8i = take([NE]).bitcast(I32)
        io_i = take([SLOT_TILES]).bitcast(I32)
        io_k = take([SLOT_TILES])
        ek = take([SLOT_TILES, NE])
        ek1 = take([SLOT_TILES])
        io_e = take([NE])
        io_ei = take([NE]).bitcast(I32)
        b1row = take([P])
        b1T = take([NE * FC])

        xload = [sem("x_loaded0"), sem("x_loaded1")]
        const_loaded = sem("const_loaded")
        late_loaded = sem("late_loaded")
        turned_loaded = sem("turned_loaded")
        pool_step = sem("pool_step")
        stats1_step = sem("stats1_step")
        stats2_step = sem("stats2_step")
        rest_ready = sem("rest_ready")
        q2_ready = sem("q2_ready")
        last_w_step = sem("last_w_step")
        dve_route_step = sem("dve_route_step")
        consts_made = sem("consts_made")
        zero_made = sem("zero_made")
        slots_zeroed = sem("slots_zeroed")
        var1_ready = sem("var1_ready")
        rstd1_ready = sem("rstd1_ready")
        var2_ready = sem("var2_ready")
        rstd2_ready = sem("rstd2_ready")
        xn_ready = sem("xn_ready")
        z_ready = sem("z_ready")
        xn_kept = [sem("xn_kept0"), sem("xn_kept1")]
        tr_ready = sem("tr_ready")
        tr_taken = sem("tr_taken")
        router_done = sem("router_done")
        q_ready = sem("q_ready")
        scales_made = sem("scales_made")
        q_taken = sem("q_taken")
        q_split = sem("q_split")
        v_ready = sem("v_ready")
        v_taken = sem("v_taken")
        w_ready = sem("w_ready")
        w_taken = sem("w_taken")
        w_split = sem("w_split")
        q_stored = [sem("q_stored0"), sem("q_stored1")]
        w_stored = [sem("w_stored0"), sem("w_stored1")]
        b1_turned = sem("b1_turned")
        b1_copied = sem("b1_copied")
        b1_stored = sem("b1_stored")
        lg_ready = sem("lg_ready")
        routed = sem("routed")
        logits_shifted = sem("logits_shifted")
        logits_exp = sem("logits_exp")
        mask_ready = sem("mask_ready")
        ranks_ready = sem("ranks_ready")
        iota_rows = sem("iota_rows")

        rows_set = sem("rows_set")
        rows_zeroed = sem("rows_zeroed")
        stack_loaded = [sem("stack_loaded0"), sem("stack_loaded1")]
        v_copied = sem("v_copied")
        scale_set = sem("scale_set")
        STAT_PARTS = (0, 0, 0, 1, 1, 2)
        MOV_PARTS = (0, 1, 2, 0, 1, 0)
        AUX = 6 * DH
        STACK_DMAS = 14

        def fill_stack(sp, i, hh):
            r0 = i * 2 * DH + hh * DH
            for k in range(6):
                sp.dma_start(stat[k * DH:(k + 1) * DH, hh], q_parts[STAT_PARTS[k], bass.ds(r0, DH), :]
                             ).then_inc(stack_loaded[hh], 16)
                sp.dma_start(mov[k * DH:(k + 1) * DH, hh], q_parts[MOV_PARTS[k], bass.ds(r0, DH), :]
                             ).then_inc(stack_loaded[hh], 16)
            w = w_parts[:, bass.ds(i * 2 + hh, 1), :].rearrange("c h n -> (c h) n")
            sp.dma_start(stat[AUX + 3:AUX + 6, hh], w).then_inc(stack_loaded[hh], 16)
            sp.dma_start(mov[AUX:AUX + 3, hh], w).then_inc(stack_loaded[hh], 16)

        def fill_v(i, hh):
            nc.gpsimd.tensor_copy(scale[:, hh:hh + 1], tau_e[:, bass.ds(2 * i + hh, 1)]).then_inc(scale_set, 1)
            nc.gpsimd.tensor_copy(Vh[:, hh], V[:, bass.ds(2 * i + hh, 1)].rearrange("p h m d -> p (h m) d")
                                  ).then_inc(v_copied, 1)

        N_CONST = 8 + NB
        N_LATE = 7 + CH
        with nc.Block() as block:
            @block.sync
            def _(sp):
                def load_x(G, par):
                    at_least(sp, xn_ready, G - 1)
                    sp.dma_start(xg[:, par], xt[:, bass.ds(G * GT, GT), :]).then_inc(xload[par], 16)

                def keep(G, par):
                    sp.wait_ge(xn_ready, G + 1)
                    sp.dma_start(XN[:, bass.ds(G * GT, GT), :], xng[:, par]).then_inc(xn_kept[par], 16)
                    sp.dma_start(xn_rows[:, bass.ds(G * GT, GT), :], xng[:, par]).then_inc(xn_kept[par], 16)

                def store_q(G, par):
                    b, tok = G // GB, (G % GB) * GN
                    sp.wait_ge(q_split, G + 1)
                    for part in range(3):
                        sp.dma_start(q_parts[part, bass.ds(b * D, D), bass.ds(tok, GN)]
                                     .rearrange("(c p) n -> p c n", p=P), qp[:, par, part]).then_inc(q_stored[par], 16)

                def store_w(G, par):
                    b, tok = G // GB, (G % GB) * GN
                    sp.wait_ge(w_split, G + 1)
                    for c in range(KC):
                        sp.dma_start(w_parts[:, bass.ds(b * H + c * HC, HC), bass.ds(tok, GN)].rearrange("c h n -> h c n"),
                                     wp[32 * c:32 * c + HC, par]).then_inc(w_stored[par], 16)

                load_x(0, 0)
                load_x(1, 1)

                def const(dst, src):
                    sp.dma_start(dst, src).then_inc(const_loaded, 16)
                const(rw, router_W.rearrange("(c p) e -> p c e", p=P))
                const(wqk[:, :, :], Wqk_t.rearrange("(c p) n -> p c n", p=P))
                const(wv[:, :, :], Wv_t.rearrange("(c p) n -> p c n", p=P))
                for c in range(KC):
                    const(l1w[:, c:c + 1], ln1_w[c * P:(c + 1) * P].rearrange("(p a) -> p a", a=1))
                    const(l1b[:, c:c + 1], ln1_b[c * P:(c + 1) * P].rearrange("(p a) -> p a", a=1))
                const(rb, router_b.partition_broadcast(P))
                for b in range(NB):
                    const(tau_e[:, b * H:(b + 1) * H], tau_t.rearrange("h a b -> (h a b)").partition_broadcast(P))
                for G in (0, 1):
                    keep(G, G)
                    load_x(G + 2, G)
                    if G == 1:
                        store_q(0, 0)
                sp.dma_start(wvc[:, :, :], Wv_c.rearrange("(c p) n -> p c n", p=P)).then_inc(turned_loaded, 16)
                sp.dma_start(b1row[0:NE * FC], b1.rearrange("e (c p) -> (e c) p", p=P)).then_inc(turned_loaded, 16)
                with sp.Fori(1, GROUPS // 2 - 1) as it:
                    for par in range(2):
                        G = 2 * it + par
                        keep(G, par)
                        load_x(G + 2, par)
                        store_q(G - 1, 1 - par)
                        store_w(G - 2, par)
                sp.wait_ge(q_stored[0], 3 * 16 * 3)
                sp.wait_ge(q_stored[1], 3 * 16 * 2)
                for par in range(2):
                    sp.wait_ge(w_stored[par], 2 * 16 * 2)
                sp.wait_ge(rows_set, 1)
                fill_stack(sp, 0, 0)
                for G in (GROUPS - 2, GROUPS - 1):
                    keep(G, G % 2)
                    store_q(G - 1, 1 - G % 2)
                    store_w(G - 2, G % 2)
                fill_stack(sp, 0, 1)
                store_w(GROUPS - 2, 0)
                store_q(GROUPS - 1, 1)
                store_w(GROUPS - 1, 1)
                sp.wait_ge(b1_copied, 1)
                sp.dma_start(b1_cols.rearrange("e p c -> p e c"),
                             b1T.rearrange("p (e c) -> p e c", e=NE)).then_inc(b1_stored, 16)

            @block.gpsimd
            def _(pool):
                nc.gpsimd.memset(nhalf[:, :], -0.5)
                nc.gpsimd.memset(zero, 0.0).then_inc(zero_made, 1)
                nc.gpsimd.memset(ident[:, :], 0.0)
                nc.gpsimd.memset(ones[:, :], 1.0)
                nc.gpsimd.memset(tri, 1.0)
                nc.gpsimd.memset(sel[:, 0:HC], -0.5)
                nc.gpsimd.memset(sel[:, HC:], 0.0)
                nc.gpsimd.memset(blockones[:, :], 1.0)
                nc.gpsimd.memset(V[:, :, :, DH:VW], 1.0)
                nc.gpsimd.iota(io_i[0:1], pattern=[[1, SLOT_TILES]], base=0, channel_multiplier=0).then_inc(pool_step, 1)
                pool.wait_ge(pool_step, 1)
                nc.gpsimd.affine_select(out=ident[:, :], in_=ident[:, :], compare_op=ALU.not_equal, fill=1.0,
                                        base=0, pattern=[[-1, P]], channel_multiplier=1)
                nc.gpsimd.affine_select(out=tri, in_=tri, compare_op=ALU.is_gt, fill=0.0,
                                        base=0, pattern=[[1, P]], channel_multiplier=-1)
                nc.gpsimd.affine_select(out=sel[:, 0:HC], in_=sel[:, 0:HC], compare_op=ALU.is_ge, fill=0.0,
                                        base=0, pattern=[[-DH, HC]], channel_multiplier=1)
                nc.gpsimd.affine_select(out=blockones[:, :].rearrange("p (a b) -> p a b", b=CD),
                                        in_=blockones[:, :].rearrange("p (a b) -> p a b", b=CD),
                                        compare_op=ALU.is_ge, fill=0.0, base=0, pattern=[[-CD, P // CD], [0, CD]],
                                        channel_multiplier=1).then_inc(pool_step, 1)
                pool.wait_ge(pool_step, 2)
                nc.gpsimd.affine_select(out=sel[:, 0:HC], in_=sel[:, 0:HC], compare_op=ALU.is_ge, fill=0.0,
                                        base=DH - 1, pattern=[[DH, HC]], channel_multiplier=-1)
                nc.gpsimd.affine_select(out=blockones[:, :].rearrange("p (a b) -> p a b", b=CD),
                                        in_=blockones[:, :].rearrange("p (a b) -> p a b", b=CD),
                                        compare_op=ALU.is_ge, fill=0.0, base=CD - 1, pattern=[[CD, P // CD], [0, CD]],
                                        channel_multiplier=-1)
                nc.gpsimd.tensor_copy(io_k[0:1], io_i[0:1]).then_inc(consts_made, 1)
                nc.gpsimd.iota(io_ei, pattern=[[1, NE]], base=0, channel_multiplier=0).then_inc(pool_step, 1)
                pool.wait_ge(pool_step, 3)
                nc.gpsimd.tensor_copy(io_e, io_ei).then_inc(iota_rows, 1)

                def rstd1(G, par):
                    pool.wait_ge(var1_ready, G + 1)
                    nc.gpsimd.tensor_tensor(rs1[:, par], ve1[:, par], nhalf[:, :], ALU.pow).then_inc(rstd1_ready, 1)

                def rstd2(G, par):
                    pool.wait_ge(var2_ready, G + 1)
                    nc.gpsimd.tensor_tensor(rs2[:, par], ve2[:, par], nhalf[:, :], ALU.pow).then_inc(rstd2_ready, 1)

                def back(G, par):
                    def step(n):
                        pool.wait_ge(pool_step, 3 + 2 * G + n)
                    rows = slice(0, 64)
                    w = wp[rows, par]
                    pool.wait_ge(w_taken, G + 1)
                    nc.gpsimd.tensor_tensor(wr[rows], wf[rows], w[:, 0], ALU.subtract).then_inc(pool_step, 1)
                    step(1)
                    apart(pool)
                    nc.gpsimd.tensor_copy(w[:, 1], wr[rows]).then_inc(pool_step, 1)
                    step(2)
                    nc.gpsimd.tensor_tensor(w[:, 2], wr[rows], w[:, 1], ALU.subtract).then_inc(w_split, 1)

                def group(G, par, last=False):
                    rstd2(G, par)
                    if not last:
                        rstd1(G + 1, 1 - par)
                    if not isinstance(G, int) or G >= 2:
                        back(G - 2, par)

                rstd1(0, 0)
                group(0, 0)
                pool.wait_ge(rstd1_ready, 2)
                nc.gpsimd.memset(stat_mov[AUX:P], 0.0).then_inc(rows_zeroed, 1)
                pool.wait_ge(rows_zeroed, 1)
                group(1, 1)
                pool.wait_ge(rstd1_ready, 3)
                pair = float(np.array([0x3F803F80], np.uint32).view(np.float32)[0])
                nc.gpsimd.memset(stat_mov[AUX:AUX + 6], pair).then_inc(rows_set, 1)
                pool.wait_ge(rows_set, 1)
                with pool.Fori(1, GROUPS // 2 - 1) as it:
                    for par in range(2):
                        group(2 * it + par, par)
                pool.wait_ge(scales_made, 1)
                pool.wait_ge(v_taken, 2 * GB)
                fill_v(0, 0)
                group(GROUPS - 2, 0)
                fill_v(0, 1)
                group(GROUPS - 1, 1, last=True)
                back(GROUPS - 2, 0)

            @block.vector
            def _(dve):
                def stats_x(G, par):
                    def step(n):
                        dve.wait_ge(stats1_step, G * 2 + n)
                        apart(dve)
                    dve.wait_ge(xload[par], 16 * (G // 2) + 16)
                    apart(dve)
                    for t in range(GT):
                        last = nc.vector.bn_stats(st1[:, par, t], xg[:, par, t])
                    last.then_inc(stats1_step, 1)
                    step(1)
                    for t in range(GT):
                        last = nc.vector.bn_aggr(mv1[:, par, t], st1[:, par, t])
                    last.then_inc(stats1_step, 1)
                    step(2)
                    nc.vector.tensor_scalar(ve1[:, par], mv1[:, par, :, 1], EPS, None, ALU.add).then_inc(var1_ready, 1)

                def make_xn(G, par):
                    def step(n):
                        dve.wait_ge(stats2_step, G * 2 + n)
                        apart(dve)
                    dve.wait_ge(rstd1_ready, G + 1)
                    at_least(dve, xn_kept[par], 32 * (G // 2))
                    at_least(dve, tr_ready, 4 * (G - 1))
                    for t in range(GT):
                        last = nc.vector.tensor_scalar(xng[:, par, t], xg[:, par, t], mv1[:, par, t, 0:1],
                                                       rs1[:, par, t:t + 1], ALU.subtract, ALU.mult)
                    last.then_inc(xn_ready, 1)
                    dve.wait_ge(xn_ready, G + 1)
                    apart(dve)
                    for t in range(GT):
                        last = nc.vector.bn_stats(st1[:, par, t], xng[:, par, t])
                    last.then_inc(stats2_step, 1)
                    step(1)
                    for t in range(GT):
                        last = nc.vector.bn_aggr(mv2[:, par, t], st1[:, par, t])
                    last.then_inc(stats2_step, 1)
                    step(2)
                    nc.vector.tensor_scalar(ve2[:, par], mv2[:, par, :, 1], EPS, None, ALU.add).then_inc(var2_ready, 1)

                def make_z(G, par):
                    dve.wait_ge(rstd2_ready, G + 1)
                    for t in range(GT):
                        last = nc.vector.tensor_scalar(zg[:, par, t], xng[:, par, t], mv2[:, par, t, 0:1],
                                                       rs2[:, par, t:t + 1], ALU.subtract, ALU.mult)
                    last.then_inc(z_ready, 1)

                def back(G, par):
                    dve.wait_ge(q_taken, 2 * G + 2)
                    at_least(dve, q_split, G)
                    nc.vector.tensor_tensor(qr, qf, qp[:, par, 0], ALU.subtract).then_inc(rest_ready, 1)
                    dve.wait_ge(rest_ready, G + 1)
                    nc.vector.tensor_copy(qp[:, par, 1], qr).then_inc(q2_ready, 1)
                    dve.wait_ge(q2_ready, G + 1)
                    nc.vector.tensor_tensor(qp[:, par, 2], qr, qp[:, par, 1], ALU.subtract).then_inc(q_split, 1)

                def group(G, par, first=False, last=False):
                    make_xn(G, par)
                    if not last:
                        stats_x(G + 1, 1 - par)
                    make_z(G, par)
                    if not first:
                        back(G - 1, 1 - par)

                stats_x(0, 0)
                group(0, 0, first=True)
                dve.wait_ge(const_loaded, 16 * N_CONST)
                nc.vector.tensor_scalar(tau_e[:, :], tau_e[:, :], 2.0 * QK_SCALE, None, ALU.mult).then_inc(scales_made, 1)
                group(1, 1)
                with dve.Fori(1, GROUPS // 2 - 1) as it:
                    for par in range(2):
                        group(2 * it + par, par)
                group(GROUPS - 2, 0)
                group(GROUPS - 1, 1, last=True)
                dve.wait_ge(router_done, GROUPS)
                nc.vector.tensor_tensor(lg, ps[:, 2, 0:TILES * NE].rearrange("p (t e) -> p t e", e=NE),
                                        rb.unsqueeze(1).broadcast_to([P, TILES, NE]), ALU.add).then_inc(lg_ready, 1)
                back(GROUPS - 1, 1)
                rows, w = slice(0, 64), wp[0:64, 1]
                dve.wait_ge(w_taken, GROUPS)
                dve.wait_ge(w_split, GROUPS - 1)
                nc.vector.tensor_tensor(wr[rows], wf[rows], w[:, 0], ALU.subtract).then_inc(last_w_step, 1)
                dve.wait_ge(last_w_step, 1)
                nc.vector.tensor_copy(w[:, 1], wr[rows]).then_inc(last_w_step, 1)
                dve.wait_ge(last_w_step, 2)
                nc.vector.tensor_tensor(w[:, 2], wr[rows], w[:, 1], ALU.subtract).then_inc(w_split, 1)

            @block.scalar
            def _(act):
                def take_turned(G, par, k):
                    act.wait_ge(tr_ready, 4 * G + k + 1)
                    if k == 0:
                        at_least(act, router_done, G - 1)
                    if k == 2:
                        at_least(act, v_ready, 2 * (G - 1))
                    if k < 2:
                        nc.scalar.copy(xnT[:, par, k], ps[:, k]).then_inc(tr_taken, 1)
                    else:
                        nc.scalar.activation(aT[:, par, k - 2], ps[:, k - 2], ACT.Identity,
                                             bias=l1b[:, k - 2:k - 1], scale=l1w[:, k - 2:k - 1]).then_inc(tr_taken, 1)

                def take_q(G, par):
                    at_least(act, q_stored[par], 3 * 16 * (G // 2))
                    for M in range(KC):
                        act.wait_ge(q_ready, 2 * G + M + 1)
                        if M == 0:
                            at_least(act, rest_ready, G)
                            at_least(act, w_ready, G)
                        nc.scalar.copy(qp[:, par, 0, M], ps[:, 3 + M])
                        nc.scalar.activation(sq[:, M], ps[:, 3 + M], ACT.Square)
                        nc.scalar.copy(qf[:, M], ps[:, 3 + M]).then_inc(q_taken, 1)

                def take_v(G, k):
                    b, m0 = G // GB, (G % GB) * GT
                    act.wait_ge(v_ready, 2 * G + k + 1)
                    nc.scalar.copy(
                        V[:, bass.ds(b * H, H), bass.ds(m0 + 2 * k, 2), 0:DH].rearrange("p h m d -> p m h d"),
                        ps[:, 5 + k].rearrange("p (m h d) -> p m h d", m=2, h=H)).then_inc(v_taken, 1)

                def take_w(G, par):
                    act.wait_ge(w_ready, G + 1)
                    at_least(act, w_stored[par], 2 * 16 * (G // 2))
                    at_least(act, w_split, G)
                    nc.scalar.copy(wp[0:64, par, 0], ps[0:64, 7])
                    nc.scalar.copy(wf[0:64], ps[0:64, 7]).then_inc(w_taken, 1)

                def group(G, par, last=False):
                    take_q(G, par)
                    if not last:
                        take_turned(G + 1, 1 - par, 0)
                        take_turned(G + 1, 1 - par, 1)
                    take_v(G, 0)
                    if not last:
                        take_turned(G + 1, 1 - par, 2)
                    take_v(G, 1)
                    if not last:
                        take_turned(G + 1, 1 - par, 3)
                    take_w(G, par)

                act.wait_ge(const_loaded, 16 * N_CONST)
                for k in range(4):
                    take_turned(0, 0, k)
                group(0, 0)
                group(1, 1)
                with act.Fori(1, GROUPS // 2 - 1) as it:
                    for par in range(2):
                        group(2 * it + par, par)
                group(GROUPS - 2, 0)
                group(GROUPS - 1, 1, last=True)
                act.wait_ge(b1_turned, 1)
                nc.scalar.copy(b1T, ps[:, 0, 0:NE * FC]).then_inc(b1_copied, 1)
                nc.scalar.copy(wvcT[:, :, :], ps[:, 1].rearrange("p (a b) -> p a b", a=KC))

            @block.tensor
            def _(pe):
                def turn(G, par, k):
                    src = xng if k < 2 else zg
                    if k == 0:
                        pe.wait_ge(xn_ready, G + 1)
                    if k == 2:
                        pe.wait_ge(z_ready, G + 1)
                    at_least(pe, tr_taken, 4 * G + k - 1)
                    for t in range(GT):
                        last = nc.tensor.transpose(ps[:, k % 2, t * P:(t + 1) * P],
                                                   src[:, par, t, (k % 2) * P:(k % 2 + 1) * P], ident[:, :])
                    last.then_inc(tr_ready, 1)

                def router(G, par):
                    pe.wait_ge(tr_taken, 4 * G + 2)
                    for t in range(GT):
                        for c in range(KC):
                            last = nc.tensor.matmul(ps[:, 2, bass.ds((G * GT + t) * NE, NE)],
                                                    xnT[:, par, c, t * P:(t + 1) * P], rw[:, c],
                                                    start=(c == 0), stop=(c == KC - 1))
                    last.then_inc(router_done, 1)

                def product_q(G, par):
                    pe.wait_ge(tr_taken, 4 * G + 4)
                    for M in range(KC):
                        at_least(pe, q_taken, 2 * (G - 1) + M + 1)
                        for c in range(KC):
                            last = nc.tensor.matmul(ps[:, 3 + M], wqk[:, c, M * P:(M + 1) * P], aT[:, par, c],
                                                    start=(c == 0), stop=(c == KC - 1))
                        last.then_inc(q_ready, 1)

                def product_v(G, par, k):
                    at_least(pe, v_taken, 2 * (G - 1) + k + 1)
                    for t in range(2):
                        for c in range(KC):
                            last = nc.tensor.matmul(ps[:, 5 + k, t * D:(t + 1) * D],
                                                    aT[:, par, c, (2 * k + t) * P:(2 * k + t + 1) * P], wv[:, c],
                                                    start=(c == 0), stop=(c == KC - 1))
                    last.then_inc(v_ready, 1)

                def product_w(G):
                    pe.wait_ge(q_taken, 2 * G + 2)
                    at_least(pe, w_taken, G)
                    for c in range(KC):
                        last = nc.tensor.matmul(ps[32 * c:32 * (c + 1), 7], sel, sq[:, c], start=True, stop=True,
                                                tile_position=(0, 32 * c))
                    last.then_inc(w_ready, 1)

                def group(G, par, last=False):
                    router(G, par)
                    product_q(G, par)
                    if not last:
                        turn(G + 1, 1 - par, 0)
                        turn(G + 1, 1 - par, 1)
                    product_v(G, par, 0)
                    if not last:
                        turn(G + 1, 1 - par, 2)
                    product_v(G, par, 1)
                    if not last:
                        turn(G + 1, 1 - par, 3)
                    product_w(G)

                pe.wait_ge(consts_made, 1)
                for k in range(4):
                    turn(0, 0, k)
                pe.wait_ge(const_loaded, 16 * N_CONST)
                group(0, 0)
                group(1, 1)
                with pe.Fori(1, GROUPS // 2 - 1) as it:
                    for par in range(2):
                        group(2 * it + par, par)
                group(GROUPS - 2, 0)
                group(GROUPS - 1, 1, last=True)
                pe.wait_ge(turned_loaded, 16 * 2)
                pe.wait_ge(tr_taken, 4 * GROUPS)
                nc.tensor.transpose(ps[:, 0, 0:NE * FC], b1row[0:NE * FC], ident[0:NE * FC, 0:NE * FC])
                for d in range(KC):
                    for k in range(KC):
                        last = nc.tensor.transpose(ps[:, 1, (d * KC + k) * P:(d * KC + k + 1) * P],
                                                   wvc[:, k, d * P:(d + 1) * P], ident[:, :])
                last.then_inc(b1_turned, 1)

        take_w = views(XNW[:, :])
        w1s = take_w([3, KC, F])
        w2s = take_w([3, FC, D])
        b1s = take([3, FC])
        b2s = take([3, D])
        xs = take([3, D])
        hT = take([FC, P])
        take_s = views(spare)
        xsT = take_s([3, KC, P])
        ysb = take_s([3, D])
        PAIRS = NB * H // 2
        STEPS = 2 * TB
        FIRST = PAIRS - SLOT_TILES // 3
        assert SLOT_TILES == 3 * (PAIRS - FIRST)
        SUBS = 10
        TILE_DMAS = 5
        AV, Y, RING = 4, 5, 6

        tile_loaded = [sem(f"tile_loaded{k}") for k in range(3)]
        logits_ready = sem("logits_ready")
        probs_ready = sem("probs_ready")
        av_done = sem("av_done")
        o_cleared = sem("o_cleared")
        o_copied = sem("o_copied")
        rec_ready = sem("rec_ready")
        ring_ready = sem("ring_ready")
        ring_taken = sem("ring_taken")
        y_ready = sem("y_ready")
        y_taken = sem("y_taken")
        y_stored = [sem(f"y_stored{k}") for k in range(3)]
        scattered = sem("scattered")

        def ring_base(i, experts):
            if isinstance(i, int) and i == 0:
                return 0
            if not experts:
                return 2 * i - 1
            return 2 * FIRST - 1 + 32 * (i - FIRST)

        def plan(i, experts):
            steps = []
            for s in range(STEPS):
                uses = []
                if experts and s < 3 * SUBS:
                    sub = s % SUBS
                    if sub == 0:
                        uses += [("x", s // SUBS, 0), ("x", s // SUBS, 1)]
                    elif sub <= FC:
                        uses += [("h", s // SUBS, sub - 1)]
                if s == 1 and not (isinstance(i, int) and i == 0):
                    uses += [("o", 1, -1)]
                if s == TB + 1:
                    uses += [("o", 0, 0)]
                steps.append(uses)
            return steps

        def use_numbers(uses_by_step):
            table, k = {}, 0
            for uses in uses_by_step:
                for u in uses:
                    table[u] = k
                    k += 1
            return table

        def bank(i, k):
            first = 0 if isinstance(i, int) and i == 0 else 1
            return RING + (first + k) % 2

        x_again = [sem("x_again0"), sem("x_again1")]
        xn_back = sem("xn_back")

        with nc.Block() as block:
            @block.sync
            def _(sp):
                def load_stack(i, hh):
                    at_least(sp, logits_ready, 2 * (STEPS * (i - 1) + TB * (hh + 1)))
                    fill_stack(sp, i, hh)

                def load_tile(i, tt):
                    n = 3 * (i - FIRST) + tt
                    at_least(sp, y_taken, n - 2)
                    e = sp.value_load(emap[0:1, bass.ds(n, 1)], min_val=0, max_val=NE - 1)

                    def get(dst, src):
                        sp.dma_start(dst, src).then_inc(tile_loaded[tt], 16)
                    get(xs[:, tt], x_slots[bass.ds(n * P, P), :])
                    get(w1s[:, tt], W1[bass.ds(e, 1)].rearrange("e (c p) f -> p (e c) f", p=P))
                    get(b1s[:, tt], b1_cols[bass.ds(e, 1)].rearrange("e p c -> (e p) c"))
                    get(w2s[:, tt], W2[bass.ds(e, 1)].rearrange("e (c p) n -> p (e c) n", p=P))
                    get(b2s[:, tt], b2[bass.ds(e, 1), :].broadcast_to([P, D]))

                sp.wait_ge(zero_made, 1)
                sp.dma_start(x_slots.rearrange("(k p) d -> p k d", p=P),
                             zero.unsqueeze(1).broadcast_to([P, SLOT_TILES, D])).then_inc(slots_zeroed, 16)
                for dst, src in ((wo, Wo_t), (wqkc, Wqk_c), (woc, Wo_c)):
                    sp.dma_start(dst[:, :, :], src.rearrange("(c p) n -> p c n", p=P)).then_inc(late_loaded, 16)
                for dst, src in ((l2w, ln2_w), (l2b, ln2_b), (g1r, gamma1), (g2r, gamma2)):
                    sp.dma_start(dst[:, :], src.partition_broadcast(P)).then_inc(late_loaded, 16)
                for h in range(CH):
                    c, r = h // 4, h % 4
                    sp.dma_start(tauc[r * CD:(r + 1) * CD, c:c + 1],
                                 tau_c.rearrange("h a b -> h (a b)")[h:h + 1, :].broadcast_to([CD, 1])
                                 ).then_inc(late_loaded, 16)
                for par in range(2):
                    sp.wait_ge(q_stored[par], 3 * 16 * GROUPS // 2)
                    sp.wait_ge(w_stored[par], 2 * 16 * GROUPS // 2)
                for i in range(FIRST - 1):
                    load_stack(i + 1, 0)
                    load_stack(i + 1, 1)
                sp.wait_ge(routed, 1)
                sp.wait_ge(b1_stored, 16)
                sp.wait_ge(scattered, 16 * TILES)
                for tt in range(3):
                    load_tile(FIRST, tt)
                load_stack(FIRST, 0)
                load_stack(FIRST, 1)

                def ahead(i):
                    load_tile(i + 1, 0)
                    load_stack(i + 1, 0)
                    load_tile(i + 1, 1)
                    load_tile(i + 1, 2)
                    load_stack(i + 1, 1)
                with sp.Fori(FIRST, PAIRS - 1) as i:
                    ahead(i)
                for G in (0, 1):
                    sp.dma_start(xg[:, G], xt[:, G * GT:(G + 1) * GT, :]).then_inc(x_again[G], 16)
                for tt, groups in ((0, (0, 1, 6, 7)), (1, (2, 3)), (2, (4, 5))):
                    sp.wait_ge(y_taken, 3 * (PAIRS - 1 - FIRST) + tt + 1)
                    for G in groups:
                        at = slice(G * GT, (G + 1) * GT)
                        sp.dma_start(XN[:, at], xn_rows[:, at]).then_inc(xn_back, 16)

            @block.gpsimd
            def _(pool):
                def copy_v(i, hh):
                    at_least(pool, av_done, STEPS * (i - 1) + TB * (hh + 1))
                    apart(pool)
                    fill_v(i, hh)

                def store_y(i, tt):
                    n = 3 * (i - FIRST) + tt
                    pool.wait_ge(y_taken, n + 1)
                    pool.dma_start(y_slots[bass.ds(n * P, P), :], ysb[:, tt]).then_inc(y_stored[tt], 16)

                pool.wait_ge(routed, 1)
                pool.wait_ge(slots_zeroed, 16)
                for par in range(2):
                    pool.wait_ge(xn_kept[par], 32 * GROUPS // 2)
                for t in range(TILES):
                    if t == TILES // 2:
                        copy_v(1, 0)
                    nc.gpsimd.indirect_dma_start(x_slots, bass.IndirectOffsetOnAxis(ap=pos_u[:, t:t + 1], axis=0),
                                                 XN[:, t], None).then_inc(scattered, 16)
                copy_v(1, 1)
                for i in range(2, FIRST + 1):
                    copy_v(i, 0)
                    copy_v(i, 1)
                with pool.Fori(FIRST, PAIRS - 1) as i:
                    store_y(i, 0)
                    copy_v(i + 1, 0)
                    store_y(i, 1)
                    store_y(i, 2)
                    copy_v(i + 1, 1)
                for tt in range(3):
                    store_y(PAIRS - 1, tt)
                for tt in range(3):
                    pool.wait_ge(y_stored[tt], 16 * (PAIRS - FIRST))

            @block.scalar
            def _(act):
                def body(i, route=False):
                    for s in range(STEPS):
                        g = STEPS * i + s
                        if route and s == 2:
                            act.wait_ge(logits_shifted, 1)
                            nc.scalar.activation(ex, lg, ACT.Exp).then_inc(logits_exp, 1)
                        if s % TB == 0:
                            act.wait_ge(scale_set, 2 * i + s // TB + 1)
                        for half in range(2):
                            act.wait_ge(logits_ready, 2 * g + half + 1)
                            if half == 0:
                                at_least(act, av_done, g - 1)
                            nc.scalar.activation(probs[:, s % 2, half * 1024:(half + 1) * 1024],
                                                 ps[:, 2 * half:2 * half + 2].rearrange("p a b -> p (a b)"),
                                                 ACT.Exp, scale=scale[:, s // TB:s // TB + 1]
                                                 ).then_inc(probs_ready, 1)
                body(0, route=True)
                with act.Fori(1, PAIRS) as i:
                    body(i)

            @block.vector
            def _(dve):
                nc.vector.memset(ps[:, AV], 0.0).then_inc(o_cleared, 1)

                def take_o(i, hh):
                    head = 2 * i + hh
                    dve.wait_ge(av_done, TB * (head + 1))
                    nc.vector.tensor_copy(osb[:, hh], ps[:, AV]).then_inc(o_copied, 1)

                def norm(i, experts, use, hh, shift):
                    head = 2 * (i + shift) + hh
                    k = use[("o", hh, shift)]
                    t4 = ps[:, bank(i, k)].rearrange("p (k j c) -> p j k c", k=4, j=NCHUNK)
                    dve.wait_ge(ring_ready, ring_base(i, experts) + k + 1)
                    r = rec[:, hh].rearrange("p (j k) -> p j k", j=NCHUNK)
                    nc.vector.reciprocal(r, t4[:, :, :, DH]).then_inc(rec_ready, 1)
                    dve.wait_ge(rec_ready, head + 1)
                    nc.vector.tensor_tensor(
                        A_heads[:, bass.ds(head // H, 1), :, bass.ds(head % H, 1)]
                        .rearrange("p b (j k) h d -> p (b h j) k d", j=NCHUNK),
                        t4[:, :, :, 0:DH], r.unsqueeze(3).broadcast_to([P, NCHUNK, 4, DH]), ALU.mult
                    ).then_inc(ring_taken, 1)

                def body(i, experts):
                    uses = plan(i, experts)
                    use = use_numbers(uses)
                    for s in range(STEPS):
                        if s == 0 and not (isinstance(i, int) and i == 0):
                            take_o(i - 1, 1)
                        if s == TB:
                            take_o(i, 0)
                        for u in uses[s]:
                            kind, a, b = u
                            k = use[u]
                            if kind == "o":
                                norm(i, experts, use, a, b)
                                continue
                            dve.wait_ge(ring_ready, ring_base(i, experts) + k + 1)
                            if kind == "x":
                                nc.vector.tensor_copy(xsT[:, a, b], ps[:, bank(i, k), 0:P]).then_inc(ring_taken, 1)
                            else:
                                nc.vector.tensor_scalar(hT[:, b], ps[:, bank(i, k), 0:P], b1s[:, a, b:b + 1], 0.0,
                                                        ALU.add, ALU.max).then_inc(ring_taken, 1)
                        if experts and s < 3 * SUBS and s % SUBS == SUBS - 1:
                            tt = s // SUBS
                            dve.wait_ge(y_ready, 3 * (i - FIRST) + tt + 1)
                            at_least(dve, y_stored[tt], 16 * (i - FIRST))
                            nc.vector.tensor_tensor(ysb[:, tt], ps[:, Y, 0:D], b2s[:, tt], ALU.add).then_inc(y_taken, 1)

                n = [0]

                def mark(ins):
                    n[0] += 1
                    ins.then_inc(dve_route_step, 1)
                    dve.wait_ge(dve_route_step, n[0])

                def over_experts(v):
                    return v.unsqueeze(2).broadcast_to([P, TILES, NE])

                def over_tiles(v):
                    return v.unsqueeze(1).broadcast_to([P, TILES, NE])
                mx, sm, pm, idx = (s32[:, k] for k in range(4))
                dve.wait_ge(lg_ready, 1)
                mark(nc.vector.tensor_reduce(mx, lg, AX.X, ALU.max))
                nc.vector.tensor_tensor(lg, lg, over_experts(mx), ALU.subtract).then_inc(logits_shifted, 1)
                dve.wait_ge(logits_exp, 1)
                mark(nc.vector.tensor_reduce(sm, ex, AX.X, ALU.add))
                mark(nc.vector.reciprocal(sm, sm))
                mark(nc.vector.tensor_tensor(ex, ex, over_experts(sm), ALU.mult))
                mark(nc.vector.tensor_reduce(gate[:, :], ex, AX.X, ALU.max))
                mark(nc.vector.tensor_tensor(lg, ex, over_experts(gate[:, :]), ALU.is_equal))
                dve.wait_ge(consts_made, 1)
                dve.wait_ge(iota_rows, 1)
                mark(nc.vector.tensor_scalar(s8[:, 0], io_e, float(NE), None, ALU.add))
                mark(nc.vector.scalar_tensor_tensor(lg, lg, -float(NE), over_tiles(s8[:, 0]), ALU.mult, ALU.add))
                mark(nc.vector.tensor_reduce(idx, lg, AX.X, ALU.min))
                nc.vector.tensor_tensor(mask, over_tiles(io_e), over_experts(idx), ALU.is_equal).then_inc(mask_ready, 1)
                dve.wait_ge(ranks_ready, 1)
                mark(nc.vector.tensor_copy(cnt, ps[:, Y, TILES * NE:2 * TILES * NE].rearrange("p (t e) -> p t e", e=NE)))
                for e in range(NE):
                    last = nc.vector.tensor_tensor_scan(cum[:, :, e], ones[:, 0:TILES], cnt[:, :, e], 0.0,
                                                        ALU.mult, ALU.add)
                mark(last)
                mark(nc.vector.tensor_scalar(s8[:, 1], cum[:, TILES - 1], float(P - 1), None, ALU.add))
                mark(nc.vector.tensor_copy(s8i, s8[:, 1]))
                mark(nc.vector.tensor_scalar(s8i, s8i, 7, None, ALU.arith_shift_right))
                mark(nc.vector.tensor_copy(s8[:, 2], s8i))
                mark(nc.vector.tensor_tensor_scan(s8[:, 3], ones[:, 0:NE], s8[:, 2], 0.0, ALU.mult, ALU.add))
                mark(nc.vector.tensor_tensor(s8[:, 4], s8[:, 3], s8[:, 2], ALU.subtract))
                mark(nc.vector.tensor_scalar(s8[:, 5], s8[:, 4], float(P), None, ALU.mult))
                mark(nc.vector.tensor_tensor(cum, cum, cnt, ALU.subtract))
                mark(nc.vector.tensor_tensor(cum, cum, over_tiles(s8[:, 5]), ALU.add))
                mark(nc.vector.tensor_tensor(cum, ps[:, Y, 0:TILES * NE].rearrange("p (t e) -> p t e", e=NE), cum, ALU.add))
                mark(nc.vector.tensor_tensor(cum, cum, mask, ALU.mult))
                mark(nc.vector.tensor_reduce(mx, cum, AX.X, ALU.add))
                ends = s8[0:1, 3].unsqueeze(1).broadcast_to([1, SLOT_TILES, NE])
                mark(nc.vector.tensor_tensor(ek[0:1], io_k[0:1].unsqueeze(2).broadcast_to([1, SLOT_TILES, NE]), ends,
                                             ALU.is_ge))
                mark(nc.vector.tensor_reduce(ek1[0:1], ek[0:1], AX.X, ALU.add))
                mark(nc.vector.tensor_scalar(ek1[0:1], ek1[0:1], float(NE - 1), None, ALU.min))
                mark(nc.vector.tensor_copy(emap[:, :], ek1[0:1]))
                nc.vector.tensor_copy(pos_u[:, :], mx).then_inc(routed, 1)
                dve.wait_ge(late_loaded, 16 * N_LATE)
                mark(nc.vector.tensor_tensor(wo[:, :, :], wo[:, :, :],
                                             g1r[:, :].unsqueeze(1).broadcast_to([P, KC, D]), ALU.mult))
                mark(nc.vector.tensor_scalar(tauc[:, :], tauc[:, :], CQ_SCALE, None, ALU.mult))
                mark(nc.vector.tensor_reduce(diag[:, :], ident[:, :].rearrange("p (a b) -> p b a", b=CD), AX.X, ALU.add))

                body(0, False)
                with dve.Fori(1, FIRST) as i:
                    body(i, False)
                body(FIRST, True)
                with dve.Fori(FIRST + 1, PAIRS) as i:
                    body(i, True)
                take_o(PAIRS - 1, 1)
                norm(PAIRS, True, {("o", 1, -1): 0}, 1, -1)

            @block.tensor
            def _(pe):
                def logits(i, s):
                    hh, m = s // TB, s % TB
                    g = STEPS * i + s
                    if m == 0:
                        pe.wait_ge(stack_loaded[hh], 16 * STACK_DMAS * (i + 1))
                    for half in range(2):
                        at_least(pe, probs_ready, 2 * g + half - 1)
                        for j in range(2):
                            q0 = (2 * half + j) * 512
                            last = nc.tensor.matmul(ps[:, 2 * half + j], stat[:, hh, m * P:(m + 1) * P],
                                                    mov[:, hh, q0:q0 + 512], start=True, stop=True)
                        last.then_inc(logits_ready, 1)

                def values(i, s):
                    hh, m = s // TB, s % TB
                    g = STEPS * i + s
                    if m == 0:
                        pe.wait_ge(v_copied, 2 * i + hh + 1)
                        at_least(pe, o_copied, 2 * i + hh)
                    pe.wait_ge(probs_ready, 2 * g + 2)
                    for j in range(NCHUNK):
                        last = nc.tensor.matmul(ps[32 * j:32 * j + VW, AV], Vh[:, hh, m],
                                                probs[:, s % 2, j * 512:(j + 1) * 512],
                                                start=(m == 0), stop=(m == TB - 1), tile_position=(0, 32 * j))
                    last.then_inc(av_done, 1)

                def turn_o(i, k, hh, shift):
                    pe.wait_ge(o_copied, 2 * (i + shift) + hh + 1)
                    for c in range(4):
                        last = nc.tensor.transpose(ps[:, bank(i, k), c * P:(c + 1) * P],
                                                   osb[:, hh, c * P:(c + 1) * P], ident[:, :])
                    last.then_inc(ring_ready, 1)

                def body(i, experts, last_one=False, route=False):
                    uses = plan(i, experts)
                    use = use_numbers(uses)
                    for s in range(STEPS):
                        if s + 1 < STEPS:
                            logits(i, s + 1)
                        elif not last_one:
                            logits(i + 1, 0)
                        if route and s == 10:
                            pe.wait_ge(mask_ready, 1)
                            picks, n = mask.rearrange("p t e -> p (t e)"), TILES * NE
                            nc.tensor.matmul(ps[:, Y, 0:n], tri, picks, start=True, stop=True)
                            nc.tensor.matmul(ps[:, Y, n:2 * n], ones[:, :], picks, start=True, stop=True
                                             ).then_inc(ranks_ready, 1)
                        sub, tt = s % SUBS, s // SUBS
                        for u in uses[s]:
                            kind, a, b = u
                            k = use[u]
                            at_least(pe, ring_taken, ring_base(i, experts) + k - 1)
                            if kind == "o":
                                turn_o(i, k, a, b)
                            elif kind == "x":
                                if b == 0:
                                    pe.wait_ge(tile_loaded[a], 16 * TILE_DMAS * (i - FIRST + 1))
                                nc.tensor.transpose(ps[:, bank(i, k), 0:P], xs[:, a, b * P:(b + 1) * P],
                                                    ident[:, :]).then_inc(ring_ready, 1)
                            else:
                                if b == 0:
                                    pe.wait_ge(ring_taken, ring_base(i, experts) + use[("x", a, 1)] + 1)
                                for c in range(KC):
                                    last = nc.tensor.matmul(ps[:, bank(i, k), 0:P], w1s[:, a, c, b * P:(b + 1) * P],
                                                            xsT[:, a, c], start=(c == 0), stop=(c == KC - 1))
                                last.then_inc(ring_ready, 1)
                        if experts and tt < 3 and sub >= 2:
                            c = sub - 2
                            pe.wait_ge(ring_taken, ring_base(i, experts) + use[("h", tt, c)] + 1)
                            if c == 0:
                                at_least(pe, y_taken, 3 * (i - FIRST) + tt)
                            ins = nc.tensor.matmul(ps[:, Y, 0:D], hT[:, c], w2s[:, tt, c],
                                                   start=(c == 0), stop=(c == FC - 1))
                            if c == FC - 1:
                                ins.then_inc(y_ready, 1)
                        values(i, s)

                logits(0, 0)
                pe.wait_ge(o_cleared, 1)
                body(0, False, route=True)
                with pe.Fori(1, FIRST) as i:
                    body(i, False)
                body(FIRST, True)
                with pe.Fori(FIRST + 1, PAIRS - 1) as i:
                    body(i, True)
                body(PAIRS - 1, True, True)
                at_least(pe, ring_taken, ring_base(PAIRS, True) - 1)
                turn_o(PAIRS, 0, 1, -1)

        take = views(work[:, :])
        AT = take([2, KC, GN])
        a2g = take([2, GT, D])
        a2T = take([KC, TOK])
        a2s = take([2, KC, GN])
        take_m = views(XN_REST)
        gram = take_m([NB, KC, D])
        t1 = take_m([NB, KC, D])
        rr = take_m([NB, KC, D])
        mb = take_m([NB, KC, D])
        pblk = take([NB, KC, P])
        dd = take([NB, KC, CD])
        dm = take([NB, KC, CD])
        ll = take([NB, KC, CD])
        c4 = take([NB, 3, KC])
        T_BANK, D_BANK, R_BANK, M_BANK = (6, 5), (7, 7), (4, 4), (6, 5)
        FIN = (2, 0)

        def use_a(G):
            return 2 * G if G < 3 else 4 * G - 6

        def use_a2(G):
            return use_a(G + 3) + 2 if G + 3 < GROUPS else 2 * (GROUPS + G)

        gathered = sem("gathered")
        ring3_ready = sem("ring3_ready")
        ring3_taken = sem("ring3_taken")
        wo_ready = sem("wo_ready")
        x1_ready = sem("x1_ready")
        stats3_step = sem("stats3_step")
        a2_step = sem("a2_step")
        var3_ready = sem("var3_ready")
        rstd3_ready = sem("rstd3_ready")
        a2_ready = sem("a2_ready")
        expert_added = sem("expert_added")
        x_added = sem("x_added")
        gram_cleared = sem("gram_cleared")
        gram_done = sem("gram_done")
        gram_copied = sem("gram_copied")
        corner_turned = sem("corner_turned")
        t_ready = sem("t_ready")
        t_copied = sem("t_copied")
        dots_ready = sem("dots_ready")
        own_ready = sem("own_ready")
        norms_ready = sem("norms_ready")
        alg_step = sem("alg_step")
        blocks_cleared = sem("blocks_cleared")
        alg_shifted = sem("alg_shifted")
        alg_exp = sem("alg_exp")
        p_ready = sem("p_ready")
        r_ready = sem("r_ready")
        r_copied = sem("r_copied")
        m_ready = sem("m_ready")
        mb_ready = sem("mb_ready")
        staged = sem("staged")
        fin_ready = sem("fin_ready")
        fin_taken = sem("fin_taken")
        out_stored = sem("out_stored")

        with nc.Block() as block:
            @block.sync
            def _(sp):
                def load(G, par):
                    sp.wait_ge(x_added, G - 1)
                    sp.dma_start(xg[:, par], xt[:, bass.ds(G * GT, GT), :]).then_inc(x_again[par], 16)

                def store(G):
                    sp.wait_ge(fin_taken, 2 * G + 2)
                    sp.dma_start(outt[:, bass.ds(G * GT, GT), :], XN[:, bass.ds(G * GT, GT)]).then_inc(out_stored, 16)
                with sp.Fori(1, GROUPS // 2) as it:
                    for par in range(2):
                        load(2 * it + par, par)
                with sp.Fori(0, GROUPS) as G:
                    store(G)
                sp.wait_ge(out_stored, 16 * GROUPS)

            @block.gpsimd
            def _(pool):
                def rstd(G, par):
                    pool.wait_ge(var3_ready, G + 1)
                    nc.gpsimd.tensor_tensor(rs1[:, par], ve1[:, par], nhalf[:, :], ALU.pow).then_inc(rstd3_ready, 1)

                def add_x(G, par):
                    pool.wait_ge(a2_ready, G + 1)
                    pool.wait_ge(x_again[par], 16 * (G // 2) + 16)
                    xv = XN[:, G * GT:(G + 1) * GT]
                    nc.gpsimd.tensor_tensor(xv, xv, xg[:, par], ALU.add).then_inc(x_added, 1)

                for G in range(GROUPS):
                    rstd(G, G % 2)
                    if G > 1:
                        add_x(G - 2, G % 2)
                    for t in range(G * GT, (G + 1) * GT):
                        nc.gpsimd.indirect_dma_start(YG[:, t], None, y_slots,
                                                     bass.IndirectOffsetOnAxis(ap=pos_u[:, t:t + 1], axis=0)
                                                     ).then_inc(gathered, 16)
                add_x(GROUPS - 2, 0)
                add_x(GROUPS - 1, 1)

            @block.scalar
            def _(act):
                def take_at(G, par):
                    for c in range(KC):
                        act.wait_ge(ring3_ready, use_a(G) + c + 1)
                        if c == 0:
                            at_least(act, wo_ready, 2 * (G - 1))
                        nc.scalar.copy(AT[:, par, c], ps[:, c]).then_inc(ring3_taken, 1)

                def take_a2(G, par):
                    for c in range(KC):
                        act.wait_ge(ring3_ready, use_a2(G) + c + 1)
                        nc.scalar.copy(a2T[:, c, bass.ds(G * GN, GN)], ps[:, c]).then_inc(ring3_taken, 1)

                def turn(G, par):
                    take_at(G + 3, 1 - par)
                    take_a2(G, par)

                def take_gram(b):
                    act.wait_ge(gram_done, GB * (b + 1))
                    bank = ps[:, 4 + b].rearrange("p (c n) -> p c n", c=KC)
                    nc.scalar.copy(gram[:, b], bank).then_inc(gram_copied, 1)
                    act.wait_ge(corner_turned, b + 1)
                    nc.scalar.copy(gram[:, b, 1, 0:P], bank[:, 1, 0:P]).then_inc(gram_copied, 1)

                def take_t(b):
                    act.wait_ge(t_ready, b + 1)
                    nc.scalar.copy(t1[:, b].rearrange("p c n -> p (c n)"), ps[:, T_BANK[b]]).then_inc(t_copied, 1)

                def exp_of(b):
                    act.wait_ge(alg_shifted, b + 1)
                    nc.scalar.activation(ll[:, b], ll[:, b], ACT.Exp).then_inc(alg_exp, 1)

                def take_r(b):
                    act.wait_ge(r_ready, b + 1)
                    nc.scalar.copy(rr[:, b].rearrange("p c n -> p (c n)"), ps[:, R_BANK[b]]).then_inc(r_copied, 1)

                def stage_f(G, par):
                    at_least(act, fin_ready, 2 * (G - 1))
                    nc.scalar.copy(a2s[:, par], a2T[:, :, bass.ds(G * GN, GN)]).then_inc(staged, 1)

                for G in range(3):
                    take_at(G, G % 2)
                for G in range(GB):
                    turn(G, G % 2)
                take_gram(0)
                take_t(0)
                take_at(GROUPS - 1, 1)
                take_a2(GROUPS - 4, 0)
                take_a2(GROUPS - 3, 1)
                exp_of(0)
                stage_f(0, 0)
                stage_f(1, 1)
                take_a2(GROUPS - 2, 0)
                take_r(0)
                take_a2(GROUPS - 1, 1)
                take_gram(1)
                take_t(1)
                stage_f(2, 0)
                exp_of(1)
                stage_f(3, 1)
                take_r(1)
                with act.Fori(GB // 2, GROUPS // 2) as it:
                    for par in range(2):
                        stage_f(2 * it + par, par)

            @block.vector
            def _(dve):
                nc.vector.memset(ps[:, 4:6], 0.0).then_inc(gram_cleared, 1)
                rows = [P, GT, D]

                def tile(v, G, t):
                    return v[:, bass.ds(G * GT + t, 1)].rearrange("p a d -> p (a d)")

                def add_expert(G, par):
                    dve.wait_ge(x_added, G + 1)
                    for t in range(GT):
                        last = nc.vector.scalar_tensor_tensor(tile(XN, G, t), tile(YG, G, t),
                                                              gate[:, bass.ds(G * GT + t, 1)], tile(XN, G, t),
                                                              ALU.mult, ALU.add)
                    last.then_inc(expert_added, 1)
                    dve.wait_ge(expert_added, G + 1)

                def make_x1(G, par):
                    for k in range(2):
                        dve.wait_ge(wo_ready, 2 * G + k + 1)
                        xv = XN[:, bass.ds(G * GT + 2 * k, 2)]
                        nc.vector.tensor_tensor(xv, ps[:, 2 + k].rearrange("p (t d) -> p t d", t=2), xv,
                                                ALU.add).then_inc(x1_ready, 1)
                    dve.wait_ge(x1_ready, 2 * G + 2)
                    for t in range(GT):
                        last = nc.vector.bn_stats(st1[:, par, t], tile(XN, G, t))
                    last.then_inc(stats3_step, 1)
                    dve.wait_ge(stats3_step, 2 * G + 1)
                    for t in range(GT):
                        last = nc.vector.bn_aggr(mv1[:, par, t], st1[:, par, t])
                    last.then_inc(stats3_step, 1)
                    dve.wait_ge(stats3_step, 2 * G + 2)
                    nc.vector.tensor_scalar(ve1[:, par], mv1[:, par, :, 1], EPS, None, ALU.add).then_inc(var3_ready, 1)

                def make_a2(G, par):
                    at_least(dve, gram_done, G - 1)
                    if G >= 2:
                        dve.wait_ge(ring3_ready, use_a2(G - 2) + KC)
                    for t in range(GT):
                        last = nc.vector.scalar_tensor_tensor(a2g[:, par, t], tile(XN, G, t), mv1[:, par, t, 0:1],
                                                              l2w[:, :], ALU.subtract, ALU.mult)
                    last.then_inc(a2_step, 1)
                    dve.wait_ge(rstd3_ready, G + 1)
                    dve.wait_ge(a2_step, G + 1)
                    for t in range(GT):
                        last = nc.vector.scalar_tensor_tensor(a2g[:, par, t], a2g[:, par, t], rs1[:, par, t:t + 1],
                                                              l2b[:, :], ALU.mult, ALU.add)
                    last.then_inc(a2_ready, 1)

                n = [0]

                def mark(ins):
                    n[0] += 1
                    ins.then_inc(alg_step, 1)
                    dve.wait_ge(alg_step, n[0])

                def wide(v):
                    return v.unsqueeze(2).broadcast_to([P, KC, CD])

                def own_dots(b):
                    dots = ps[:, D_BANK[b], 0:KC * P].rearrange("p (k c) -> p k c", k=KC)
                    dve.wait_ge(dots_ready, b + 1)
                    for r in range(P // CD):
                        q = slice(r * CD, (r + 1) * CD)
                        last = nc.vector.tensor_copy(dd[q, b], dots[q, :, q])
                    mark(last)
                    nc.vector.tensor_tensor(dm[:, b], dd[:, b], diag[:, :].unsqueeze(1).broadcast_to([P, KC, CD]),
                                            ALU.mult).then_inc(own_ready, 1)
                    dve.wait_ge(own_ready, b + 1)
                    mark(nc.vector.tensor_reduce(c4[:, b, 0], dm[:, b], AX.X, ALU.add))

                def shifted_logits(b):
                    l = ll[:, b]
                    dve.wait_ge(norms_ready, b + 1)
                    mark(nc.vector.scalar_tensor_tensor(
                        l, dd[:, b], 2.0, ps[:, D_BANK[b], KC * P:KC * (P + CD)].rearrange("p (k c) -> p k c", k=KC),
                        ALU.mult, ALU.subtract))
                    mark(nc.vector.tensor_tensor(l, l, wide(c4[:, b, 0]), ALU.subtract))
                    mark(nc.vector.tensor_tensor(l, l, wide(tauc[:, :]), ALU.mult))
                    mark(nc.vector.tensor_reduce(c4[:, b, 1], l, AX.X, ALU.max))
                    nc.vector.tensor_tensor(l, l, wide(c4[:, b, 1]), ALU.subtract).then_inc(alg_shifted, 1)

                def probabilities(b):
                    l = ll[:, b]
                    dve.wait_ge(alg_exp, b + 1)
                    mark(nc.vector.tensor_reduce(c4[:, b, 2], l, AX.X, ALU.add))
                    mark(nc.vector.reciprocal(c4[:, b, 2], c4[:, b, 2]))
                    for r in range(P // CD):
                        q = slice(r * CD, (r + 1) * CD)
                        last = nc.vector.tensor_tensor(pblk[q, b, :, q], l[q],
                                                       c4[q, b, 2].unsqueeze(2).broadcast_to([CD, KC, CD]), ALU.mult)
                    last.then_inc(p_ready, 1)

                def fold(b):
                    dve.wait_ge(m_ready, b + 1)
                    nc.vector.tensor_tensor(mb[:, b], ps[:, M_BANK[b]].rearrange("p (c n) -> p c n", c=KC),
                                            g2r[:, :].unsqueeze(1).broadcast_to([P, KC, D]), ALU.mult
                                            ).then_inc(mb_ready, 1)

                def final(G, par):
                    add_expert(G, par)
                    for k in range(2):
                        dve.wait_ge(fin_ready, 2 * G + k + 1)
                        xv = XN[:, bass.ds(G * GT + 2 * k, 2)]
                        nc.vector.tensor_tensor(xv, ps[:, FIN[par] + k].rearrange("p (t d) -> p t d", t=2), xv,
                                                ALU.add).then_inc(fin_taken, 1)

                dve.wait_ge(xn_back, 16 * GROUPS)
                make_x1(0, 0)
                nc.vector.memset(pblk, 0.0).then_inc(blocks_cleared, 1)
                for G in range(GB + 1):
                    make_x1(G + 1, (G + 1) % 2)
                    make_a2(G, G % 2)
                make_x1(GROUPS - 2, 0)
                make_a2(GROUPS - 3, 1)
                own_dots(0)
                make_a2(GROUPS - 2, 0)
                shifted_logits(0)
                make_x1(GROUPS - 1, 1)
                dve.wait_ge(blocks_cleared, 1)
                probabilities(0)
                make_a2(GROUPS - 1, 1)
                fold(0)
                dve.wait_ge(gathered, 16 * TILES)
                final(0, 0)
                own_dots(1)
                final(1, 1)
                shifted_logits(1)
                probabilities(1)
                final(2, 0)
                fold(1)
                final(3, 1)
                with dve.Fori(GB // 2, GROUPS // 2) as it:
                    for par in range(2):
                        final(2 * it + par, par)

            @block.tensor
            def _(pe):
                def turn_a(G):
                    b, t0 = G // GB, (G % GB) * GT
                    for c in range(KC):
                        at_least(pe, ring3_taken, use_a(G) + c - 1)
                        for t in range(GT):
                            last = nc.tensor.transpose(ps[:, c, t * P:(t + 1) * P], A_rows[:, b, t0 + t, c * P:(c + 1) * P],
                                                       ident[:, :])
                        last.then_inc(ring3_ready, 1)

                def project(G, par):
                    pe.wait_ge(ring3_taken, use_a(G) + 2)
                    for k in range(2):
                        at_least(pe, x1_ready, 2 * (G - 1) + k + 1)
                        for t in range(2):
                            for c in range(KC):
                                last = nc.tensor.matmul(ps[:, 2 + k, t * D:(t + 1) * D],
                                                        AT[:, par, c, (2 * k + t) * P:(2 * k + t + 1) * P], wo[:, c],
                                                        start=(c == 0), stop=(c == KC - 1))
                        last.then_inc(wo_ready, 1)

                def turn_a2(G, par):
                    pe.wait_ge(a2_ready, G + 1)
                    for c in range(KC):
                        pe.wait_ge(ring3_taken, use_a2(G) + c - 1)
                        for t in range(GT):
                            last = nc.tensor.transpose(ps[:, c, t * P:(t + 1) * P], a2g[:, par, t, c * P:(c + 1) * P],
                                                       ident[:, :])
                        last.then_inc(ring3_ready, 1)

                def gram_of(G, par):
                    pe.wait_ge(a2_ready, G + 1)
                    bank = ps[:, 4 + G // GB]
                    for t in range(GT):
                        nc.tensor.matmul(bank[:, 0:D], a2g[:, par, t, 0:P], a2g[:, par, t],
                                         start=False, stop=False, skip_group_check=True)
                        last = nc.tensor.matmul(bank[:, D + P:2 * D], a2g[:, par, t, P:D], a2g[:, par, t, P:D],
                                                start=False, stop=False, skip_group_check=True)
                    last.then_inc(gram_done, 1)

                def corner(b):
                    pe.wait_ge(gram_copied, 2 * b + 1)
                    nc.tensor.transpose(ps[:, 4 + b, D:D + P], gram[:, b, 0, P:D], ident[:, :]).then_inc(corner_turned, 1)

                def product_t(b):
                    pe.wait_ge(gram_copied, 2 * b + 2)
                    for M in range(KC):
                        for c in range(KC):
                            last = nc.tensor.matmul(ps[:, T_BANK[b], M * D:(M + 1) * D], gram[:, b, c, M * P:(M + 1) * P],
                                                    wqkc[:, c], start=(c == 0), stop=(c == KC - 1))
                    last.then_inc(t_ready, 1)

                def product_dots(b):
                    pe.wait_ge(t_copied, b + 1)
                    at_least(pe, alg_shifted, b)
                    for M in range(KC):
                        for c in range(KC):
                            last = nc.tensor.matmul(ps[:, D_BANK[b], M * P:(M + 1) * P],
                                                    wqkc[:, c, M * P:(M + 1) * P], t1[:, b, c, M * P:(M + 1) * P],
                                                    start=(c == 0), stop=(c == KC - 1))
                    last.then_inc(dots_ready, 1)

                def product_norms(b):
                    pe.wait_ge(own_ready, b + 1)
                    nc.tensor.matmul(ps[:, D_BANK[b], KC * P:KC * (P + CD)], blockones[:, :],
                                     dm[:, b].rearrange("p k c -> p (k c)"), start=True, stop=True).then_inc(norms_ready, 1)

                def product_r(b):
                    pe.wait_ge(p_ready, b + 1)
                    at_least(pe, r_copied, b)
                    for c in range(KC):
                        last = nc.tensor.matmul(ps[:, R_BANK[b], c * D:(c + 1) * D], pblk[:, b, c], woc[:, c],
                                                start=True, stop=True)
                    last.then_inc(r_ready, 1)

                def product_m(b):
                    pe.wait_ge(r_copied, b + 1)
                    for k in range(KC):
                        for d in range(KC):
                            last = nc.tensor.matmul(ps[:, M_BANK[b], k * D:(k + 1) * D], wvcT[:, d, k * P:(k + 1) * P],
                                                    rr[:, b, d], start=(d == 0), stop=(d == KC - 1))
                    last.then_inc(m_ready, 1)

                def finals(G, par):
                    b = G // GB
                    pe.wait_ge(staged, G + 1)
                    for k in range(2):
                        at_least(pe, fin_taken, 2 * (G - 2) + k + 1)
                        for t in range(2):
                            for c in range(KC):
                                last = nc.tensor.matmul(ps[:, FIN[par] + k, t * D:(t + 1) * D],
                                                        a2s[:, par, c, (2 * k + t) * P:(2 * k + t + 1) * P],
                                                        mb[:, bass.ds(b, 1), c].rearrange("p a n -> p (a n)"),
                                                        start=(c == 0), stop=(c == KC - 1))
                        last.then_inc(fin_ready, 1)

                def turn(G, par):
                    turn_a(G + 3)
                    gram_of(G, par)
                    turn_a2(G, par)
                    project(G + 3, 1 - par)

                pe.wait_ge(gram_cleared, 1)
                for G in range(3):
                    turn_a(G)
                    project(G, G % 2)
                for G in range(GB):
                    turn(G, G % 2)
                corner(0)
                turn_a(GROUPS - 1)
                product_t(0)
                gram_of(GROUPS - 4, 0)
                product_dots(0)
                turn_a2(GROUPS - 4, 0)
                project(GROUPS - 1, 1)
                gram_of(GROUPS - 3, 1)
                turn_a2(GROUPS - 3, 1)
                product_norms(0)
                gram_of(GROUPS - 2, 0)
                turn_a2(GROUPS - 2, 0)
                product_r(0)
                product_m(0)
                gram_of(GROUPS - 1, 1)
                turn_a2(GROUPS - 1, 1)
                corner(1)
                product_t(1)
                pe.wait_ge(ring3_taken, 4 * GROUPS)
                pe.wait_ge(mb_ready, 1)
                finals(0, 0)
                product_dots(1)
                finals(1, 1)
                product_norms(1)
                finals(2, 0)
                product_r(1)
                finals(3, 1)
                product_m(1)
                pe.wait_ge(mb_ready, 2)
                with pe.Fori(GB // 2, GROUPS // 2) as it:
                    for par in range(2):
                        finals(2 * it + par, par)


_INS = {"x": "L0_attn_x", "Wqk_t": "L0_attn_Wqk_t", "Wv_t": "L0_attn_Wv_t", "Wo_t": "L0_attn_Wo_t",
        "tau_t": "L0_attn_tau_t", "Wqk_c": "L0_attn_Wqk_c", "Wv_c": "L0_attn_Wv_c", "Wo_c": "L0_attn_Wo_c",
        "tau_c": "L0_attn_tau_c", "ln1_w": "L0_attn_ln1_w", "ln1_b": "L0_attn_ln1_b", "ln2_w": "L0_attn_ln2_w",
        "ln2_b": "L0_attn_ln2_b", "gamma1": "L0_attn_gamma1", "gamma2": "L0_attn_gamma2",
        "router_W": "L0_ffn_router_W", "router_b": "L0_ffn_router_b", "W1": "L0_ffn_W1", "b1": "L0_ffn_b1",
        "W2": "L0_ffn_W2", "b2": "L0_ffn_b2"}


def kernel(**inputs):
    import numpy as _np
    import concourse.bacc as _bacc
    from concourse import mybir as _mybir
    from concourse.bass_utils import run_bass_kernel_spmd as _run

    nc = _bacc.Bacc("TRN2", target_bir_lowering=False, num_devices=1)
    arrays, args = {}, {}
    for short, name in _INS.items():
        a = _np.ascontiguousarray(inputs[name])
        arrays[f"in_{name}_dram"] = a
        args[short] = nc.dram_tensor(f"in_{name}_dram", a.shape, _mybir.dt.from_np(a.dtype), kind="ExternalInput").ap()
    args["out"] = nc.dram_tensor("out_0_dram", inputs["L0_attn_x"].shape, _mybir.dt.float32, kind="ExternalOutput").ap()
    build(nc, **args)
    r = _run(nc, [arrays], core_ids=[0])
    return r.results[0]["out_0_dram"]
```
